# Optimizing a Trainium2 kernel written in Bass

```python
import numpy as np
import jax
import jax.numpy as jnp

def _softmax(x, axis=-1):
    return jax.nn.softmax(x, axis=axis)

def _gelu(x):
    return jax.nn.gelu(x, approximate=True)

def _silu(x):
    return jax.nn.silu(x)

def _sigmoid(x):
    return jax.nn.sigmoid(x)

def _layernorm(x, axis=-1, eps=1e-05):
    m = jnp.mean(x, axis=axis, keepdims=True)
    v = jnp.var(x, axis=axis, keepdims=True)
    return (x - m) / jnp.sqrt(v + eps)

def _scatter_add(tgt, idx, src, axis=0):
    return tgt.at[idx].add(src)

def _segment_sum(src, seg, n):
    return jax.ops.segment_sum(src, seg, n)
kernel_name = 'mk_adaln_d2_jaxref_r8_555c92'

def setup_inputs(seed: int=0):
    np.random.seed(seed)
    _w = jnp.asarray

    def _L0_attn_setup():
        import jax, jax.numpy as jnp
        import numpy as np
        B, S, HID = (4, 128, 128)
        H, D = (16, 64)
        NEG_INF = -10000000000.0

        def rope_alternate(inputs, position, min_timescale=1.0, max_timescale=10000.0):
            d = inputs.shape[-1]
            half = d // 2
            fraction = 2.0 * jnp.arange(half, dtype=jnp.float32) / d
            timescale = min_timescale * (max_timescale / min_timescale) ** fraction
            sinusoid = position[:, :, None, None] / timescale
            sin, cos = (jnp.sin(sinusoid), jnp.cos(sinusoid))
            first, second = jnp.split(inputs, 2, axis=-1)
            return jnp.concatenate([(first * cos - second * sin).astype(inputs.dtype), (second * cos + first * sin).astype(inputs.dtype)], axis=-1)
        key = jax.random.key(seed)
        k1, k2, k3 = jax.random.split(key, 3)
        x = jax.random.normal(k1, (B, S, HID), dtype=jnp.float32)
        wqkv = jax.random.normal(k2, (HID, 3 * H * D), dtype=jnp.float32) * (1.0 / np.sqrt(HID))
        wo = jax.random.normal(k3, (H * D, HID), dtype=jnp.float32) * (1.0 / np.sqrt(H * D))
        return {'x': x, 'wqkv': wqkv, 'wo': wo}
    _L0_attn_in = _L0_attn_setup()

    def _L0_ffn_setup():
        import jax, jax.numpy as jnp
        import numpy as np
        HIDDEN = 128
        INTER = 512
        N_EXPERTS = 8

        def geglu(x, w1, w2, w3):
            return jax.nn.gelu(x @ w1, approximate=False) * (x @ w2) @ w3
        key = jax.random.key(seed)
        ks = jax.random.split(key, 8)
        s = 0.02
        x = jax.random.normal(ks[0], (2, 256, HIDDEN), dtype=jnp.float32)
        w1s = jax.random.normal(ks[1], (HIDDEN, INTER), dtype=jnp.float32) * s
        w2s = jax.random.normal(ks[2], (HIDDEN, INTER), dtype=jnp.float32) * s
        w3s = jax.random.normal(ks[3], (INTER, HIDDEN), dtype=jnp.float32) * s
        W1 = jax.random.normal(ks[4], (N_EXPERTS, HIDDEN, INTER), dtype=jnp.float32) * s
        W2 = jax.random.normal(ks[5], (N_EXPERTS, HIDDEN, INTER), dtype=jnp.float32) * s
        W3 = jax.random.normal(ks[6], (N_EXPERTS, INTER, HIDDEN), dtype=jnp.float32) * s
        Wg = jax.random.normal(ks[7], (HIDDEN, N_EXPERTS), dtype=jnp.float32) * s
        return {'x': x, 'w1s': w1s, 'w2s': w2s, 'w3s': w3s, 'W1': W1, 'W2': W2, 'W3': W3, 'Wg': Wg}
    _L0_ffn_in = _L0_ffn_setup()
    _L0_c = _w((lambda *s: np.random.randn(*s).astype(np.float32) * 0.05)(2, 128))
    _L0_wmod = _w((lambda *s: np.random.randn(*s).astype(np.float32) * 0.05)(128, 6 * 128) * 128 ** (-0.5))

    def _L1_attn_setup():
        import jax, jax.numpy as jnp
        import numpy as np
        D_MODEL = 128
        N_HEADS = 16
        HEAD_DIM = D_MODEL // N_HEADS
        LORA_RANK = 16
        LORA_SCALING = 1.0 / LORA_RANK

        def lora_linear(x, w, a, b):
            return x @ w.T + LORA_SCALING * (x @ a.T @ b.T)
        key = jax.random.key(seed)
        ks = jax.random.split(key, 14)
        B, S = (4, 256)

        def w(k, shape, scale=0.02):
            return jax.random.normal(k, shape, dtype=jnp.float32) * scale
        inp = {'x': jax.random.normal(ks[0], (B, S, D_MODEL), dtype=jnp.float32), 'wq': w(ks[1], (D_MODEL, D_MODEL)), 'aq': w(ks[2], (LORA_RANK, D_MODEL)), 'bq': w(ks[3], (D_MODEL, LORA_RANK)), 'wk': w(ks[4], (D_MODEL, D_MODEL)), 'ak': w(ks[5], (LORA_RANK, D_MODEL)), 'bk': w(ks[6], (D_MODEL, LORA_RANK)), 'wv': w(ks[7], (D_MODEL, D_MODEL)), 'av': w(ks[8], (LORA_RANK, D_MODEL)), 'bv': w(ks[9], (D_MODEL, LORA_RANK)), 'wo': w(ks[10], (D_MODEL, D_MODEL)), 'ao': w(ks[11], (LORA_RANK, D_MODEL)), 'bo': w(ks[12], (D_MODEL, LORA_RANK))}
        return inp
    _L1_attn_in = _L1_attn_setup()

    def _L1_ffn_setup():
        import jax, jax.numpy as jnp
        import numpy as np
        NUM_EXPERTS = 8
        EXPERT_CAPACITY = 2.0
        DIM = 128
        HIDDEN_DIM = 512
        key = jax.random.key(seed)
        k_x, k_g, k_w1, k_w2 = jax.random.split(key, 4)
        n, t, d, f, e = (8, 128, DIM, HIDDEN_DIM, NUM_EXPERTS)
        x = jax.random.normal(k_x, (n, t, d), dtype=jnp.float32)
        gate_w = jax.random.normal(k_g, (e, d), dtype=jnp.float32) * 0.02
        w1 = jax.random.normal(k_w1, (e, d, f), dtype=jnp.float32) * 0.02
        w2 = jax.random.normal(k_w2, (e, f, d), dtype=jnp.float32) * 0.02
        return {'x': x, 'gate_w': gate_w, 'w1': w1, 'w2': w2}
    _L1_ffn_in = _L1_ffn_setup()
    _L1_c = _w((lambda *s: np.random.randn(*s).astype(np.float32) * 0.05)(2, 128))
    _L1_wmod = _w((lambda *s: np.random.randn(*s).astype(np.float32) * 0.05)(128, 6 * 128) * 128 ** (-0.5))
    _d = {'L0_attn_x': _L0_attn_in['x'], 'L0_attn_wqkv': _L0_attn_in['wqkv'], 'L0_attn_wo': _L0_attn_in['wo'], 'L0_ffn_w1s': _L0_ffn_in['w1s'], 'L0_ffn_w2s': _L0_ffn_in['w2s'], 'L0_ffn_w3s': _L0_ffn_in['w3s'], 'L0_ffn_W1': _L0_ffn_in['W1'], 'L0_ffn_W2': _L0_ffn_in['W2'], 'L0_ffn_W3': _L0_ffn_in['W3'], 'L0_ffn_Wg': _L0_ffn_in['Wg'], 'L0_c': _L0_c, 'L0_wmod': _L0_wmod, 'L1_attn_wq': _L1_attn_in['wq'], 'L1_attn_aq': _L1_attn_in['aq'], 'L1_attn_bq': _L1_attn_in['bq'], 'L1_attn_wk': _L1_attn_in['wk'], 'L1_attn_ak': _L1_attn_in['ak'], 'L1_attn_bk': _L1_attn_in['bk'], 'L1_attn_wv': _L1_attn_in['wv'], 'L1_attn_av': _L1_attn_in['av'], 'L1_attn_bv': _L1_attn_in['bv'], 'L1_attn_wo': _L1_attn_in['wo'], 'L1_attn_ao': _L1_attn_in['ao'], 'L1_attn_bo': _L1_attn_in['bo'], 'L1_ffn_gate_w': _L1_ffn_in['gate_w'], 'L1_ffn_w1': _L1_ffn_in['w1'], 'L1_ffn_w2': _L1_ffn_in['w2'], 'L1_c': _L1_c, 'L1_wmod': _L1_wmod}
    _x0 = _d['L0_attn_x']
    _d['L0_attn_x'] = jax.random.normal(jax.random.fold_in(jax.random.key(seed), 1), (2, 1024, 128), dtype=_x0.dtype)
    del _x0
    return _d

def reference(L0_attn_x, L0_attn_wqkv, L0_attn_wo, L0_ffn_w1s, L0_ffn_w2s, L0_ffn_w3s, L0_ffn_W1, L0_ffn_W2, L0_ffn_W3, L0_ffn_Wg, L0_c, L0_wmod, L1_attn_wq, L1_attn_aq, L1_attn_bq, L1_attn_wk, L1_attn_ak, L1_attn_bk, L1_attn_wv, L1_attn_av, L1_attn_bv, L1_attn_wo, L1_attn_ao, L1_attn_bo, L1_ffn_gate_w, L1_ffn_w1, L1_ffn_w2, L1_c, L1_wmod):

    def _L0_attn_ref(x, wqkv, wo):
        import jax, jax.numpy as jnp
        import numpy as np
        B, S, HID = (4, 128, 128)
        H, D = (16, 64)
        NEG_INF = -10000000000.0

        def rope_alternate(inputs, position, min_timescale=1.0, max_timescale=10000.0):
            d = inputs.shape[-1]
            half = d // 2
            fraction = 2.0 * jnp.arange(half, dtype=jnp.float32) / d
            timescale = min_timescale * (max_timescale / min_timescale) ** fraction
            sinusoid = position[:, :, None, None] / timescale
            sin, cos = (jnp.sin(sinusoid), jnp.cos(sinusoid))
            first, second = jnp.split(inputs, 2, axis=-1)
            return jnp.concatenate([(first * cos - second * sin).astype(inputs.dtype), (second * cos + first * sin).astype(inputs.dtype)], axis=-1)
        b, s, _ = x.shape
        qkv = jnp.einsum('bsh,hf->bsf', x, wqkv).reshape(b, s, 3, H, D)
        q, k, v = (qkv[:, :, 0], qkv[:, :, 1], qkv[:, :, 2])
        pos = jnp.broadcast_to(jnp.arange(s, dtype=jnp.float32)[None, :], (b, s))
        q = rope_alternate(q, pos)
        k = rope_alternate(k, pos)
        q = q / jnp.sqrt(jnp.float32(D)).astype(q.dtype)
        logits = jnp.einsum('bqhd,bkhd->bhqk', q, k)
        causal = jnp.where(jnp.tril(jnp.ones((s, s), dtype=bool))[None, None], 0.0, NEG_INF).astype(logits.dtype)
        probs = jax.nn.softmax(logits + causal, axis=-1)
        ctx = jnp.einsum('bhqk,bkhd->bqhd', probs, v).reshape(b, s, H * D)
        return jnp.einsum('bsf,fh->bsh', ctx, wo)

    def _L0_ffn_ref(x, w1s, w2s, w3s, W1, W2, W3, Wg):
        import jax, jax.numpy as jnp
        import numpy as np
        HIDDEN = 128
        INTER = 512
        N_EXPERTS = 8

        def geglu(x, w1, w2, w3):
            return jax.nn.gelu(x @ w1, approximate=False) * (x @ w2) @ w3
        B, T, C = x.shape
        xf = x.reshape(-1, C)
        shared = geglu(xf, w1s, w2s, w3s)
        logits = xf @ Wg
        idx = jnp.argmax(logits, axis=-1)
        final = jnp.zeros_like(xf)
        for e in range(N_EXPERTS):
            y = geglu(xf, W1[e], W2[e], W3[e])
            final = final + jnp.where((idx == e)[:, None], y, 0.0)
        return (shared + final).reshape(B, T, C)

    def _L1_attn_ref(x, wq, aq, bq, wk, ak, bk, wv, av, bv, wo, ao, bo):
        import jax, jax.numpy as jnp
        import numpy as np
        D_MODEL = 128
        N_HEADS = 16
        HEAD_DIM = D_MODEL // N_HEADS
        LORA_RANK = 16
        LORA_SCALING = 1.0 / LORA_RANK

        def lora_linear(x, w, a, b):
            return x @ w.T + LORA_SCALING * (x @ a.T @ b.T)
        B, S, _ = x.shape

        def split_heads(t):
            return t.reshape(B, S, N_HEADS, HEAD_DIM).transpose(0, 2, 1, 3)
        q = split_heads(lora_linear(x, wq, aq, bq))
        k = split_heads(lora_linear(x, wk, ak, bk))
        v = split_heads(lora_linear(x, wv, av, bv))
        scores = jnp.einsum('bhqd,bhkd->bhqk', q, k) / jnp.sqrt(jnp.float32(HEAD_DIM))
        causal = jnp.tril(jnp.ones((S, S), dtype=bool))
        scores = jnp.where(causal, scores, -jnp.inf)
        attn = jax.nn.softmax(scores, axis=-1)
        ctx = jnp.einsum('bhqk,bhkd->bhqd', attn, v)
        ctx = ctx.transpose(0, 2, 1, 3).reshape(B, S, D_MODEL)
        return lora_linear(ctx, wo, ao, bo)

    def _L1_ffn_ref(x, gate_w, w1, w2):
        import jax, jax.numpy as jnp
        import numpy as np
        NUM_EXPERTS = 8
        EXPERT_CAPACITY = 2.0
        DIM = 128
        HIDDEN_DIM = 512
        n, t, d = x.shape
        e = gate_w.shape[0]
        k = int(EXPERT_CAPACITY * t / e)
        scores = jnp.einsum('ntd,ed->nte', x, gate_w)
        probs = jax.nn.softmax(scores, axis=-1)
        g, m = jax.lax.top_k(probs.transpose(0, 2, 1), k)
        batch_idx = jnp.arange(n)[:, None, None]
        xin = x[batch_idx, m]
        h = jnp.einsum('nekd,edf->nekf', xin, w1)
        h = jax.nn.gelu(h, approximate=False)
        h = jnp.einsum('nekf,efd->nekd', h, w2)
        out_tok = g[..., None] * h
        out = jnp.zeros((n, t, d), dtype=x.dtype).at[batch_idx, m].add(out_tok)
        return out
    x = L0_attn_x
    mod = (_silu(L0_c) @ L0_wmod).reshape(L0_c.shape[0], 6, 1, -1)
    sa, ca, ga, sb, cb, gb = (mod[:, 0], mod[:, 1], mod[:, 2], mod[:, 3], mod[:, 4], mod[:, 5])
    ga = (2 * (ga >= 0) - 1) * jnp.maximum(jnp.abs(ga), 0.25)
    gb = (2 * (gb >= 0) - 1) * jnp.maximum(jnp.abs(gb), 0.25)
    h = _layernorm(x, axis=-1) * (1 + ca) + sa
    x = x + ga * _L0_attn_ref(h, L0_attn_wqkv, L0_attn_wo)
    h = _layernorm(x, axis=-1) * (1 + cb) + sb
    x = x + gb * _L0_ffn_ref(h, L0_ffn_w1s, L0_ffn_w2s, L0_ffn_w3s, L0_ffn_W1, L0_ffn_W2, L0_ffn_W3, L0_ffn_Wg)
    mod = (_silu(L1_c) @ L1_wmod).reshape(L1_c.shape[0], 6, 1, -1)
    sa, ca, ga, sb, cb, gb = (mod[:, 0], mod[:, 1], mod[:, 2], mod[:, 3], mod[:, 4], mod[:, 5])
    ga = (2 * (ga >= 0) - 1) * jnp.maximum(jnp.abs(ga), 0.25)
    gb = (2 * (gb >= 0) - 1) * jnp.maximum(jnp.abs(gb), 0.25)
    h = _layernorm(x, axis=-1) * (1 + ca) + sa
    x = x + ga * _L1_attn_ref(h, L1_attn_wq, L1_attn_aq, L1_attn_bq, L1_attn_wk, L1_attn_ak, L1_attn_bk, L1_attn_wv, L1_attn_av, L1_attn_bv, L1_attn_wo, L1_attn_ao, L1_attn_bo)
    h = _layernorm(x, axis=-1) * (1 + cb) + sb
    x = x + gb * _L1_ffn_ref(h, L1_ffn_gate_w, L1_ffn_w1, L1_ffn_w2)
    return x

_drawn_inputs = setup_inputs


def setup_inputs(seed=0):
    import zlib

    import numpy as np

    out = dict(_drawn_inputs(seed))
    spreads = {}
    factors = {'L0_ffn_w1s': 8.0,
     'L0_ffn_w2s': 8.0,
     'L0_ffn_w3s': 8.0,
     'L0_ffn_W1': 8.0,
     'L0_ffn_W2': 8.0,
     'L0_ffn_W3': 8.0,
     'L0_ffn_Wg': 8.0,
     'L1_attn_wq': 8.0,
     'L1_attn_aq': 38.304,
     'L1_attn_bq': 38.683,
     'L1_attn_wk': 8.0,
     'L1_attn_ak': 36.629,
     'L1_attn_bk': 37.856,
     'L1_attn_wv': 8.0,
     'L1_attn_av': 56.372,
     'L1_attn_bv': 59.063,
     'L1_attn_wo': 8.0,
     'L1_attn_ao': 59.765,
     'L1_attn_bo': 59.132,
     'L1_ffn_gate_w': 8.0,
     'L1_ffn_w1': 8.0,
     'L1_ffn_w2': 8.0,
     'L1_c': 8.0,
     'L1_wmod': 8.0}
    for name, (base, spread) in spreads.items():
        noise = np.random.default_rng([zlib.crc32(name.encode()), seed]).standard_normal(out[name].shape)
        drawn = base * np.exp(spread * noise) if base else spread * noise
        out[name] = jnp.asarray(drawn.astype(out[name].dtype))
    for name, factor in factors.items():
        out[name] = (out[name] * factor).astype(out[name].dtype)
    return out
```

```python
from contextlib import ExitStack

import numpy as np

import concourse.bass as bass
from concourse import mybir

ALU = mybir.AluOpType
ACT = mybir.ActivationFunctionType
F32 = mybir.dt.float32
F16 = mybir.dt.float16
BF16 = mybir.dt.bfloat16
AX_X = mybir.AxisListType.X

P = 128
B, S, D = 2, 1024, 128
TPB = S // P
NT = B * TPB
H = 16
HD0, HD1 = 64, 8
FF = 512
FC = FF // P
NE = 8
TOPK = 2 * S // NE
BANK = 512
EPS = 1e-5
MASKED = -1e30
SA, CA, GA, SB, CB, GB = range(6)


class Core:

    def __init__(self, nc):
        self.nc = nc
        self.n = 0

    def scope(self):
        return Scope(self)


class Scope(ExitStack):

    def __init__(self, core):
        super().__init__()
        self.core = core

    def _name(self, name):
        self.core.n += 1
        return f"{name}_{self.core.n}"

    def sbuf(self, name, shape, dt):
        return self.enter_context(self.core.nc.sbuf_tensor(self._name(name), shape, dt))

    def psum(self, name, shape, dt=F32):
        return self.enter_context(self.core.nc.psum_tensor(self._name(name), shape, dt))

    def sem(self, name):
        handle = self.enter_context(self.core.nc.semaphore(self._name(name)))
        self.callback(lambda: self.core.nc.gpsimd.sem_clear(handle))
        return handle

    def block(self):
        return self.enter_context(self.core.nc.Block())


class Consts:
    pass


def load_constants(core, top, ins):
    c = Consts()
    c.x = top.sbuf("x", [P, NT, D], F32)
    c.identf = top.sbuf("identf", [P, P], F32)
    c.identh = top.sbuf("identh", [P, P], F16)
    c.identb = top.sbuf("identb", [P, P], BF16)
    c.causal = top.sbuf("causal", [P, P], BF16)
    c.hT = top.sbuf("hT", [P, NT * P], F32)
    c.mod = [top.sbuf(f"mod{layer}", [P, 6, B], F32) for layer in range(2)]
    c.gate_b = [top.sbuf(f"gate_b{layer}", [P, B, D], F32) for layer in range(2)]
    with core.scope() as s:
        loaded, made = s.sem("loaded"), s.sem("made")
        block = s.block()

        @block.sync
        def _(sp):
            sp.dma_start(c.x[:], ins["L0_attn_x"].rearrange("b (t p) d -> p (b t) d", p=P)).then_inc(loaded, 16)
            sp.wait_ge(loaded, 16)

        @block.gpsimd
        def _(pool):
            pool.memset(c.identf[:], 0.0).then_inc(made, 1)
            pool.memset(c.causal[:], 0.0).then_inc(made, 1)
            pool.wait_ge(made, 2)
            pool.affine_select(out=c.identf[:], in_=c.identf[:], compare_op=ALU.not_equal, fill=1.0, base=0,
                               pattern=[[-1, P]], channel_multiplier=1).then_inc(made, 1)
            pool.affine_select(out=c.causal[:], in_=c.causal[:], compare_op=ALU.is_ge, fill=MASKED, base=0,
                               pattern=[[-1, P]], channel_multiplier=1).then_inc(made, 1)
            pool.wait_ge(made, 4)
            pool.tensor_copy(c.identh[:], c.identf[:]).then_inc(made, 1)
            pool.tensor_copy(c.identb[:], c.identf[:]).then_inc(made, 1)
    return c


def modulation(core, c, layer, cond, wmod):
    with core.scope() as s:
        ct = s.sbuf("ct", [P, B], F32)
        wm = s.sbuf("wm", [P, 6 * D], F32)
        ex = s.sbuf("ex", [P, B], F32)
        silu = s.sbuf("silu", [P, B], F32)
        silu_b = s.sbuf("silu_b", [P, B, P], F32)
        g = s.sbuf("g", [P, 2, B, P], F32)
        mod_ps = s.psum("mod_ps", [P, 6, B])
        row_ps = s.psum("row_ps", [P, B, D])
        loaded, exped, silu_ready, products, step = (s.sem(n) for n in ("loaded", "exped", "silu", "products", "step"))
        block = s.block()

        @block.sync
        def _(sp):
            sp.dma_start(ct[:], cond).then_inc(loaded, 16)
            sp.dma_start(wm[:], wmod).then_inc(loaded, 16)

        @block.scalar
        def _(act):
            act.wait_ge(loaded, 32)
            act.activation(ex[:], ct[:], ACT.Exp, scale=-1.0).then_inc(exped, 1)

        @block.tensor
        def _(pe):
            pe.wait_ge(silu_ready, 2)
            for j in range(6):
                pe.matmul(mod_ps[:, j, :], wm[:, j * D:(j + 1) * D], silu[:], start=True, stop=True)
            for b in range(B):
                last = pe.matmul(row_ps[:, b, :], silu_b[:, b, :], wm[:, GB * D:(GB + 1) * D], start=True, stop=True)
            last.then_inc(products, 1)

        @block.vector
        def _(dve):
            dve.wait_ge(exped, 1)
            dve.tensor_scalar(ex[:], ex[:], 1.0, None, ALU.add).then_inc(step, 1)
            dve.wait_ge(step, 1)
            dve.reciprocal(ex[:], ex[:]).then_inc(step, 1)
            dve.wait_ge(step, 2)
            dve.tensor_tensor(silu[:], ex[:], ct[:], ALU.mult).then_inc(silu_ready, 1)
            dve.wait_ge(silu_ready, 1)
            dve.tensor_copy(silu_b[:], silu[:].unsqueeze(2).broadcast_to([P, B, P])).then_inc(silu_ready, 1)
            dve.wait_ge(products, 1)
            mod = c.mod[layer]
            dve.tensor_copy(mod[:], mod_ps[:]).then_inc(step, 1)
            dve.tensor_copy(c.gate_b[layer][:], row_ps[:]).then_inc(step, 1)
            dve.wait_ge(step, 4)
            n = 4
            for j in (CA, CB):
                dve.tensor_scalar(mod[:, j, :], mod[:, j, :], 1.0, None, ALU.add).then_inc(step, 1)
                n += 1
            for gate, sgn, mag in ((mod[:, GA, :], g[:, 0, :, 0], g[:, 1, :, 0]), (c.gate_b[layer][:], g[:, 0], g[:, 1])):
                dve.wait_ge(step, n)
                dve.tensor_scalar(sgn, gate, 0.0, 2.0, ALU.is_ge, ALU.mult).then_inc(step, 1)
                dve.tensor_scalar(mag, gate, -1.0, None, ALU.mult).then_inc(step, 1)
                dve.wait_ge(step, n + 2)
                dve.tensor_tensor(mag, mag, gate, ALU.max).then_inc(step, 1)
                dve.tensor_scalar(sgn, sgn, -1.0, None, ALU.add).then_inc(step, 1)
                dve.wait_ge(step, n + 4)
                dve.tensor_scalar(mag, mag, 0.25, None, ALU.max).then_inc(step, 1)
                dve.wait_ge(step, n + 5)
                dve.tensor_tensor(gate, mag, sgn, ALU.mult).then_inc(step, 1)
                n += 6


def norm_modulate(core, c, layer, shift, scale):
    mod = c.mod[layer]
    with core.scope() as s:
        xc = s.sbuf("xc", [P, NT, D], F32)
        sq = s.sbuf("sq", [P, NT, D], F32)
        mean = s.sbuf("mean", [P, NT], F32)
        var = s.sbuf("var", [P, NT], F32)
        xT = [s.psum(f"xT{i}", [P, BANK]) for i in range(4)]
        step, squared, rooted, xhat, turned = (s.sem(n) for n in ("step", "squared", "rooted", "xhat", "turned"))
        block = s.block()
        per_bank = BANK // P

        def bcast(v):
            return v.unsqueeze(2).broadcast_to([P, NT, D])

        @block.vector
        def _(dve):
            dve.tensor_reduce(mean[:], c.x[:], AX_X, ALU.add).then_inc(step, 1)
            dve.wait_ge(step, 1)
            dve.tensor_scalar(mean[:], mean[:], 1.0 / D, None, ALU.mult).then_inc(step, 1)
            dve.wait_ge(step, 2)
            dve.tensor_tensor(xc[:], c.x[:], bcast(mean[:]), ALU.subtract).then_inc(step, 1)
            dve.wait_ge(squared, 1)
            dve.tensor_reduce(var[:], sq[:], AX_X, ALU.add).then_inc(step, 1)
            dve.wait_ge(step, 4)
            dve.tensor_scalar(var[:], var[:], 1.0 / D, EPS, ALU.mult, ALU.add).then_inc(step, 1)
            dve.wait_ge(rooted, 1)
            dve.reciprocal(var[:], var[:]).then_inc(step, 1)
            dve.wait_ge(step, 6)
            for q in range(4):
                part = slice(q * per_bank, (q + 1) * per_bank)
                dve.tensor_tensor(xc[:, part, :], xc[:, part, :],
                                  var[:, part].unsqueeze(2).broadcast_to([P, per_bank, D]), ALU.mult).then_inc(xhat, 1)

        @block.scalar
        def _(act):
            act.wait_ge(step, 3)
            act.activation(sq[:], xc[:], ACT.Square).then_inc(squared, 1)
            act.wait_ge(step, 5)
            act.activation(var[:], var[:], ACT.Sqrt).then_inc(rooted, 1)
            for q in range(4):
                b = q * per_bank // TPB
                act.wait_ge(turned, q + 1)
                act.activation(c.hT[:, q * BANK:(q + 1) * BANK], xT[q][:], ACT.Identity,
                               bias=mod[:, shift, b:b + 1], scale=mod[:, scale, b:b + 1])

        @block.tensor
        def _(pe):
            for q in range(4):
                pe.wait_ge(xhat, q + 1)
                for k in range(per_bank):
                    last = pe.transpose(xT[q][:, k * P:(k + 1) * P], xc[:, q * per_bank + k, :], c.identf[:])
                last.then_inc(turned, 1)


def project_rope(core, c, b, wqkv, rope, Qp, Kp, V):
    CH = 6
    QK = 4
    HPC = BANK // HD0
    with core.scope() as s:
        h_tile = [s.sbuf(f"h_tile{i}", [P, P], F32) for i in range(2)]
        by_cos = [s.sbuf(f"by_cos{i}", [P, HPC, 2, HD0 // 2], F32) for i in range(2)]
        by_sin = [s.sbuf(f"by_sin{i}", [P, HPC, 2, HD0 // 2], F32) for i in range(2)]
        turned = [s.sbuf(f"turned{i}", [P, HPC, 2, HD0 // 2], F32) for i in range(2)]
        parts = [s.sbuf(f"parts{i}", [P, QK, HPC, 2, HD0], F16) for i in range(2)]
        proj = [s.psum(f"proj{i}", [P, BANK]) for i in range(4)]
        partsT = [s.psum(f"partsT{i}", [P, HPC, P], F16) for i in range(2)]
        (h_ready, projected, rope_read, v_read, roped, hi_done, lo_done, t_done, t_read) = (
            s.sem(n) for n in ("h_ready", "projected", "rope_read", "v_read", "roped", "hi_done", "lo_done",
                               "t_done", "t_read"))
        block = s.block()
        LOOPS = TPB // 2

        @block.tensor
        def _(pe):
            with pe.Fori(0, LOOPS, 1) as it:
                for a in range(2):
                    pe.wait_ge(h_ready, 2 * it + a + 1)
                    for ch in range(CH):
                        g = a * CH + ch - 4
                        tile, before = g // CH, g % CH
                        if before < QK:
                            pe.wait_ge(rope_read, (2 * it + tile + 1) * QK + before + 1)
                        else:
                            pe.wait_ge(v_read, (2 * it + tile + 1) * 2 + before - QK + 1)
                        pe.matmul(proj[(a * CH + ch) % 4][:], h_tile[a][:], wqkv[:, ch * BANK:(ch + 1) * BANK],
                                  start=True, stop=True).then_inc(projected, 1)
                for a in range(2):
                    for ch in range(QK):
                        g = a * QK + ch
                        pe.wait_ge(lo_done, 2 * QK * it + g + 1 + 2)
                        pe.wait_ge(t_read, 2 * QK * it + g + 1)
                        for h in range(HPC):
                            last = pe.transpose(partsT[g % 2][:, h, :],
                                                parts[a][:, ch, h].rearrange("p a d -> p (a d)"), c.identh[:])
                        last.then_inc(t_done, 1)

        @block.vector
        def _(dve):
            dve.sem_inc(rope_read, QK)
            dve.sem_inc(lo_done, 2)
            with dve.Fori(0, LOOPS, 1) as it:
                def low_part(g):
                    dve.wait_ge(hi_done, 2 * QK * it + g + 1)
                    dve.tensor_tensor(parts[g // QK][:, g % QK, :, 1, :],
                                      turned[g % 2][:].rearrange("p h a d -> p h (a d)"),
                                      parts[g // QK][:, g % QK, :, 0, :], ALU.subtract).then_inc(lo_done, 1)
                for a in range(2):
                    for ch in range(QK):
                        g = a * QK + ch
                        table = 2 * (ch // 2)
                        dve.wait_ge(projected, 2 * CH * it + a * CH + ch + 1)
                        dve.wait_ge(roped, 2 * QK * it + g + 1)
                        src = proj[(a * CH + ch) % 4][:].rearrange("p (h a d) -> p h a d", h=HPC, a=2)
                        for out, t in ((by_cos, table), (by_sin, table + 1)):
                            tab = rope[:, 2 * it + a, t, :].rearrange("p (a d) -> p a d", a=2)
                            last = dve.tensor_tensor(out[g % 2][:].rearrange("p h a d -> p h (a d)"),
                                                     src.rearrange("p h a d -> p h (a d)"),
                                                     rope[:, 2 * it + a, t, :].unsqueeze(1).broadcast_to([P, HPC, HD0]),
                                                     ALU.mult)
                        last.then_inc(rope_read, 1)
                        if g >= 1:
                            low_part(g - 1)
                low_part(2 * QK - 1)

        @block.gpsimd
        def _(pool):
            pool.sem_inc(roped, 2)
            with pool.Fori(0, LOOPS, 1) as it:
                for g in range(2 * QK):
                    pool.wait_ge(rope_read, 2 * QK * it + g + 1 + QK)
                    pool.wait_ge(lo_done, 2 * QK * it + g + 1)
                    for half in range(2):
                        last = pool.tensor_tensor(turned[g % 2][:, :, half, :], by_cos[g % 2][:, :, half, :],
                                                  by_sin[g % 2][:, :, 1 - half, :], ALU.add)
                    last.then_inc(roped, 1)

        @block.scalar
        def _(act):
            act.sem_inc(v_read, 2)
            act.sem_inc(t_read, 2)
            act.sem_inc(t_done, 2 * QK)
            with act.Fori(0, LOOPS, 1) as it:
                for a in range(2):
                    act.copy(h_tile[a][:], c.hT[:, bass.ds((2 * it + a) * P + b * S, P)]).then_inc(h_ready, 1)
                for a in range(2):
                    for ch in range(QK):
                        g = a * QK + ch
                        act.wait_ge(roped, 2 * QK * it + g + 1 + 2)
                        act.wait_ge(t_done, 2 * QK * it + g + 1)
                        act.copy(parts[a][:, ch, :, 0, :],
                                 turned[g % 2][:].rearrange("p h a d -> p h (a d)")).then_inc(hi_done, 1)
                    for half in range(2):
                        act.wait_ge(projected, 2 * CH * it + a * CH + QK + half + 1)
                        act.copy(V[:, 2 * it + a, half * BANK:(half + 1) * BANK],
                                 proj[(a * CH + QK + half) % 4][:]).then_inc(v_read, 1)
                for a in range(2):
                    for ch in range(QK):
                        g = a * QK + ch
                        act.wait_ge(t_done, 2 * QK * it + g + 1 + 2 * QK)
                        dst = Qp if ch < 2 else Kp
                        act.copy(dst[:, (ch % 2) * HPC:(ch % 2 + 1) * HPC, bass.ds((2 * it + a) * P, P)],
                                 partsT[g % 2][:]).then_inc(t_read, 1)


def attend(core, c, U, Qp, Kp, V, ctxT, q_orders, k_heads):
    UNITS = H // U
    HW = P // U
    chunks = [1 if i < 4 else 2 for i in range(TPB)]
    CPU = U * sum(chunks)
    items = [(i, h) for i in range(TPB) for h in range(U)]
    first_chunk = {}
    n = 0
    for i, h in items:
        first_chunk[i, h] = n
        n += chunks[i]
    N = len(items)
    through = {i: U * sum(chunks[:i + 1]) // 2 for i in range(TPB)}
    with core.scope() as s:
        Qs = [s.sbuf(f"Qs{i}", [P, q_orders, U, S], F16) for i in range(2)]
        Ks = [s.sbuf(f"Ks{i}", [P, k_heads, S], F16) for i in range(2)]
        Vs = [s.sbuf(f"Vs{i}", [P, TPB, U, HW], F32) for i in range(2)]
        prob = [s.sbuf(f"prob{i}", [P, S], F32) for i in range(2)]
        probT = [s.sbuf(f"probT{i}", [P, U, S], F32) for i in range(2)]
        negmax = s.sbuf("negmax", [P, 4], F32)
        total = s.sbuf("total", [P, 2, U], F32)
        inv = s.sbuf("inv", [P, 2, U], F32)
        inv_b = [s.sbuf(f"inv_b{i}", [P, U, HW], F32) for i in range(2)]
        inv_row = [s.sbuf(f"inv_row{i}", [P, P], F32) for i in range(2)]
        score = [s.psum(f"score{i}", [P, S]) for i in range(2)]
        probT_ps = [s.psum(f"probT_ps{i}", [P, BANK]) for i in range(2)]
        ctx_ps = [s.psum(f"ctx_ps{i}", [P, 2, P]) for i in range(2)]
        staged = [s.sem(f"staged{i}") for i in range(2)]
        (scored, maxed, exped, t_done, inv_ready, inv_rowed, inv_copied, pv_done, ctx_done, chain) = (
            s.sem(n) for n in ("scored", "maxed", "exped", "t_done", "inv_ready", "inv_rowed", "inv_copied",
                               "pv_done", "ctx_done", "chain"))
        evac = [s.sem(f"evac{i}") for i in range(2)]
        block = s.block()
        LOOPS = UNITS // 2
        DMAS = (1 if q_orders == 1 else 3) + 2

        @block.sync
        def _(sp):
            def load(u, a):
                heads = bass.ds(u * U, U)
                sp.dma_start(Qs[a][:, 0], Qp[:, heads, :]).then_inc(staged[a], 16)
                if q_orders == 2:
                    sp.dma_start(Qs[a][0:HD0, 1], Qp[HD0:P, heads, :]).then_inc(staged[a], 16)
                    sp.dma_start(Qs[a][HD0:P, 1], Qp[0:HD0, heads, :]).then_inc(staged[a], 16)
                sp.dma_start(Ks[a][:], Kp[:, bass.ds(u * k_heads, k_heads), :]).then_inc(staged[a], 16)
                sp.dma_start(Vs[a][:].rearrange("p t h d -> p t (h d)"), V[:, :, bass.ds(u * P, P)]).then_inc(staged[a], 16)
            load(0, 0)
            load(1, 1)
            with sp.Fori(0, LOOPS - 1, 1) as it:
                for a in range(2):
                    sp.wait_ge(ctx_done, (2 * it + a + 1) * TPB + 2)
                    load(2 * it + a + 2, a)

        @block.tensor
        def _(pe):
            with pe.Fori(0, LOOPS, 1) as it:
                for a in range(2):
                    def item(n):
                        return (2 * it + a) * N + n

                    def scores(n):
                        i, h = items[n]
                        out = score[n % 2]
                        pe.wait_ge(exped, item(n) + 1)
                        width = (i + 1) * P
                        for order in range(q_orders):
                            for k0 in range(0, width, BANK):
                                k1 = min(k0 + BANK, width)
                                pe.matmul(out[:, k0:k1], Qs[a][:, order, h, i * P:(i + 1) * P],
                                          Ks[a][:, h if k_heads > 1 else 0, k0:k1], start=(order == 0),
                                          stop=(order == q_orders - 1 and k1 < width))
                        pe.matmul(out[:, i * P:width], c.identb[:], c.causal[:], start=False,
                                  stop=True).then_inc(scored, 1)

                    def turn(n):
                        i, h = items[n]
                        pe.wait_ge(exped, item(n) + 1 + 2)
                        for k in range(chunks[i]):
                            m = first_chunk[i, h] + k
                            pe.wait_ge(evac[m % 2], (2 * it + a) * (CPU // 2) + m // 2 + 1)
                            for j in range(4 * k, min(4 * k + 4, i + 1)):
                                last = pe.transpose(probT_ps[m % 2][:, (j % 4) * P:(j % 4 + 1) * P],
                                                    prob[n % 2][:, j * P:(j + 1) * P], c.identf[:])
                            last.then_inc(t_done, 1)

                    def context(i):
                        tile = (2 * it + a) * TPB + i
                        pe.wait_ge(ctx_done, tile + 1)
                        pe.wait_ge(inv_ready, tile + 1 + 2)
                        pe.matmul(ctx_ps[i % 2][:, 1, :], inv_b[i % 2][:].rearrange("p h d -> p (h d)"), c.identf[:],
                                  start=True, stop=True).then_inc(inv_rowed, 1)
                        for e in range(2):
                            pe.wait_ge(evac[e], (2 * it + a) * (CPU // 2) + through[i] + 1)
                        for j in range(i + 1):
                            for h in range(U):
                                last = pe.matmul(ctx_ps[i % 2][h * HW:(h + 1) * HW, 0, :], Vs[a][:, j, h, :],
                                                 probT[i % 2][:, h, j * P:(j + 1) * P], start=(j == 0), stop=(j == i))
                        last.then_inc(pv_done, 1)

                    pe.wait_ge(staged[a], (it + 1) * (16 * DMAS))
                    scores(0)
                    for n in range(N):
                        if n + 1 < N:
                            scores(n + 1)
                        turn(n)
                        i, h = items[n]
                        if h == 0 and i >= 1:
                            context(i - 1)
                    context(TPB - 1)

        def evacuate(eng, copy, it, a, n, e):
            i, h = items[n]
            for k in range(chunks[i]):
                m = first_chunk[i, h] + k
                if m % 2 != e:
                    continue
                eng.wait_ge(t_done, (2 * it + a) * CPU + m + 1 + 4)
                eng.wait_ge(pv_done, (2 * it + a) * TPB + i + 1)
                width = min(4, i + 1 - 4 * k) * P
                copy(probT[i % 2][:, h, 4 * k * P:4 * k * P + width], probT_ps[m % 2][:, 0:width]).then_inc(evac[e], 1)

        @block.vector
        def _(dve):
            dve.sem_inc(evac[0], 1)
            dve.sem_inc(ctx_done, 2)
            dve.sem_inc(pv_done, 2)
            with dve.Fori(0, LOOPS, 1) as it:
                for a in range(2):
                    u = 2 * it + a

                    def invert(i):
                        tile = u * TPB + i
                        dve.wait_ge(exped, u * N + (i + 1) * U + 2)
                        dve.wait_ge(inv_rowed, tile + 1)
                        dve.reciprocal(inv[:, i % 2, :], total[:, i % 2, :]).then_inc(chain, 1)
                        dve.wait_ge(chain, tile + 1)
                        dve.tensor_copy(inv_b[i % 2][:], inv[:, i % 2, :].unsqueeze(2).broadcast_to([P, U, HW]))\
                           .then_inc(inv_ready, 1)

                    def normalise(i):
                        tile = u * TPB + i
                        dve.wait_ge(inv_copied, tile + 1 + 2)
                        dve.tensor_tensor(ctxT[:, u, i * P:(i + 1) * P], ctx_ps[i % 2][:, 0, :], inv_row[i % 2][:],
                                          ALU.mult).then_inc(ctx_done, 1)

                    for n in range(N):
                        i, h = items[n]
                        dve.wait_ge(scored, u * N + n + 1)
                        dve.wait_ge(exped, u * N + n + 1)
                        dve.tensor_reduce(negmax[:, n % 4:n % 4 + 1], score[n % 2][:, 0:(i + 1) * P], AX_X, ALU.max,
                                          negate=True).then_inc(maxed, 1)
                        if n >= 1:
                            evacuate(dve, dve.tensor_copy, it, a, n - 1, 0)
                        if h == 0 and i >= 1:
                            invert(i - 1)
                        if h == 1 and i >= 1:
                            normalise(i - 1)
                    evacuate(dve, dve.tensor_copy, it, a, N - 1, 0)
                    invert(TPB - 1)
                    normalise(TPB - 1)

        @block.scalar
        def _(act):
            act.sem_inc(exped, 2)
            act.sem_inc(evac[1], 1)
            act.sem_inc(t_done, 4)
            act.sem_inc(inv_rowed, 2)
            act.sem_inc(inv_copied, 2)
            act.sem_inc(inv_ready, 2)
            with act.Fori(0, LOOPS, 1) as it:
                for a in range(2):
                    u = 2 * it + a

                    def copy_row(i):
                        tile = u * TPB + i
                        act.wait_ge(pv_done, tile + 1 + 2)
                        act.wait_ge(ctx_done, tile + 1)
                        act.copy(inv_row[i % 2][:], ctx_ps[i % 2][:, 1, :]).then_inc(inv_copied, 1)

                    for n in range(N):
                        i, h = items[n]
                        act.wait_ge(maxed, u * N + n + 1)
                        before = first_chunk[items[n - 2]] + chunks[items[n - 2][0]] - (CPU if n < 2 else 0)
                        act.wait_ge(t_done, u * CPU + before + 4)
                        if h == 0:
                            act.wait_ge(inv_ready, u * TPB + i + 1)
                        act.activation(prob[n % 2][:, 0:(i + 1) * P], score[n % 2][:, 0:(i + 1) * P], ACT.Exp,
                                       bias=negmax[:, n % 4:n % 4 + 1], accum_out=total[:, i % 2, h:h + 1])\
                           .then_inc(exped, 1)
                        if n >= 1:
                            evacuate(act, act.copy, it, a, n - 1, 1)
                        if h == 1 and i >= 1:
                            copy_row(i - 1)
                    evacuate(act, act.copy, it, a, N - 1, 1)
                    copy_row(TPB - 1)


def project_out(core, c, b, layer, units, ctxT, wo):
    HALF = S // BANK
    with core.scope() as s:
        y = [s.sbuf(f"y{i}", [P, BANK], F32) for i in range(HALF)]
        y_ps = [s.psum(f"y_ps{i}", [P, BANK]) for i in range(HALF)]
        yT = [s.psum(f"yT{i}", [P, BANK]) for i in range(HALF)]
        summed, gated, turned = (s.sem(n) for n in ("summed", "gated", "turned"))
        block = s.block()

        @block.tensor
        def _(pe):
            for half in range(HALF):
                for u in range(units):
                    last = pe.matmul(y_ps[half][:], wo[:, u, :], ctxT[:, u, half * BANK:(half + 1) * BANK],
                                     start=(u == 0), stop=(u == units - 1))
                last.then_inc(summed, 1)
            for half in range(HALF):
                pe.wait_ge(gated, half + 1)
                for k in range(BANK // P):
                    last = pe.transpose(yT[half][:, k * P:(k + 1) * P], y[half][:, k * P:(k + 1) * P], c.identf[:])
                last.then_inc(turned, 1)

        @block.scalar
        def _(act):
            for half in range(HALF):
                act.wait_ge(summed, half + 1)
                act.activation(y[half][:], y_ps[half][:], ACT.Copy, scale=c.mod[layer][:, GA, b:b + 1])\
                   .then_inc(gated, 1)

        @block.vector
        def _(dve):
            for half in range(HALF):
                dve.wait_ge(turned, half + 1)
                t0 = b * TPB + half * (BANK // P)
                xs = c.x[:, t0:t0 + BANK // P, :].rearrange("p t d -> p (t d)")
                dve.tensor_tensor(xs, yT[half][:], xs, ALU.add)


def route_top1(core, c, wg_in, pick):
    with core.scope() as s:
        wg = s.sbuf("wg", [P, NE], F32)
        best = s.sbuf("best", [P, NT], F32)
        place = s.sbuf("place", [P, NE], F32)
        hit = s.sbuf("hit", [P, NT, NE], F32)
        logits = s.psum("logits", [P, NT, NE])
        loaded, placed, scored, step = (s.sem(n) for n in ("loaded", "placed", "scored", "step"))
        block = s.block()

        @block.sync
        def _(sp):
            sp.dma_start(wg[:], wg_in).then_inc(loaded, 16)

        @block.gpsimd
        def _(pool):
            pool.iota(place[:], pattern=[[-1, NE]], base=NE, channel_multiplier=0,
                      allow_small_or_imprecise_dtypes=True).then_inc(placed, 1)

        @block.tensor
        def _(pe):
            pe.wait_ge(loaded, 16)
            for t in range(NT):
                last = pe.matmul(logits[:, t, :], c.hT[:, t * P:(t + 1) * P], wg[:], start=True, stop=True)
            last.then_inc(scored, 1)

        @block.vector
        def _(dve):
            def wide(v):
                return v.unsqueeze(2).broadcast_to([P, NT, NE])
            dve.memset(pick[:], 1.0).then_inc(step, 1)
            dve.wait_ge(scored, 1)
            dve.tensor_reduce(best[:], logits[:], AX_X, ALU.max).then_inc(step, 1)
            dve.wait_ge(step, 2)
            dve.tensor_tensor(hit[:], logits[:], wide(best[:]), ALU.is_ge).then_inc(step, 1)
            dve.wait_ge(step, 3)
            dve.wait_ge(placed, 1)
            dve.tensor_tensor(hit[:], hit[:], place[:].unsqueeze(1).broadcast_to([P, NT, NE]), ALU.mult).then_inc(step, 1)
            dve.wait_ge(step, 4)
            dve.tensor_reduce(best[:], hit[:], AX_X, ALU.max).then_inc(step, 1)
            dve.wait_ge(step, 5)
            dve.tensor_tensor(pick[:, :, 1:1 + NE], hit[:], wide(best[:]), ALU.is_equal).then_inc(step, 1)


def experts(core, c, up, up2, down, n, weight, acc):
    gated = up2 is not None
    CHUNKS = NT * P // BANK
    TPC = BANK // P
    E = min(n, 2)
    LOOPS = n // E
    STEPS = CHUNKS * FC
    DMAS = 3 if gated else 2
    with core.scope() as s:
        w_up = [s.sbuf(f"w_up{i}", [P, FF], F32) for i in range(E)]
        w_up2 = [s.sbuf(f"w_up2{i}", [P, FF], F32) for i in range(E)] if gated else None
        w_down = [s.sbuf(f"w_down{i}", [P, FC, D], F32) for i in range(E)]
        gelu = [s.sbuf(f"gelu{i}", [P, BANK], F32) for i in range(2)] if gated else None
        hidden = [s.sbuf(f"hidden{i}", [P, FC, BANK], F32) for i in range(2)]
        u_ps = [s.psum(f"u_ps{i}", [P, BANK]) for i in range(2)]
        u2_ps = [s.psum(f"u2_ps{i}", [P, BANK]) for i in range(2)] if gated else None
        y_ps = [s.psum(f"y_ps{i}", [P, TPC, D]) for i in range(2)]
        staged = [s.sem(f"staged{i}") for i in range(E)]
        upped, gelued, multiplied, y_ready, y_read = (
            s.sem(n) for n in ("upped", "gelued", "multiplied", "y_ready", "y_read"))
        hidden_ready = multiplied if gated else gelued
        block = s.block()

        def loop(eng):
            return eng.Fori(0, LOOPS, 1) if LOOPS > 1 else Once()

        @block.sync
        def _(sp):
            def load(e, a):
                sp.dma_start(w_up[a][:], up(e)).then_inc(staged[a], 16)
                if gated:
                    sp.dma_start(w_up2[a][:], up2(e)).then_inc(staged[a], 16)
                sp.dma_start(w_down[a][:], down(e)).then_inc(staged[a], 16)
            for a in range(E):
                load(a, a)
            if LOOPS > 1:
                with sp.Fori(0, LOOPS - 1, 1) as it:
                    for a in range(E):
                        sp.wait_ge(y_ready, (E * it + a + 1) * CHUNKS + 2)
                        load(E * it + a + E, a)

        @block.tensor
        def _(pe):
            pe.sem_inc(y_ready, 2)
            with loop(pe) as it:
                for a in range(E):
                    def down_product(ch):
                        g = (E * it + a) * CHUNKS + ch
                        pe.wait_ge(hidden_ready, (g + 1) * FC + 2)
                        pe.wait_ge(y_read, g + 1)
                        for t in range(TPC):
                            for f in range(FC):
                                last = pe.matmul(y_ps[ch % 2][:, t, :], hidden[ch % 2][:, f, t * P:(t + 1) * P],
                                                 w_down[a][:, f, :], start=(f == 0), stop=(f == FC - 1))
                        last.then_inc(y_ready, 1)

                    pe.wait_ge(staged[a], (it + 1) * (16 * DMAS))
                    for ch in range(CHUNKS):
                        rhs = c.hT[:, ch * BANK:(ch + 1) * BANK]
                        for f in range(FC):
                            k = (E * it + a) * STEPS + ch * FC + f
                            pe.wait_ge(gelued, k + 1)
                            pe.matmul(u_ps[f % 2][:], w_up[a][:, f * P:(f + 1) * P], rhs,
                                      start=True, stop=True).then_inc(upped, 1)
                            if gated:
                                pe.wait_ge(multiplied, k + 1)
                                pe.matmul(u2_ps[f % 2][:], w_up2[a][:, f * P:(f + 1) * P], rhs,
                                          start=True, stop=True).then_inc(upped, 1)
                            if f == 1 and ch >= 1:
                                down_product(ch - 1)
                    down_product(CHUNKS - 1)

        @block.scalar
        def _(act):
            act.sem_inc(gelued, 2)
            with loop(act) as it:
                for a in range(E):
                    for ch in range(CHUNKS):
                        for f in range(FC):
                            k = (E * it + a) * STEPS + ch * FC + f
                            if gated:
                                act.wait_ge(upped, 2 * k + 1)
                                act.wait_ge(multiplied, k + 1)
                                act.activation(gelu[f % 2][:], u_ps[f % 2][:], ACT.Gelu).then_inc(gelued, 1)
                            else:
                                act.wait_ge(upped, k + 1)
                                if f == 0:
                                    act.wait_ge(y_ready, (E * it + a) * CHUNKS + ch + 1)
                                act.activation(hidden[ch % 2][:, f, :], u_ps[f % 2][:], ACT.Gelu).then_inc(gelued, 1)

        @block.vector
        def _(dve):
            if gated:
                dve.sem_inc(multiplied, 2)
            dve.sem_inc(y_read, 2)
            with loop(dve) as it:
                for a in range(E):
                    def accumulate(ch):
                        g = (E * it + a) * CHUNKS + ch
                        dve.wait_ge(y_ready, g + 1 + 2)
                        dve.wait_ge(y_read, g + 2)
                        for t in range(TPC):
                            tile = ch * TPC + t
                            last = dve.scalar_tensor_tensor(out=acc[:, tile, :], in0=y_ps[ch % 2][:, t, :],
                                                            scalar=weight(tile, E * it + a), in1=acc[:, tile, :],
                                                            op0=ALU.mult, op1=ALU.add)
                        last.then_inc(y_read, 1)

                    for ch in range(CHUNKS):
                        if gated:
                            for f in range(FC):
                                k = (E * it + a) * STEPS + ch * FC + f
                                dve.wait_ge(gelued, k + 1 + 2)
                                dve.wait_ge(upped, 2 * k + 2)
                                if f == 0:
                                    dve.wait_ge(y_ready, (E * it + a) * CHUNKS + ch + 1)
                                dve.tensor_tensor(hidden[ch % 2][:, f, :], u2_ps[f % 2][:], gelu[f % 2][:],
                                                  ALU.mult).then_inc(multiplied, 1)
                        if ch >= 1:
                            accumulate(ch - 1)
                    accumulate(CHUNKS - 1)


class Once:

    def __enter__(self):
        return 0

    def __exit__(self, *_):
        return False


def clear(core, buffers):
    with core.scope() as s:
        block = s.block()

        @block.vector
        def _(dve):
            for buffer in buffers:
                dve.memset(buffer, 0.0)


def add_gated(core, c, layer, acc, out):
    with core.scope() as s:
        scaled, added, stored = s.sem("scaled"), s.sem("added"), s.sem("stored")
        block = s.block()

        @block.vector
        def _(dve):
            for b in range(B):
                part = acc[:, b * TPB:(b + 1) * TPB, :]
                dve.tensor_tensor(part, part, c.gate_b[layer][:, b, :].unsqueeze(1).broadcast_to([P, TPB, D]),
                                  ALU.mult).then_inc(scaled, 1)
            for b in range(B):
                tiles = slice(b * TPB, (b + 1) * TPB)
                dve.wait_ge(scaled, b + 1)
                dve.tensor_tensor(c.x[:, tiles, :], c.x[:, tiles, :], acc[:, tiles, :], ALU.add).then_inc(added, 1)

        @block.sync
        def _(sp):
            if out is not None:
                for b in range(B):
                    sp.wait_ge(added, b + 1)
                    sp.dma_start(out[b].rearrange("(t p) d -> p t d", p=P),
                                 c.x[:, b * TPB:(b + 1) * TPB, :]).then_inc(stored, 16)
                sp.wait_ge(stored, 16 * B)


def lora_weights(core, ins, wqkv, wo):
    RANK = 16
    with core.scope() as s:
        a_qkv = s.sbuf("a_qkv", [RANK, 3, D], F32)
        b_qkv = s.sbuf("b_qkv", [RANK, 3, D], F32)
        a_o = s.sbuf("a_o", [RANK, 4, P], F32)
        b_o = s.sbuf("b_o", [RANK, D], F32)
        low_qkv = s.psum("low_qkv", [P, 3, D])
        low_o = s.psum("low_o", [P, 4, D])
        loaded, product = s.sem("loaded"), s.sem("product")
        block = s.block()
        loads = ((a_qkv, "a_qkv"), (b_qkv, "b_qkv"), (a_o, "a_o"), (b_o, "b_o"), (wqkv, "w_qkv"), (wo, "w_o"))

        @block.sync
        def _(sp):
            for buffer, name in loads:
                sp.dma_start(buffer[:], ins["lora_" + name]).then_inc(loaded, 16)

        @block.tensor
        def _(pe):
            pe.wait_ge(loaded, 16 * len(loads))
            for j in range(3):
                last = pe.matmul(low_qkv[:, j, :], a_qkv[:, j, :], b_qkv[:, j, :], start=True, stop=True)
            last.then_inc(product, 1)
            for g in range(4):
                last = pe.matmul(low_o[:, g, :], a_o[:, g, :], b_o[:], start=True, stop=True)
            last.then_inc(product, 1)

        @block.vector
        def _(dve):
            dve.wait_ge(loaded, 16 * len(loads))
            dve.wait_ge(product, 2)
            dve.scalar_tensor_tensor(out=wqkv[:], in0=low_qkv[:], scalar=1.0 / RANK, in1=wqkv[:],
                                     op0=ALU.mult, op1=ALU.add)
            dve.scalar_tensor_tensor(out=wo[:], in0=low_o[:], scalar=1.0 / RANK, in1=wo[:],
                                     op0=ALU.mult, op1=ALU.add)


def project_narrow(core, c, b, wqkv, Qp, Kp, V):
    G = 4
    LOOPS = TPB // 2
    with core.scope() as s:
        h_tile = [s.sbuf(f"h_tile{i}", [P, P], F32) for i in range(2)]
        qk = [s.sbuf(f"qk{i}", [P, 2, H, HD1], F32) for i in range(2)]
        parts = [s.sbuf(f"parts{i}", [P, 2, H, 2, 2, HD1], F16) for i in range(2)]
        proj = [s.psum(f"proj{i}", [P, 3 * D]) for i in range(2)]
        partsT = [[s.psum(f"partsT{i}{j}", [P, 2, G, P], F16) for j in range(2)] for i in range(2)]
        h_ready, projected, copied, hi_done, lo_done, t_done, q_read, k_read = (
            s.sem(n) for n in ("h_ready", "projected", "copied", "hi_done", "lo_done", "t_done", "q_read", "k_read"))
        block = s.block()

        def slots(a, which):
            v = parts[a][:, which]
            return (v[:, :, :, 0, :], v[:, :, :, 1, :]) if which == 0 else (v[:, :, 0, :, :], v[:, :, 1, :, :])

        @block.tensor
        def _(pe):
            with pe.Fori(0, LOOPS, 1) as it:
                for a in range(2):
                    pe.wait_ge(h_ready, 2 * it + a + 1)
                    pe.wait_ge(copied, 2 * it + a + 1)
                    pe.matmul(proj[a][:], h_tile[a][:], wqkv[:].rearrange("p j d -> p (j d)"),
                              start=True, stop=True).then_inc(projected, 1)
                for a in range(2):
                    pe.wait_ge(lo_done, 2 * it + a + 1)
                    pe.wait_ge(q_read, 2 * it + a + 1)
                    pe.wait_ge(k_read, 2 * it + a + 1)
                    for which in range(2):
                        for g in range(G):
                            last = pe.transpose(partsT[a][which][:, 0, g, :],
                                                parts[a][:, which, g * G:(g + 1) * G].rearrange("p h a b d -> p (h a b d)"),
                                                c.identh[:])
                    last.then_inc(t_done, 1)

        @block.scalar
        def _(act):
            act.sem_inc(copied, 2)
            act.sem_inc(k_read, 2)
            with act.Fori(0, LOOPS, 1) as it:
                for a in range(2):
                    act.wait_ge(projected, 2 * it + a + 1)
                    act.copy(h_tile[a][:], c.hT[:, bass.ds((2 * it + a) * P + b * S, P)]).then_inc(h_ready, 1)
                for a in range(2):
                    act.wait_ge(projected, 2 * it + a + 1 + 2)
                    act.wait_ge(q_read, 2 * it + a + 1)
                    q, k, v = (proj[a][:, j * D:(j + 1) * D] for j in range(3))
                    act.mul(qk[a][:, 0].rearrange("p h d -> p (h d)"), q, float(HD1) ** -0.5)
                    act.copy(qk[a][:, 1].rearrange("p h d -> p (h d)"), k)
                    act.copy(V[:, 2 * it + a, :].rearrange("p (h d) -> p h d", h=H)[:, :, 0:HD1],
                             v.rearrange("p (h d) -> p h d", h=H)).then_inc(copied, 1)
                for a in range(2):
                    act.wait_ge(t_done, 2 * it + a + 1)
                    act.copy(Kp[:, :, bass.ds((2 * it + a) * P, P)], partsT[a][1][:, 0]).then_inc(k_read, 1)

        @block.vector
        def _(dve):
            dve.sem_inc(projected, 2)
            dve.sem_inc(q_read, 2)
            with dve.Fori(0, LOOPS, 1) as it:
                for a in range(2):
                    dve.wait_ge(copied, 2 * it + a + 1 + 2)
                    for which in range(2):
                        src = qk[a][:, which].unsqueeze(2).broadcast_to([P, H, 2, HD1])
                        last = dve.tensor_copy(slots(a, which)[0], src)
                    last.then_inc(hi_done, 1)
                    dve.wait_ge(hi_done, 2 * it + a + 1)
                    for which in range(2):
                        src = qk[a][:, which].unsqueeze(2).broadcast_to([P, H, 2, HD1])
                        last = dve.tensor_tensor(slots(a, which)[1], src, slots(a, which)[0], ALU.subtract)
                    last.then_inc(lo_done, 1)
                for a in range(2):
                    dve.wait_ge(t_done, 2 * it + a + 1)
                    q_heads = Qp[:].rearrange("p (g r) s -> p g r s", r=G)
                    for r in range(G):
                        rows = slice(32 * r, 32 * r + 32)
                        last = dve.tensor_copy(q_heads[rows, :, r, bass.ds((2 * it + a) * P, P)], partsT[a][0][rows, 0])
                    last.then_inc(q_read, 1)


def route_experts_choice(core, c, wg_in, weight):
    with core.scope() as s:
        wg = s.sbuf("wg", [P, NE], F32)
        peak = s.sbuf("peak", [P, NT], F32)
        prob = s.sbuf("prob", [P, NT, NE], F32)
        prob_t = s.sbuf("prob_t", [P, TPB, B, NE], F32)
        rows = s.sbuf("rows", [B * NE, S], F32)
        left = s.sbuf("left", [B * NE, S], F32)
        top = s.sbuf("top", [B * NE, 8], F32)
        logits = s.psum("logits", [P, NT, NE])
        rows_ps = [s.psum(f"rows_ps{i}", [B * NE, BANK]) for i in range(2)]
        weight_ps = s.psum("weight_ps", [P, TPB, B, NE])
        loaded, scored, exped, step, turned, found, back = (
            s.sem(n) for n in ("loaded", "scored", "exped", "step", "turned", "found", "back"))
        block = s.block()

        @block.sync
        def _(sp):
            sp.dma_start(wg[:], wg_in).then_inc(loaded, 16)

        @block.tensor
        def _(pe):
            pe.wait_ge(loaded, 16)
            for t in range(NT):
                last = pe.matmul(logits[:, t, :], c.hT[:, t * P:(t + 1) * P], wg[:], start=True, stop=True)
            last.then_inc(scored, 1)
            pe.wait_ge(step, 6)
            for t in range(TPB):
                last = pe.transpose(rows_ps[t // 4][:, (t % 4) * P:(t % 4 + 1) * P],
                                    prob_t[:, t].rearrange("p b e -> p (b e)"), c.identf[:])
            last.then_inc(turned, 1)
            pe.wait_ge(back, 1)
            for t in range(TPB):
                last = pe.transpose(weight_ps[:, t].rearrange("p b e -> p (b e)"), rows[:, t * P:(t + 1) * P],
                                    c.identf[0:B * NE, 0:B * NE])
            last.then_inc(turned, 1)

        @block.scalar
        def _(act):
            act.wait_ge(step, 2)
            act.activation(prob[:], prob[:], ACT.Exp).then_inc(exped, 1)

        @block.vector
        def _(dve):
            def wide(v):
                return v.unsqueeze(2).broadcast_to([P, NT, NE])
            dve.wait_ge(scored, 1)
            dve.tensor_reduce(peak[:], logits[:], AX_X, ALU.max).then_inc(step, 1)
            dve.wait_ge(step, 1)
            dve.tensor_tensor(prob[:], logits[:], wide(peak[:]), ALU.subtract).then_inc(step, 1)
            dve.wait_ge(exped, 1)
            dve.tensor_reduce(peak[:], prob[:], AX_X, ALU.add).then_inc(step, 1)
            dve.wait_ge(step, 3)
            dve.reciprocal(peak[:], peak[:]).then_inc(step, 1)
            dve.wait_ge(step, 4)
            dve.tensor_tensor(prob[:], prob[:], wide(peak[:]), ALU.mult).then_inc(step, 1)
            dve.wait_ge(step, 5)
            dve.tensor_copy(prob_t[:].rearrange("p t b e -> p b t e"), prob[:].rearrange("p (b t) e -> p b t e", b=B))\
               .then_inc(step, 1)
            dve.wait_ge(turned, 1)
            for i in range(2):
                dve.tensor_copy(rows[:, i * BANK:(i + 1) * BANK], rows_ps[i][:])
                last = dve.tensor_copy(left[:, i * BANK:(i + 1) * BANK], rows_ps[i][:])
            last.then_inc(found, 2)
            for it in range(TOPK // 8):
                dve.wait_ge(found, 2 * it + 2)
                dve.max(top[:], left[:]).then_inc(found, 1)
                dve.wait_ge(found, 2 * it + 3)
                dve.match_replace(out=left[:], in_to_replace=top[:], in_values=left[:], imm_value=-1.0).then_inc(found, 1)
            dve.wait_ge(found, 2 * (TOPK // 8) + 2)
            dve.scalar_tensor_tensor(out=rows[:], in0=left[:], scalar=0.0, in1=rows[:], op0=ALU.is_lt,
                                     op1=ALU.mult).then_inc(back, 1)
            dve.wait_ge(turned, 2)
            dve.tensor_copy(weight[:], weight_ps[:])


def block0(core, c, top, ins):
    norm_modulate(core, c, 0, SA, CA)
    with core.scope() as s:
        Qp = s.sbuf("Qp", [P, H, S], F16)
        Kp = s.sbuf("Kp", [P, H, S], F16)
        V = s.sbuf("V", [P, TPB, H * HD0], F32)
        wqkv = s.sbuf("wqkv", [P, 3 * H * HD0], F32)
        wo = s.sbuf("wo", [P, H * HD0 // P, D], F32)
        rope = s.sbuf("rope", [P, TPB, 4, HD0], F32)
        with core.scope() as ld:
            loaded = ld.sem("loaded")
            block = ld.block()

            @block.sync
            def _(sp):
                sp.dma_start(wqkv[:], ins["L0_attn_wqkv"]).then_inc(loaded, 16)
                sp.dma_start(rope[:].rearrange("p t j d -> p t (j d)"), ins["rope"].rearrange("(t p) j d -> p t (j d)", p=P)).then_inc(loaded, 16)
                sp.dma_start(wo[:], ins["L0_attn_wo"].rearrange("(u p) d -> p u d", p=P)).then_inc(loaded, 16)
                sp.wait_ge(loaded, 48)
        ctxT = Qp[:].bitcast(F32).rearrange("p (u two) s -> p u (two s)", two=2)
        for b in range(B):
            project_rope(core, c, b, wqkv, rope, Qp, Kp, V)
            attend(core, c, 2, Qp, Kp, V, ctxT, 2, 2)
            project_out(core, c, b, 0, H // 2, ctxT, wo)
    norm_modulate(core, c, 0, SB, CB)
    with core.scope() as s:
        pick = s.sbuf("pick", [P, NT, 1 + NE], F32)
        acc = s.sbuf("acc", [P, NT, D], F32)
        clear(core, [acc[:]])
        route_top1(core, c, ins["L0_ffn_Wg"], pick)
        experts(core, c, lambda e: ins["L0_ffn_w1s"], lambda e: ins["L0_ffn_w2s"],
                lambda e: ins["L0_ffn_w3s"].rearrange("(f p) d -> p f d", p=P), 1, lambda t, e: pick[:, t, 0:1], acc)
        experts(core, c, lambda e: ins["L0_ffn_W1"][e], lambda e: ins["L0_ffn_W2"][e],
                lambda e: ins["L0_ffn_W3"][e].rearrange("(f p) d -> p f d", p=P), NE,
                lambda t, e: pick[:, t, bass.ds(e + 1, 1)], acc)
        add_gated(core, c, 0, acc, None)


def block1(core, c, top, ins, out):
    norm_modulate(core, c, 1, SA, CA)
    with core.scope() as s:
        Qp = s.sbuf("Qp", [P, H, S], F16)
        Kp = s.sbuf("Kp", [P, 4, S], F16)
        V = s.sbuf("V", [P, TPB, H * 32], F32)
        ctxT = s.sbuf("ctxT", [P, 4, S], F32)
        wqkv = s.sbuf("wqkv", [P, 3, D], F32)
        wo = s.sbuf("wo", [P, 4, D], F32)
        lora_weights(core, ins, wqkv, wo)
        clear(core, [Qp[:].bitcast(F32), V[:]])
        for b in range(B):
            project_narrow(core, c, b, wqkv, Qp, Kp, V)
            attend(core, c, 4, Qp, Kp, V, ctxT, 1, 1)
            project_out(core, c, b, 1, 4, ctxT, wo)
    norm_modulate(core, c, 1, SB, CB)
    with core.scope() as s:
        weight = s.sbuf("weight", [P, TPB, B, NE], F32)
        acc = s.sbuf("acc", [P, NT, D], F32)
        clear(core, [acc[:]])
        route_experts_choice(core, c, ins["gate_wT"], weight)
        experts(core, c, lambda e: ins["L1_ffn_w1"][e], None,
                lambda e: ins["L1_ffn_w2"][e].rearrange("(f p) d -> p f d", p=P), NE,
                lambda t, e: weight[:, t % TPB, t // TPB, bass.ds(e, 1)], acc)
        add_gated(core, c, 1, acc, out)


def build(nc, ins, out):
    core = Core(nc)
    with core.scope() as top:
        c = load_constants(core, top, ins)
        modulation(core, c, 0, ins["L0_cT"], ins["L0_wmod"])
        modulation(core, c, 1, ins["L1_cT"], ins["L1_wmod"])
        block0(core, c, top, ins)
        block1(core, c, top, ins, out)


def rope_tables():
    half = HD0 // 2
    fraction = (np.float32(2.0) * np.arange(half, dtype=np.float32) / np.float32(HD0)).astype(np.float32)
    timescale = np.power(np.float32(10000.0), fraction).astype(np.float32)
    angle = np.arange(S, dtype=np.float32)[:, None] / timescale
    cos, sin = np.cos(angle), np.sin(angle)
    k = [np.concatenate([cos, cos], 1), np.concatenate([sin, -sin], 1)]
    q = [t * np.float32(HD0 ** -0.5) for t in k]
    return np.stack(q + k, 1).astype(np.float32)


def layout(inputs):
    a = {n: np.asarray(v) for n, v in inputs.items()}
    keep = ["L0_attn_x", "L0_attn_wqkv", "L0_attn_wo", "L0_ffn_w1s", "L0_ffn_w2s", "L0_ffn_w3s", "L0_ffn_W1",
            "L0_ffn_W2", "L0_ffn_W3", "L0_ffn_Wg", "L0_wmod", "L1_wmod", "L1_ffn_w1", "L1_ffn_w2"]
    arrays = {n: a[n] for n in keep}
    arrays["L0_cT"], arrays["L1_cT"] = a["L0_c"].T, a["L1_c"].T
    arrays["gate_wT"] = a["L1_ffn_gate_w"].T
    arrays["rope"] = rope_tables()
    arrays["lora_w_qkv"] = np.stack([a["L1_attn_w" + n].T for n in "qkv"], 1)
    arrays["lora_a_qkv"] = np.stack([a["L1_attn_a" + n] for n in "qkv"], 1)
    arrays["lora_b_qkv"] = np.stack([a["L1_attn_b" + n].T for n in "qkv"], 1)

    def pad(v):
        v = v.reshape(v.shape[0], 4, 4, HD1)
        return np.pad(v, ((0, 0), (0, 0), (0, 0), (0, 32 - HD1))).reshape(v.shape[0], 4, P)
    arrays["lora_w_o"] = pad(a["L1_attn_wo"]).transpose(2, 1, 0)
    arrays["lora_a_o"] = pad(a["L1_attn_ao"])
    arrays["lora_b_o"] = a["L1_attn_bo"].T
    return {n: np.ascontiguousarray(v) for n, v in arrays.items()}


def kernel(**inputs):
    import concourse.bacc as bacc
    from concourse.bass_utils import run_bass_kernel_spmd

    nc = bacc.Bacc("TRN2", target_bir_lowering=False, num_devices=1)
    arrays = layout(inputs)
    ins = {n: nc.dram_tensor(n, v.shape, mybir.dt.from_np(v.dtype), kind="ExternalInput").ap()
           for n, v in arrays.items()}
    out = nc.dram_tensor("out", (B, S, D), F32, kind="ExternalOutput").ap()
    build(nc, ins, out)
    return run_bass_kernel_spmd(nc, [arrays], core_ids=[0]).results[0]["out"]
```

```python
from contextlib import ExitStack

import numpy as np

import concourse.bass as bass
from concourse import mybir

ALU = mybir.AluOpType
ACT = mybir.ActivationFunctionType
F32 = mybir.dt.float32
F16 = mybir.dt.float16
BF16 = mybir.dt.bfloat16
AX_X = mybir.AxisListType.X

P = 128
B, S, D = 2, 1024, 128
TPB = S // P
NT = B * TPB
H = 16
HD0, HD1 = 64, 8
FF = 512
FC = FF // P
NE = 8
TOPK = 2 * S // NE
BANK = 512
EPS = 1e-5
MASKED = -1e30
SA, CA, GA, SB, CB, GB = range(6)
ORDER = [0, 2, 4, 6, 7, 5, 3, 1]


class Core:

    def __init__(self, nc):
        self.nc = nc
        self.n = 0

    def scope(self):
        return Scope(self)


class Scope(ExitStack):

    def __init__(self, core):
        super().__init__()
        self.core = core

    def _name(self, name):
        self.core.n += 1
        return f"{name}_{self.core.n}"

    def sbuf(self, name, shape, dt):
        return self.enter_context(self.core.nc.sbuf_tensor(self._name(name), shape, dt))

    def psum(self, name, shape, dt=F32):
        return self.enter_context(self.core.nc.psum_tensor(self._name(name), shape, dt))

    def sem(self, name):
        handle = self.enter_context(self.core.nc.semaphore(self._name(name)))
        self.callback(lambda: self.core.nc.gpsimd.sem_clear(handle))
        return handle

    def gpsimd_dma_sem(self, name):
        return self.core.nc.alloc_semaphore(self._name(name))

    def block(self):
        return self.enter_context(self.core.nc.Block())


class Consts:
    pass


def load_constants(core, top, ins):
    c = Consts()
    c.x = top.sbuf("x", [P, NT, D], F32)
    c.identf = top.sbuf("identf", [P, P], F32)
    c.identh = top.sbuf("identh", [P, P], F16)
    c.identb = top.sbuf("identb", [P, P], BF16)
    c.causal = top.sbuf("causal", [P, P], BF16)
    c.hT = top.sbuf("hT", [P, NT * P], F32)
    c.mod = [top.sbuf(f"mod{layer}", [P, 6, B], F32) for layer in range(2)]
    c.gate_b = [top.sbuf(f"gate_b{layer}", [P, B, D], F32) for layer in range(2)]
    with core.scope() as s:
        loaded, made = s.sem("loaded"), s.sem("made")
        block = s.block()

        @block.sync
        def _(sp):
            sp.dma_start(c.x[:], ins["L0_attn_x"].rearrange("b (t p) d -> p (b t) d", p=P)).then_inc(loaded, 16)
            sp.wait_ge(loaded, 16)

        @block.gpsimd
        def _(pool):
            pool.memset(c.identf[:], 0.0).then_inc(made, 1)
            pool.memset(c.causal[:], 0.0).then_inc(made, 1)
            pool.wait_ge(made, 2)
            pool.affine_select(out=c.identf[:], in_=c.identf[:], compare_op=ALU.not_equal, fill=1.0, base=0,
                               pattern=[[-1, P]], channel_multiplier=1).then_inc(made, 1)
            pool.affine_select(out=c.causal[:], in_=c.causal[:], compare_op=ALU.is_ge, fill=MASKED, base=0,
                               pattern=[[-1, P]], channel_multiplier=1).then_inc(made, 1)
            pool.wait_ge(made, 4)
            pool.tensor_copy(c.identh[:], c.identf[:]).then_inc(made, 1)
            pool.tensor_copy(c.identb[:], c.identf[:]).then_inc(made, 1)
    return c


def modulation(core, c, layer, cond, wmod):
    with core.scope() as s:
        ct = s.sbuf("ct", [P, B], F32)
        wm = s.sbuf("wm", [P, 6 * D], F32)
        ex = s.sbuf("ex", [P, B], F32)
        silu = s.sbuf("silu", [P, B], F32)
        silu_b = s.sbuf("silu_b", [P, B, P], F32)
        g = s.sbuf("g", [P, 2, B, P], F32)
        mod_ps = s.psum("mod_ps", [P, 6, B])
        row_ps = s.psum("row_ps", [P, B, D])
        loaded, exped, silu_ready, products, step = (s.sem(n) for n in ("loaded", "exped", "silu", "products", "step"))
        block = s.block()

        @block.sync
        def _(sp):
            sp.dma_start(ct[:], cond).then_inc(loaded, 16)
            sp.dma_start(wm[:], wmod).then_inc(loaded, 16)

        @block.scalar
        def _(act):
            act.wait_ge(loaded, 32)
            act.activation(ex[:], ct[:], ACT.Exp, scale=-1.0).then_inc(exped, 1)

        @block.tensor
        def _(pe):
            pe.wait_ge(silu_ready, 2)
            for j in range(6):
                pe.matmul(mod_ps[:, j, :], wm[:, j * D:(j + 1) * D], silu[:], start=True, stop=True)
            for b in range(B):
                last = pe.matmul(row_ps[:, b, :], silu_b[:, b, :], wm[:, GB * D:(GB + 1) * D], start=True, stop=True)
            last.then_inc(products, 1)

        @block.vector
        def _(dve):
            dve.wait_ge(exped, 1)
            dve.tensor_scalar(ex[:], ex[:], 1.0, None, ALU.add).then_inc(step, 1)
            dve.wait_ge(step, 1)
            dve.reciprocal(ex[:], ex[:]).then_inc(step, 1)
            dve.wait_ge(step, 2)
            dve.tensor_tensor(silu[:], ex[:], ct[:], ALU.mult).then_inc(silu_ready, 1)
            dve.wait_ge(silu_ready, 1)
            dve.tensor_copy(silu_b[:], silu[:].unsqueeze(2).broadcast_to([P, B, P])).then_inc(silu_ready, 1)
            dve.wait_ge(products, 1)
            mod = c.mod[layer]
            dve.tensor_copy(mod[:], mod_ps[:]).then_inc(step, 1)
            dve.tensor_copy(c.gate_b[layer][:], row_ps[:]).then_inc(step, 1)
            dve.wait_ge(step, 4)
            n = 4
            for j in (CA, CB):
                dve.tensor_scalar(mod[:, j, :], mod[:, j, :], 1.0, None, ALU.add).then_inc(step, 1)
                n += 1
            for gate, sgn, mag in ((mod[:, GA, :], g[:, 0, :, 0], g[:, 1, :, 0]), (c.gate_b[layer][:], g[:, 0], g[:, 1])):
                dve.wait_ge(step, n)
                dve.tensor_scalar(sgn, gate, 0.0, 2.0, ALU.is_ge, ALU.mult).then_inc(step, 1)
                dve.tensor_scalar(mag, gate, -1.0, None, ALU.mult).then_inc(step, 1)
                dve.wait_ge(step, n + 2)
                dve.tensor_tensor(mag, mag, gate, ALU.max).then_inc(step, 1)
                dve.tensor_scalar(sgn, sgn, -1.0, None, ALU.add).then_inc(step, 1)
                dve.wait_ge(step, n + 4)
                dve.tensor_scalar(mag, mag, 0.25, None, ALU.max).then_inc(step, 1)
                dve.wait_ge(step, n + 5)
                dve.tensor_tensor(gate, mag, sgn, ALU.mult).then_inc(step, 1)
                n += 6


def norm_modulate(core, c, layer, shift, scale):
    mod = c.mod[layer]
    with core.scope() as s:
        xc = s.sbuf("xc", [P, NT, D], F32)
        sq = s.sbuf("sq", [P, NT, D], F32)
        mean = s.sbuf("mean", [P, NT], F32)
        var = s.sbuf("var", [P, NT], F32)
        xT = [s.psum(f"xT{i}", [P, BANK]) for i in range(4)]
        step, squared, rooted, xhat, turned = (s.sem(n) for n in ("step", "squared", "rooted", "xhat", "turned"))
        block = s.block()
        per_bank = BANK // P

        def bcast(v):
            return v.unsqueeze(2).broadcast_to([P, NT, D])

        @block.vector
        def _(dve):
            dve.tensor_reduce(mean[:], c.x[:], AX_X, ALU.add).then_inc(step, 1)
            dve.wait_ge(step, 1)
            dve.tensor_scalar(mean[:], mean[:], 1.0 / D, None, ALU.mult).then_inc(step, 1)
            dve.wait_ge(step, 2)
            dve.tensor_tensor(xc[:], c.x[:], bcast(mean[:]), ALU.subtract).then_inc(step, 1)
            dve.wait_ge(squared, 1)
            dve.tensor_reduce(var[:], sq[:], AX_X, ALU.add).then_inc(step, 1)
            dve.wait_ge(step, 4)
            dve.tensor_scalar(var[:], var[:], 1.0 / D, EPS, ALU.mult, ALU.add).then_inc(step, 1)
            dve.wait_ge(rooted, 1)
            dve.reciprocal(var[:], var[:]).then_inc(step, 1)
            dve.wait_ge(step, 6)
            for q in range(4):
                part = slice(q * per_bank, (q + 1) * per_bank)
                dve.tensor_tensor(xc[:, part, :], xc[:, part, :],
                                  var[:, part].unsqueeze(2).broadcast_to([P, per_bank, D]), ALU.mult).then_inc(xhat, 1)

        @block.scalar
        def _(act):
            act.wait_ge(step, 3)
            act.activation(sq[:], xc[:], ACT.Square).then_inc(squared, 1)
            act.wait_ge(step, 5)
            act.activation(var[:], var[:], ACT.Sqrt).then_inc(rooted, 1)
            for q in range(4):
                b = q * per_bank // TPB
                act.wait_ge(turned, q + 1)
                act.activation(c.hT[:, q * BANK:(q + 1) * BANK], xT[q][:], ACT.Identity,
                               bias=mod[:, shift, b:b + 1], scale=mod[:, scale, b:b + 1])

        @block.tensor
        def _(pe):
            for q in range(4):
                pe.wait_ge(xhat, q + 1)
                for k in range(per_bank):
                    last = pe.transpose(xT[q][:, k * P:(k + 1) * P], xc[:, q * per_bank + k, :], c.identf[:])
                last.then_inc(turned, 1)


def project_rope(core, c, b, wqkv, rope, Qp, Kp, V):
    CH = 6
    QK = 4
    HPC = BANK // HD0
    RING = QK
    with core.scope() as s:
        h_tile = [s.sbuf(f"h_tile{i}", [P, P], F32) for i in range(2)]
        by_cos = [s.sbuf(f"by_cos{i}", [P, HPC, 2, HD0 // 2], F32) for i in range(RING)]
        by_sin = [s.sbuf(f"by_sin{i}", [P, HPC, 2, HD0 // 2], F32) for i in range(RING)]
        turned = [s.sbuf(f"turned{i}", [P, HPC, 2, HD0 // 2], F32) for i in range(RING)]
        parts = [s.sbuf(f"parts{i}", [P, QK, HPC, 2, HD0], F16) for i in range(2)]
        proj = [s.psum(f"proj{i}", [P, BANK]) for i in range(4)]
        partsT = [s.psum(f"partsT{i}", [P, HPC, P], F16) for i in range(2)]
        (h_ready, projected, rope_read, v_read, roped, hi_done, lo_done, t_done, t_read) = (
            s.sem(n) for n in ("h_ready", "projected", "rope_read", "v_read", "roped", "hi_done", "lo_done",
                               "t_done", "t_read"))
        block = s.block()
        LOOPS = TPB // 2

        @block.tensor
        def _(pe):
            def project(t, a):
                pe.wait_ge(h_ready, t + 1)
                for ch in range(CH):
                    tile, before = divmod(ch - 4, CH)
                    if before < QK:
                        pe.wait_ge(rope_read, (t + tile + 1) * QK + before + 1)
                    else:
                        pe.wait_ge(v_read, (t + tile + 1) * 2 + before - QK + 1)
                    pe.matmul(proj[(a * CH + ch) % 4][:], h_tile[a][:], wqkv[:, ch * BANK:(ch + 1) * BANK],
                              start=True, stop=True).then_inc(projected, 1)

            def turn(t, a):
                for ch in range(QK):
                    pe.wait_ge(lo_done, QK * t + ch + 1 + RING)
                    pe.wait_ge(t_read, QK * t + ch + 1)
                    for h in range(HPC):
                        last = pe.transpose(partsT[ch % 2][:, h, :],
                                            parts[a][:, ch, h].rearrange("p a d -> p (a d)"), c.identh[:])
                    last.then_inc(t_done, 1)

            project(0, 0)
            project(1, 1)
            with pe.Fori(0, LOOPS - 1, 1) as it:
                for a in range(2):
                    turn(2 * it + a, a)
                    project(2 * it + a + 2, a)
            turn(TPB - 2, 0)
            turn(TPB - 1, 1)

        @block.vector
        def _(dve):
            dve.sem_inc(rope_read, QK)
            dve.sem_inc(lo_done, RING)

            def low_part(t, a, ch):
                dve.wait_ge(hi_done, QK * t + ch + 1)
                dve.tensor_tensor(parts[a][:, ch, :, 1, :], turned[ch % RING][:].rearrange("p h a d -> p h (a d)"),
                                  parts[a][:, ch, :, 0, :], ALU.subtract).then_inc(lo_done, 1)

            def rotate(t, a, first=False):
                for ch in range(QK):
                    table = 2 * (ch // 2)
                    dve.wait_ge(projected, CH * t + ch + 1)
                    dve.wait_ge(roped, QK * t + ch + 1)
                    src = proj[(a * CH + ch) % 4][:].rearrange("p (h d) -> p h d", h=HPC)
                    for out, tab in ((by_cos, table), (by_sin, table + 1)):
                        last = dve.tensor_tensor(out[ch % RING][:].rearrange("p h a d -> p h (a d)"), src,
                                                 rope[:, t, tab, :].unsqueeze(1).broadcast_to([P, HPC, HD0]), ALU.mult)
                    last.then_inc(rope_read, 1)
                    if ch:
                        low_part(t, a, ch - 1)
                    elif not first:
                        low_part(t - 1, 1 - a, QK - 1)

            rotate(0, 0, first=True)
            rotate(1, 1)
            with dve.Fori(0, LOOPS - 1, 1) as it:
                for a in range(2):
                    rotate(2 * it + a + 2, a)
            low_part(TPB - 1, 1, QK - 1)

        @block.gpsimd
        def _(pool):
            pool.sem_inc(roped, RING)
            with pool.Fori(0, LOOPS, 1) as it:
                for g in range(2 * QK):
                    pool.wait_ge(rope_read, 2 * QK * it + g + 1 + QK)
                    pool.wait_ge(lo_done, 2 * QK * it + g + 1)
                    for half in range(2):
                        last = pool.tensor_tensor(turned[g % RING][:, :, half, :], by_cos[g % RING][:, :, half, :],
                                                  by_sin[g % RING][:, :, 1 - half, :], ALU.add)
                    last.then_inc(roped, 1)

        @block.scalar
        def _(act):
            act.sem_inc(v_read, 2)
            act.sem_inc(t_read, 2)

            def h_copy(t, a):
                act.copy(h_tile[a][:], c.hT[:, bass.ds(t * P + b * S, P)]).then_inc(h_ready, 1)

            def high_part(t, a, ch):
                act.wait_ge(roped, QK * t + ch + 1 + RING)
                act.copy(parts[a][:, ch, :, 0, :],
                         turned[ch % RING][:].rearrange("p h a d -> p h (a d)")).then_inc(hi_done, 1)

            def evacuate(t, ch):
                act.wait_ge(t_done, QK * t + ch + 1)
                dst = Qp if ch < 2 else Kp
                act.copy(dst[:, (ch % 2) * HPC:(ch % 2 + 1) * HPC, bass.ds(t * P, P)], partsT[ch % 2][:])\
                   .then_inc(t_read, 1)

            def tile(t, a, first=False, last=False):
                for half in range(2):
                    act.wait_ge(projected, CH * t + QK + half + 1)
                    act.copy(V[:, t, half * BANK:(half + 1) * BANK], proj[(a * CH + QK + half) % 4][:])\
                       .then_inc(v_read, 1)
                for ch in range(QK):
                    high_part(t, a, ch)
                    if not first:
                        evacuate(t - 1, ch)
                if not last:
                    h_copy(t + 2, a)

            h_copy(0, 0)
            h_copy(1, 1)
            tile(0, 0, first=True)
            tile(1, 1)
            with act.Fori(0, LOOPS - 2, 1) as it:
                for a in range(2):
                    tile(2 * it + a + 2, a)
            tile(TPB - 2, 0, last=True)
            tile(TPB - 1, 1, last=True)
            for ch in range(QK):
                evacuate(TPB - 1, ch)


def attend(core, c, U, Qp, Kp, V, ctxT, q_orders, k_heads):
    HW = P // U
    LOOPS = H // U // 2
    TILES = 2 * TPB
    tiles = [(a, i) for a in range(2) for i in ORDER]
    items = [(p, h) for p in range(TILES) for h in range(U)]
    N = len(items)
    width = [(i + 1) * P for _, i in tiles]
    chunks = [-(-w // BANK) for w in width]
    first_chunk, n_chunks = [], 0
    for p, h in items:
        first_chunk.append(n_chunks)
        n_chunks += chunks[p]
    through = [U * sum(chunks[:p + 1]) // 2 for p in range(TILES)]
    INVERT, CONTEXT, COPY, NORMALISE = 1, 2, U + 2, U + 3
    with core.scope() as s:
        Qs = [s.sbuf(f"Qs{i}", [P, q_orders, U, S], F16) for i in range(2)]
        Ks = [s.sbuf(f"Ks{i}", [P, k_heads, S], F16) for i in range(2)]
        Vs = [s.sbuf(f"Vs{i}", [P, TPB, U, HW], F32) for i in range(2)]
        prob = [s.sbuf(f"prob{i}", [P, S], F32) for i in range(2)]
        probT = [s.sbuf(f"probT{i}", [P, U, S], F32) for i in range(2)]
        negmax = s.sbuf("negmax", [P, 4], F32)
        total = s.sbuf("total", [P, 4, U], F32)
        inv = s.sbuf("inv", [P, 2, U], F32)
        inv_b = [s.sbuf(f"inv_b{i}", [P, U, HW], F32) for i in range(2)]
        inv_row = [s.sbuf(f"inv_row{i}", [P, P], F32) for i in range(2)]
        score = [s.psum(f"score{i}", [P, S]) for i in range(2)]
        probT_ps = [s.psum(f"probT_ps{i}", [P, BANK]) for i in range(2)]
        ctx_ps = [s.psum(f"ctx_ps{i}", [P, 4, P]) for i in range(2)]
        staged = [s.sem(f"staged{i}") for i in range(2)]
        (scored, maxed, exped, t_done, inv_made, inv_ready, inv_copied, pv_done, ctx_done) = (
            s.sem(n) for n in ("scored", "maxed", "exped", "t_done", "inv_made", "inv_ready", "inv_copied",
                               "pv_done", "ctx_done"))
        evac = [s.sem(f"evac{i}") for i in range(2)]
        block = s.block()
        DMAS = (1 if q_orders == 1 else 3) + 2

        def steps(n, item_tasks, tile_tasks):
            for lag, task in item_tasks:
                if 0 <= n - lag < N:
                    task(n - lag)
            for lag, task in tile_tasks:
                p, rest = divmod(n - lag + 1, U)
                if rest == 0 and 1 <= p <= TILES:
                    task(p - 1)
                elif task.__name__ == "context" and 1 <= p <= TILES:
                    task(p - 1, rest)

        @block.sync
        def _(sp):
            def load(u, a):
                heads = bass.ds(u * U, U)
                sp.dma_start(Qs[a][:, 0], Qp[:, heads, :]).then_inc(staged[a], 16)
                if q_orders == 2:
                    sp.dma_start(Qs[a][0:HD0, 1], Qp[HD0:P, heads, :]).then_inc(staged[a], 16)
                    sp.dma_start(Qs[a][HD0:P, 1], Qp[0:HD0, heads, :]).then_inc(staged[a], 16)
                sp.dma_start(Ks[a][:], Kp[:, bass.ds(u * k_heads, k_heads), :]).then_inc(staged[a], 16)
                sp.dma_start(Vs[a][:].rearrange("p t h d -> p t (h d)"), V[:, :, bass.ds(u * P, P)]).then_inc(staged[a], 16)
            load(0, 0)
            load(1, 1)
            with sp.Fori(0, LOOPS - 1, 1) as it:
                for a in range(2):
                    sp.wait_ge(ctx_done, (2 * it + a + 1) * TPB + 2)
                    load(2 * it + a + 2, a)

        @block.tensor
        def _(pe):
            with pe.Fori(0, LOOPS, 1) as it:
                def scores(n):
                    p, h = items[n]
                    a, i = tiles[p]
                    if n % (N // 2) == 0:
                        pe.wait_ge(staged[a], (it + 1) * (16 * DMAS))
                    pe.wait_ge(exped, it * N + n + 1)
                    out = score[n % 2]
                    for order in range(q_orders):
                        for k0 in range(0, width[p], BANK):
                            k1 = min(k0 + BANK, width[p])
                            pe.matmul(out[:, k0:k1], Qs[a][:, order, h, i * P:(i + 1) * P],
                                      Ks[a][:, h if k_heads > 1 else 0, k0:k1], start=(order == 0),
                                      stop=(order == q_orders - 1 and k1 < width[p]))
                    pe.matmul(out[:, i * P:width[p]], c.identb[:], c.causal[:], start=False,
                              stop=True).then_inc(scored, 1)

                def turn(n):
                    p, h = items[n]
                    pe.wait_ge(exped, it * N + n + 1 + 2)
                    for k in range(chunks[p]):
                        m = first_chunk[n] + k
                        pe.wait_ge(evac[m % 2], it * (n_chunks // 2) + m // 2 + 1)
                        for j in range(4 * k, min(4 * k + 4, tiles[p][1] + 1)):
                            last = pe.transpose(probT_ps[m % 2][:, (j % 4) * P:(j % 4 + 1) * P],
                                                prob[n % 2][:, j * P:(j + 1) * P], c.identf[:])
                        last.then_inc(t_done, 1)

                def context(p, slice_no=0):
                    a, i = tiles[p]
                    if slice_no == 0:
                        pe.wait_ge(ctx_done, it * TILES + p + 1)
                        pe.wait_ge(inv_ready, it * TILES + p + 1)
                        pe.matmul(ctx_ps[p % 2][:, 1, :], inv_b[p % 2][:].rearrange("p h d -> p (h d)"), c.identf[:],
                                  start=True, stop=True)
                        for e in range(2):
                            pe.wait_ge(evac[e], it * (n_chunks // 2) + through[p] + 1)
                    for j in range((i + 1) * slice_no // U, (i + 1) * (slice_no + 1) // U):
                        for h in range(U):
                            last = pe.matmul(ctx_ps[p % 2][h * HW:(h + 1) * HW, 0, :], Vs[a][:, j, h, :],
                                             probT[p % 2][:, h, j * P:(j + 1) * P], start=(j == 0), stop=(j == i))
                    if slice_no == U - 1:
                        last.then_inc(pv_done, 1)

                for n in range(-1, N + CONTEXT + U):
                    steps(n, ((-1, scores), (1, turn)), ((CONTEXT, context),))

        def evacuate(eng, copy, it, n, e):
            p, h = items[n]
            for k in range(chunks[p]):
                m = first_chunk[n] + k
                if m % 2 == e:
                    eng.wait_ge(t_done, it * n_chunks + m + 1 + 4)
                    eng.wait_ge(pv_done, it * TILES + p + 1)
                    w = min(BANK, width[p] - k * BANK)
                    copy(probT[p % 2][:, h, k * BANK:k * BANK + w], probT_ps[e][:, 0:w]).then_inc(evac[e], 1)

        @block.vector
        def _(dve):
            dve.sem_inc(evac[0], 1)
            dve.sem_inc(ctx_done, 2)
            dve.sem_inc(pv_done, 2)
            with dve.Fori(0, LOOPS, 1) as it:
                def row_max(n):
                    p, h = items[n]
                    dve.wait_ge(scored, it * N + n + 1)
                    dve.tensor_reduce(negmax[:, n % 4:n % 4 + 1], score[n % 2][:, 0:width[p]], AX_X, ALU.max,
                                      negate=True).then_inc(maxed, 1)

                def invert(p):
                    dve.wait_ge(exped, it * N + (p + 1) * U + 2)
                    dve.wait_ge(pv_done, it * TILES + p + 1)
                    dve.reciprocal(inv[:, p % 2, :], total[:, p % 4, :]).then_inc(inv_made, 1)
                    dve.wait_ge(inv_made, it * TILES + p + 1)
                    dve.tensor_copy(inv_b[p % 2][:], inv[:, p % 2, :].unsqueeze(2).broadcast_to([P, U, HW]))\
                       .then_inc(inv_ready, 1)

                def normalise(p):
                    a, i = tiles[p]
                    dve.wait_ge(inv_copied, it * TILES + p + 1 + 2)
                    dve.tensor_tensor(ctxT[:, 2 * it + a, i * P:(i + 1) * P], ctx_ps[p % 2][:, 0, :],
                                      inv_row[p % 2][:], ALU.mult).then_inc(ctx_done, 1)

                for n in range(-1, N + NORMALISE + 1):
                    steps(n, ((-1, row_max), (1, lambda n: evacuate(dve, dve.tensor_copy, it, n, 0))),
                          ((INVERT, invert), (NORMALISE, normalise)))

        @block.scalar
        def _(act):
            act.sem_inc(exped, 2)
            act.sem_inc(evac[1], 1)
            act.sem_inc(t_done, 4)
            act.sem_inc(inv_copied, 2)
            with act.Fori(0, LOOPS, 1) as it:
                def exponentials(n):
                    p, h = items[n]
                    act.wait_ge(maxed, it * N + n + 1)
                    before = first_chunk[n - 1] if n else n_chunks - chunks[-1]
                    act.wait_ge(t_done, (it * n_chunks + before + 4) if n else (it * n_chunks + 4 - chunks[-1]))
                    act.activation(prob[n % 2][:, 0:width[p]], score[n % 2][:, 0:width[p]], ACT.Exp,
                                   bias=negmax[:, n % 4:n % 4 + 1], accum_out=total[:, p % 4, h:h + 1])\
                       .then_inc(exped, 1)

                def copy_row(p):
                    act.wait_ge(pv_done, it * TILES + p + 1 + 2)
                    act.wait_ge(ctx_done, it * TILES + p + 1)
                    act.copy(inv_row[p % 2][:], ctx_ps[p % 2][:, 1, :]).then_inc(inv_copied, 1)

                for n in range(N + COPY + 1):
                    steps(n, ((0, exponentials), (1, lambda n: evacuate(act, act.copy, it, n, 1))),
                          ((COPY, copy_row),))


def project_out(core, c, b, layer, units, ctxT, wo):
    HALF = S // BANK
    with core.scope() as s:
        y = [s.sbuf(f"y{i}", [P, BANK], F32) for i in range(HALF)]
        y_ps = [s.psum(f"y_ps{i}", [P, BANK]) for i in range(HALF)]
        yT = [s.psum(f"yT{i}", [P, BANK]) for i in range(HALF)]
        summed, gated, turned = (s.sem(n) for n in ("summed", "gated", "turned"))
        block = s.block()

        @block.tensor
        def _(pe):
            for half in range(HALF):
                for u in range(units):
                    last = pe.matmul(y_ps[half][:], wo[:, u, :], ctxT[:, u, half * BANK:(half + 1) * BANK],
                                     start=(u == 0), stop=(u == units - 1))
                last.then_inc(summed, 1)
            for half in range(HALF):
                pe.wait_ge(gated, half + 1)
                for k in range(BANK // P):
                    last = pe.transpose(yT[half][:, k * P:(k + 1) * P], y[half][:, k * P:(k + 1) * P], c.identf[:])
                last.then_inc(turned, 1)

        @block.scalar
        def _(act):
            for half in range(HALF):
                act.wait_ge(summed, half + 1)
                act.activation(y[half][:], y_ps[half][:], ACT.Copy, scale=c.mod[layer][:, GA, b:b + 1])\
                   .then_inc(gated, 1)

        @block.vector
        def _(dve):
            for half in range(HALF):
                dve.wait_ge(turned, half + 1)
                t0 = b * TPB + half * (BANK // P)
                xs = c.x[:, t0:t0 + BANK // P, :].rearrange("p t d -> p (t d)")
                dve.tensor_tensor(xs, yT[half][:], xs, ALU.add)


SLOT_TILES = NT + NE


class Routing:

    def __init__(self, core, s):
        self.slot = s.sbuf("slot", [P, NT], mybir.dt.uint32)
        self.expert = s.sbuf("expert", [P, SLOT_TILES], mybir.dt.int32)
        self.h = s.sbuf("h", [P, NT, D], F32)
        nc = core.nc
        self.x_sorted = nc.dram_tensor("x_sorted", [SLOT_TILES * P, D], F32).ap()
        self.y_sorted = nc.dram_tensor("y_sorted", [SLOT_TILES * P, D], F32).ap()


def route_top1(core, c, wg_in, r, zeros):
    with core.scope() as s:
        wg = s.sbuf("wg", [P, NE], F32)
        best = s.sbuf("best", [P, NT], F32)
        place = s.sbuf("place", [P, NE], F32)
        steps_k = s.sbuf("steps_k", [P, NT], F32)
        tile_no = s.sbuf("tile_no", [P, SLOT_TILES], F32)
        ones = s.sbuf("ones", [P, P], F32)
        before = s.sbuf("before", [P, P], F32)
        hit = s.sbuf("hit", [P, NT, NE], F32)
        mask = s.sbuf("mask", [P, NE, NT], F32)
        same = s.sbuf("same", [P, NE, NT], F32)
        upto = s.sbuf("upto", [P, NE, NT], F32)
        earlier = s.sbuf("earlier", [P, NE, NT], F32)
        tiles = s.sbuf("tiles", [P, NE], F32)
        end = s.sbuf("end", [P, NE], F32)
        start = s.sbuf("start", [P, NE], F32)
        past = s.sbuf("past", [P, SLOT_TILES, NE], F32)
        owner = s.sbuf("owner", [P, SLOT_TILES], F32)
        slot_f = s.sbuf("slot_f", [P, NT], F32)
        logits = s.psum("logits", [P, NT * 4, NE])
        rank = s.psum("rank", [P, BANK])
        count = s.psum("count", [P, BANK])
        hx = [s.psum(f"hx{i}", [P, BANK]) for i in range(4)]
        loaded, placed, zeroed, scored, step, ranked, turned = (
            s.sem(n) for n in ("loaded", "placed", "zeroed", "scored", "step", "ranked", "turned"))
        block = s.block()

        @block.sync
        def _(sp):
            sp.dma_start(wg[:], wg_in).then_inc(loaded, 16)
            for t0 in range(0, SLOT_TILES, NE):
                sp.dma_start(r.x_sorted[t0 * P:(t0 + NE) * P, :].rearrange("(t p) d -> p t d", p=P),
                             zeros[:, 0:NE, :]).then_inc(zeroed, 16)
            sp.wait_ge(zeroed, 16 * (SLOT_TILES // NE))

        @block.gpsimd
        def _(pool):
            pool.iota(place[:], pattern=[[-1, NE]], base=NE, channel_multiplier=0,
                      allow_small_or_imprecise_dtypes=True)
            pool.iota(steps_k[:], pattern=[[P, NT]], base=0, channel_multiplier=0,
                      allow_small_or_imprecise_dtypes=True)
            pool.iota(tile_no[:], pattern=[[1, SLOT_TILES]], base=0, channel_multiplier=0,
                      allow_small_or_imprecise_dtypes=True)
            pool.memset(ones[:], 1.0).then_inc(placed, 1)
            pool.wait_ge(placed, 1)
            pool.affine_select(out=before[:], in_=ones[:], compare_op=ALU.is_gt, fill=0.0, base=0,
                               pattern=[[1, P]], channel_multiplier=-1).then_inc(placed, 1)

        @block.tensor
        def _(pe):
            pe.wait_ge(loaded, 16)
            for t in range(NT):
                last = pe.matmul(logits[:, t, :], c.hT[:, t * P:(t + 1) * P], wg[:], start=True, stop=True)
            last.then_inc(scored, 1)
            for t in range(NT):
                last = pe.transpose(hx[t // 4][:, (t % 4) * P:(t % 4 + 1) * P], c.hT[:, t * P:(t + 1) * P], c.identf[:])
            last.then_inc(turned, 1)
            pe.wait_ge(placed, 2)
            pe.wait_ge(ranked, 1)
            pe.matmul(rank[:, 0:NE * NT], before[:], mask[:].rearrange("p e t -> p (e t)"), start=True, stop=False)
            pe.matmul(rank[:, 0:NE * NT], ones[:], earlier[:].rearrange("p e t -> p (e t)"), start=False, stop=True)
            pe.matmul(count[:, 0:NE], ones[:], upto[:, :, NT - 1], start=True, stop=True).then_inc(ranked, 1)

        @block.scalar
        def _(act):
            act.wait_ge(turned, 1)
            for q in range(4):
                act.copy(r.h[:, 4 * q:4 * q + 4, :].rearrange("p t d -> p (t d)"), hx[q][:])

        @block.vector
        def _(dve):
            count_steps = [0]

            def link(instruction):
                count_steps[0] += 1
                instruction.then_inc(step, 1)
                dve.wait_ge(step, count_steps[0])

            def wide(v):
                return v.unsqueeze(2).broadcast_to([P, NT, NE])
            lg = logits[:, 0:NT, :]
            dve.memset(same[:], 1.0)
            dve.wait_ge(scored, 1)
            link(dve.tensor_reduce(best[:], lg, AX_X, ALU.max))
            dve.memset(same[:, :, 0:1], 0.0)
            link(dve.tensor_tensor(hit[:], lg, wide(best[:]), ALU.is_ge))
            dve.wait_ge(placed, 1)
            link(dve.tensor_tensor(hit[:], hit[:], place[:].unsqueeze(1).broadcast_to([P, NT, NE]), ALU.mult))
            link(dve.tensor_reduce(best[:], hit[:], AX_X, ALU.max))
            link(dve.tensor_tensor(mask[:].rearrange("p e t -> p t e"), hit[:], wide(best[:]), ALU.is_equal))
            flat = [v[:].rearrange("p e t -> p (e t)") for v in (same, mask, upto, earlier)]
            link(dve.tensor_tensor_scan(flat[2], flat[0], flat[1], 0.0, ALU.mult, ALU.add))
            dve.tensor_tensor(flat[3], flat[2], flat[1], ALU.subtract).then_inc(ranked, 1)
            dve.wait_ge(ranked, 2)
            link(dve.tensor_tensor(upto[:], count[:, 0:NE].unsqueeze(2).broadcast_to([P, NE, NT]),
                                   steps_k[:].unsqueeze(1).broadcast_to([P, NE, NT]), ALU.is_gt))
            link(dve.tensor_reduce(tiles[:], upto[:], AX_X, ALU.add))
            link(dve.tensor_tensor_scan(end[:], ones[:, 0:NE], tiles[:], 0.0, ALU.mult, ALU.add))
            link(dve.tensor_tensor(start[:], end[:], tiles[:], ALU.subtract))
            link(dve.tensor_scalar(start[:], start[:], float(P), None, ALU.mult))
            link(dve.tensor_tensor(upto[:], rank[:, 0:NE * NT].rearrange("p (e t) -> p e t", e=NE),
                                   start[:].unsqueeze(2).broadcast_to([P, NE, NT]), ALU.add))
            link(dve.tensor_tensor(upto[:], upto[:], mask[:], ALU.mult))
            link(dve.tensor_reduce(slot_f[:], upto[:].rearrange("p e t -> p t e"), AX_X, ALU.add))
            dve.tensor_copy(r.slot[:], slot_f[:])
            link(dve.tensor_tensor(past[:], tile_no[:].unsqueeze(2).broadcast_to([P, SLOT_TILES, NE]),
                                   end[:].unsqueeze(1).broadcast_to([P, SLOT_TILES, NE]), ALU.is_ge))
            link(dve.tensor_reduce(owner[:], past[:], AX_X, ALU.add))
            link(dve.tensor_scalar(owner[:], owner[:], float(NE - 1), None, ALU.min))
            dve.tensor_copy(r.expert[:], owner[:])


def scatter_tokens(pool, r, done):
    for t in range(NT):
        pool.indirect_dma_start(out=r.x_sorted, out_offset=bass.IndirectOffsetOnAxis(ap=r.slot[:, t:t + 1], axis=0),
                                in_=r.h[:, t, :], in_offset=None).then_inc(done, 16)
    pool.wait_ge(done, 16 * NT)


def gather_tokens(core, r, acc):
    with core.scope() as s:
        y = s.sbuf("y", [P, NT, D], F32)
        done = [s.gpsimd_dma_sem(f"done{q}") for q in range(4)]
        block = s.block()

        @block.gpsimd
        def _(pool):
            for t in range(NT):
                pool.indirect_dma_start(out=y[:, t, :], out_offset=None, in_=r.y_sorted,
                                        in_offset=bass.IndirectOffsetOnAxis(ap=r.slot[:, t:t + 1], axis=0))\
                    .then_inc(done[t // 4], 16)

        @block.vector
        def _(dve):
            for q in range(4):
                part = slice(4 * q, 4 * q + 4)
                dve.wait_ge(done[q], 16 * 4)
                dve.tensor_tensor(acc[:, part, :], acc[:, part, :], y[:, part, :], ALU.add)


def sorted_experts(core, c, up, up2, down, r):
    AHEAD = 4
    LOOPS = SLOT_TILES // AHEAD
    with core.scope() as s:
        def ring(name, shape, n=2):
            return [s.sbuf(f"{name}{i}", shape, F32) for i in range(n)]
        x_in, w_up, w_up2, w_down = (ring(n, shape, AHEAD) for n, shape in
                                     (("x_in", [P, D]), ("w_up", [P, FF]), ("w_up2", [P, FF]), ("w_down", [P, FC, D])))
        xT, y_out, gelu, hidden = (ring(n, shape) for n, shape in
                                   (("xT", [P, P]), ("y_out", [P, D]), ("gelu", [P, FC, P]), ("hidden", [P, FC, P])))
        xT_ps, u_ps, u2_ps, y_ps = ([s.psum(f"{n}{i}", [P, FC, P]) for i in range(2)]
                                    for n in ("xT_ps", "u_ps", "u2_ps", "y_ps"))
        x_staged, w_staged = ([s.sem(f"{n}{i}") for i in range(AHEAD)] for n in ("x_staged", "w_staged"))
        stored = [s.sem(f"stored{i}") for i in range(2)]
        x_turned, x_ready, upped, gelued, hidden_ready, y_ready, y_copied = (
            s.sem(n) for n in ("x_turned", "x_ready", "upped", "gelued", "hidden_ready", "y_ready", "y_copied"))
        block = s.block()

        def ring_of(it, k):
            return AHEAD * it + k, k % AHEAD, it + k // AHEAD

        @block.sync
        def _(sp):
            def load(it, k):
                t, a, _ = ring_of(it, k)
                sp.dma_start(x_in[a][:], r.x_sorted[bass.ds(t * P, P), :]).then_inc(x_staged[a], 16)
                e = sp.value_load(r.expert[0:1, bass.ds(t, 1)], min_val=0, max_val=NE - 1)
                sp.dma_start(w_up[a][:], up(e)).then_inc(w_staged[a], 16)
                sp.dma_start(w_up2[a][:], up2(e)).then_inc(w_staged[a], 16)
                sp.dma_start(w_down[a][:], down(e)).then_inc(w_staged[a], 16)

            def store(it, k):
                t, a, _ = ring_of(it, k)
                sp.wait_ge(y_copied, t + 1 + 2)
                sp.dma_start(r.y_sorted[bass.ds(t * P, P), :], y_out[a % 2][:]).then_inc(stored[a % 2], 16)

            for k in range(AHEAD):
                load(0, k)
            with sp.Fori(0, LOOPS - 1, 1) as it:
                for k in range(AHEAD):
                    sp.wait_ge(y_ready, AHEAD * it + k + 1)
                    load(it, k + AHEAD)
                    store(it, k)
            for k in range(AHEAD):
                store(LOOPS - 1, k)
            for i in range(2):
                sp.wait_ge(stored[i], 16 + SLOT_TILES // 2 * 16)

        @block.tensor
        def _(pe):
            def turn(it, k):
                t, a, turns = ring_of(it, k)
                pe.wait_ge(x_staged[a], (turns + 1) * 16)
                pe.wait_ge(x_ready, t + 1)
                pe.transpose(xT_ps[a % 2][:, 0, :], x_in[a][:], c.identf[:]).then_inc(x_turned, 1)

            def inner(it, k):
                t, a, turns = ring_of(it, k)
                pe.wait_ge(w_staged[a], (turns + 1) * 48)
                pe.wait_ge(x_ready, t + 1 + 2)
                pe.wait_ge(hidden_ready, t + 1)
                for out, w in ((u_ps, w_up), (u2_ps, w_up2)):
                    for f in range(FC):
                        last = pe.matmul(out[a % 2][:, f, :], w[a][:, f * P:(f + 1) * P], xT[a % 2][:],
                                         start=True, stop=True)
                    last.then_inc(upped, 1)

            def outer(it, k):
                t, a, _ = ring_of(it, k)
                pe.wait_ge(hidden_ready, t + 1 + 2)
                pe.wait_ge(y_copied, t + 1)
                for f in range(FC):
                    last = pe.matmul(y_ps[a % 2][:, 0, :], hidden[a % 2][:, f, :], w_down[a][:, f, :],
                                     start=(f == 0), stop=(f == FC - 1))
                last.then_inc(y_ready, 1)

            turn(0, 0)
            inner(0, 0)
            turn(0, 1)
            with pe.Fori(0, LOOPS - 1, 1) as it:
                for k in range(AHEAD):
                    inner(it, k + 1)
                    turn(it, k + 2)
                    outer(it, k)
            for k in range(AHEAD):
                if k + 1 < AHEAD:
                    inner(LOOPS - 1, k + 1)
                if k + 2 < AHEAD:
                    turn(LOOPS - 1, k + 2)
                outer(LOOPS - 1, k)

        @block.scalar
        def _(act):
            with act.Fori(0, LOOPS, 1) as it:
                for k in range(AHEAD):
                    t, a, _ = ring_of(it, k)
                    act.wait_ge(upped, 2 * t + 1)
                    act.wait_ge(hidden_ready, t + 1)
                    act.activation(gelu[a % 2][:], u_ps[a % 2][:], ACT.Gelu).then_inc(gelued, 1)

        @block.vector
        def _(dve):
            dve.sem_inc(x_ready, 2)
            dve.sem_inc(hidden_ready, 2)
            dve.sem_inc(y_copied, 2)
            for i in range(2):
                dve.sem_inc(stored[i], 16)

            def x_copy(it, k):
                t, a, _ = ring_of(it, k)
                dve.wait_ge(x_turned, t + 1)
                dve.tensor_copy(xT[a % 2][:], xT_ps[a % 2][:, 0, :]).then_inc(x_ready, 1)

            def hide(it, k):
                t, a, _ = ring_of(it, k)
                dve.wait_ge(gelued, t + 1)
                dve.wait_ge(upped, 2 * t + 2)
                dve.tensor_tensor(hidden[a % 2][:], u2_ps[a % 2][:], gelu[a % 2][:], ALU.mult).then_inc(hidden_ready, 1)

            def y_copy(it, k):
                t, a, _ = ring_of(it, k)
                dve.wait_ge(y_ready, t + 1)
                dve.wait_ge(stored[a % 2], (2 * it + k // 2 + 1) * 16)
                dve.tensor_copy(y_out[a % 2][:], y_ps[a % 2][:, 0, :]).then_inc(y_copied, 1)

            x_copy(0, 0)
            hide(0, 0)
            x_copy(0, 1)
            with dve.Fori(0, LOOPS - 1, 1) as it:
                for k in range(AHEAD):
                    hide(it, k + 1)
                    x_copy(it, k + 2)
                    y_copy(it, k)
            for k in range(AHEAD):
                if k + 1 < AHEAD:
                    hide(LOOPS - 1, k + 1)
                if k + 2 < AHEAD:
                    x_copy(LOOPS - 1, k + 2)
                y_copy(LOOPS - 1, k)


def experts(core, c, up, up2, down, n, weight, acc, meanwhile=None):
    gated = up2 is not None
    CHUNKS = NT * P // BANK
    TPC = BANK // P
    E = min(n, 2)
    LOOPS = n // E
    STEPS = CHUNKS * FC
    DMAS = 3 if gated else 2
    with core.scope() as s:
        w_up = [s.sbuf(f"w_up{i}", [P, FF], F32) for i in range(E)]
        w_up2 = [s.sbuf(f"w_up2{i}", [P, FF], F32) for i in range(E)] if gated else None
        w_down = [s.sbuf(f"w_down{i}", [P, FC, D], F32) for i in range(E)]
        gelu = [s.sbuf(f"gelu{i}", [P, BANK], F32) for i in range(2)] if gated else None
        hidden = [s.sbuf(f"hidden{i}", [P, FC, BANK], F32) for i in range(2)]
        u_ps = [s.psum(f"u_ps{i}", [P, BANK]) for i in range(2)]
        u2_ps = [s.psum(f"u2_ps{i}", [P, BANK]) for i in range(2)] if gated else None
        y_ps = [s.psum(f"y_ps{i}", [P, TPC, D]) for i in range(2)]
        staged = [s.sem(f"staged{i}") for i in range(E)]
        upped, gelued, multiplied, y_ready, y_read = (
            s.sem(n) for n in ("upped", "gelued", "multiplied", "y_ready", "y_read"))
        hidden_ready = multiplied if gated else gelued
        block = s.block()

        if meanwhile is not None:
            sent = s.gpsimd_dma_sem("sent")

            @block.gpsimd
            def _(pool):
                meanwhile(pool, sent)

        def loop(eng):
            return eng.Fori(0, LOOPS, 1) if LOOPS > 1 else Once()

        @block.sync
        def _(sp):
            def load(e, a):
                sp.dma_start(w_up[a][:], up(e)).then_inc(staged[a], 16)
                if gated:
                    sp.dma_start(w_up2[a][:], up2(e)).then_inc(staged[a], 16)
                sp.dma_start(w_down[a][:], down(e)).then_inc(staged[a], 16)
            for a in range(E):
                load(a, a)
            if LOOPS > 1:
                with sp.Fori(0, LOOPS - 1, 1) as it:
                    for a in range(E):
                        sp.wait_ge(y_ready, (E * it + a + 1) * CHUNKS + 2)
                        load(E * it + a + E, a)

        @block.tensor
        def _(pe):
            pe.sem_inc(y_ready, 2)
            with loop(pe) as it:
                for a in range(E):
                    def down_product(ch):
                        g = (E * it + a) * CHUNKS + ch
                        pe.wait_ge(hidden_ready, (g + 1) * FC + 2)
                        pe.wait_ge(y_read, g + 1)
                        for t in range(TPC):
                            for f in range(FC):
                                last = pe.matmul(y_ps[ch % 2][:, t, :], hidden[ch % 2][:, f, t * P:(t + 1) * P],
                                                 w_down[a][:, f, :], start=(f == 0), stop=(f == FC - 1))
                        last.then_inc(y_ready, 1)

                    pe.wait_ge(staged[a], (it + 1) * (16 * DMAS))
                    for ch in range(CHUNKS):
                        rhs = c.hT[:, ch * BANK:(ch + 1) * BANK]
                        for f in range(FC):
                            k = (E * it + a) * STEPS + ch * FC + f
                            pe.wait_ge(gelued, k + 1)
                            pe.matmul(u_ps[f % 2][:], w_up[a][:, f * P:(f + 1) * P], rhs,
                                      start=True, stop=True).then_inc(upped, 1)
                            if gated:
                                pe.wait_ge(multiplied, k + 1)
                                pe.matmul(u2_ps[f % 2][:], w_up2[a][:, f * P:(f + 1) * P], rhs,
                                          start=True, stop=True).then_inc(upped, 1)
                            if f == 1 and ch >= 1:
                                down_product(ch - 1)
                    down_product(CHUNKS - 1)

        @block.scalar
        def _(act):
            act.sem_inc(gelued, 2)
            with loop(act) as it:
                for a in range(E):
                    for ch in range(CHUNKS):
                        for f in range(FC):
                            k = (E * it + a) * STEPS + ch * FC + f
                            if gated:
                                act.wait_ge(upped, 2 * k + 1)
                                act.wait_ge(multiplied, k + 1)
                                act.activation(gelu[f % 2][:], u_ps[f % 2][:], ACT.Gelu).then_inc(gelued, 1)
                            else:
                                act.wait_ge(upped, k + 1)
                                if f == 0:
                                    act.wait_ge(y_ready, (E * it + a) * CHUNKS + ch + 1)
                                act.activation(hidden[ch % 2][:, f, :], u_ps[f % 2][:], ACT.Gelu).then_inc(gelued, 1)

        @block.vector
        def _(dve):
            if gated:
                dve.sem_inc(multiplied, 2)
            dve.sem_inc(y_read, 2)
            with loop(dve) as it:
                for a in range(E):
                    def accumulate(ch):
                        g = (E * it + a) * CHUNKS + ch
                        dve.wait_ge(y_ready, g + 1 + 2)
                        dve.wait_ge(y_read, g + 2)
                        for t in range(TPC):
                            tile = ch * TPC + t
                            last = dve.scalar_tensor_tensor(out=acc[:, tile, :], in0=y_ps[ch % 2][:, t, :],
                                                            scalar=weight(tile, E * it + a), in1=acc[:, tile, :],
                                                            op0=ALU.mult, op1=ALU.add)
                        last.then_inc(y_read, 1)

                    for ch in range(CHUNKS):
                        if gated:
                            for f in range(FC):
                                k = (E * it + a) * STEPS + ch * FC + f
                                dve.wait_ge(gelued, k + 1 + 2)
                                dve.wait_ge(upped, 2 * k + 2)
                                if f == 0:
                                    dve.wait_ge(y_ready, (E * it + a) * CHUNKS + ch + 1)
                                dve.tensor_tensor(hidden[ch % 2][:, f, :], u2_ps[f % 2][:], gelu[f % 2][:],
                                                  ALU.mult).then_inc(multiplied, 1)
                        if ch >= 1:
                            accumulate(ch - 1)
                    accumulate(CHUNKS - 1)


class Once:

    def __enter__(self):
        return 0

    def __exit__(self, *_):
        return False


def clear(core, buffers, value=0.0):
    with core.scope() as s:
        block = s.block()

        @block.vector
        def _(dve):
            for buffer in buffers:
                dve.memset(buffer, value)


def add_gated(core, c, layer, acc, out):
    with core.scope() as s:
        scaled, added, stored = s.sem("scaled"), s.sem("added"), s.sem("stored")
        block = s.block()

        @block.vector
        def _(dve):
            for b in range(B):
                part = acc[:, b * TPB:(b + 1) * TPB, :]
                dve.tensor_tensor(part, part, c.gate_b[layer][:, b, :].unsqueeze(1).broadcast_to([P, TPB, D]),
                                  ALU.mult).then_inc(scaled, 1)
            for b in range(B):
                tiles = slice(b * TPB, (b + 1) * TPB)
                dve.wait_ge(scaled, b + 1)
                dve.tensor_tensor(c.x[:, tiles, :], c.x[:, tiles, :], acc[:, tiles, :], ALU.add).then_inc(added, 1)

        @block.sync
        def _(sp):
            if out is not None:
                for b in range(B):
                    sp.wait_ge(added, b + 1)
                    sp.dma_start(out[b].rearrange("(t p) d -> p t d", p=P),
                                 c.x[:, b * TPB:(b + 1) * TPB, :]).then_inc(stored, 16)
                sp.wait_ge(stored, 16 * B)


def lora_weights(core, ins, wqkv, wo):
    RANK = 16
    with core.scope() as s:
        a_qkv = s.sbuf("a_qkv", [RANK, 3, D], F32)
        b_qkv = s.sbuf("b_qkv", [RANK, 3, D], F32)
        a_o = s.sbuf("a_o", [RANK, 4, P], F32)
        b_o = s.sbuf("b_o", [RANK, D], F32)
        low_qkv = s.psum("low_qkv", [P, 3, D])
        low_o = s.psum("low_o", [P, 4, D])
        loaded, product = s.sem("loaded"), s.sem("product")
        block = s.block()
        loads = ((a_qkv, "a_qkv"), (b_qkv, "b_qkv"), (a_o, "a_o"), (b_o, "b_o"), (wqkv, "w_qkv"), (wo, "w_o"))

        @block.sync
        def _(sp):
            for buffer, name in loads:
                sp.dma_start(buffer[:], ins["lora_" + name]).then_inc(loaded, 16)

        @block.tensor
        def _(pe):
            pe.wait_ge(loaded, 16 * len(loads))
            for j in range(3):
                last = pe.matmul(low_qkv[:, j, :], a_qkv[:, j, :], b_qkv[:, j, :], start=True, stop=True)
            last.then_inc(product, 1)
            for g in range(4):
                last = pe.matmul(low_o[:, g, :], a_o[:, g, :], b_o[:], start=True, stop=True)
            last.then_inc(product, 1)

        @block.vector
        def _(dve):
            dve.wait_ge(loaded, 16 * len(loads))
            dve.wait_ge(product, 2)
            dve.scalar_tensor_tensor(out=wqkv[:], in0=low_qkv[:], scalar=1.0 / RANK, in1=wqkv[:],
                                     op0=ALU.mult, op1=ALU.add)
            dve.scalar_tensor_tensor(out=wo[:], in0=low_o[:], scalar=1.0 / RANK, in1=wo[:],
                                     op0=ALU.mult, op1=ALU.add)


def project_narrow(core, c, b, wqkv, Qp, Kp, V):
    G = 4
    LOOPS = TPB // 2
    with core.scope() as s:
        h_tile = [s.sbuf(f"h_tile{i}", [P, P], F32) for i in range(2)]
        qk = [s.sbuf(f"qk{i}", [P, 2, H, HD1], F32) for i in range(2)]
        parts = [s.sbuf(f"parts{i}", [P, 2, H, 2, 2, HD1], F16) for i in range(2)]
        proj = [s.psum(f"proj{i}", [P, 3 * D]) for i in range(2)]
        partsT = [[s.psum(f"partsT{i}{j}", [P, 2, G, P], F16) for j in range(2)] for i in range(2)]
        h_ready, projected, copied, hi_done, lo_done, t_done, q_read, k_read = (
            s.sem(n) for n in ("h_ready", "projected", "copied", "hi_done", "lo_done", "t_done", "q_read", "k_read"))
        block = s.block()

        def slots(a, which):
            v = parts[a][:, which]
            return (v[:, :, :, 0, :], v[:, :, :, 1, :]) if which == 0 else (v[:, :, 0, :, :], v[:, :, 1, :, :])

        @block.tensor
        def _(pe):
            with pe.Fori(0, LOOPS, 1) as it:
                for a in range(2):
                    pe.wait_ge(h_ready, 2 * it + a + 1)
                    pe.wait_ge(copied, 2 * it + a + 1)
                    pe.matmul(proj[a][:], h_tile[a][:], wqkv[:].rearrange("p j d -> p (j d)"),
                              start=True, stop=True).then_inc(projected, 1)
                for a in range(2):
                    pe.wait_ge(lo_done, 2 * it + a + 1)
                    pe.wait_ge(q_read, 2 * it + a + 1)
                    pe.wait_ge(k_read, 2 * it + a + 1)
                    for which in range(2):
                        for g in range(G):
                            last = pe.transpose(partsT[a][which][:, 0, g, :],
                                                parts[a][:, which, g * G:(g + 1) * G].rearrange("p h a b d -> p (h a b d)"),
                                                c.identh[:])
                    last.then_inc(t_done, 1)

        @block.scalar
        def _(act):
            act.sem_inc(copied, 2)
            act.sem_inc(k_read, 2)
            with act.Fori(0, LOOPS, 1) as it:
                for a in range(2):
                    act.wait_ge(projected, 2 * it + a + 1)
                    act.copy(h_tile[a][:], c.hT[:, bass.ds((2 * it + a) * P + b * S, P)]).then_inc(h_ready, 1)
                for a in range(2):
                    act.wait_ge(projected, 2 * it + a + 1 + 2)
                    act.wait_ge(q_read, 2 * it + a + 1)
                    q, k, v = (proj[a][:, j * D:(j + 1) * D] for j in range(3))
                    act.mul(qk[a][:, 0].rearrange("p h d -> p (h d)"), q, float(HD1) ** -0.5)
                    act.copy(qk[a][:, 1].rearrange("p h d -> p (h d)"), k)
                    act.copy(V[:, 2 * it + a, :].rearrange("p (h d) -> p h d", h=H)[:, :, 0:HD1],
                             v.rearrange("p (h d) -> p h d", h=H)).then_inc(copied, 1)
                for a in range(2):
                    act.wait_ge(t_done, 2 * it + a + 1)
                    act.copy(Kp[:, :, bass.ds((2 * it + a) * P, P)], partsT[a][1][:, 0]).then_inc(k_read, 1)

        @block.vector
        def _(dve):
            dve.sem_inc(projected, 2)
            dve.sem_inc(q_read, 2)
            with dve.Fori(0, LOOPS, 1) as it:
                for a in range(2):
                    dve.wait_ge(copied, 2 * it + a + 1 + 2)
                    for which in range(2):
                        src = qk[a][:, which].unsqueeze(2).broadcast_to([P, H, 2, HD1])
                        last = dve.tensor_copy(slots(a, which)[0], src)
                    last.then_inc(hi_done, 1)
                    dve.wait_ge(hi_done, 2 * it + a + 1)
                    for which in range(2):
                        src = qk[a][:, which].unsqueeze(2).broadcast_to([P, H, 2, HD1])
                        last = dve.tensor_tensor(slots(a, which)[1], src, slots(a, which)[0], ALU.subtract)
                    last.then_inc(lo_done, 1)
                for a in range(2):
                    dve.wait_ge(t_done, 2 * it + a + 1)
                    q_heads = Qp[:].rearrange("p (g r) s -> p g r s", r=G)
                    for r in range(G):
                        rows = slice(32 * r, 32 * r + 32)
                        last = dve.tensor_copy(q_heads[rows, :, r, bass.ds((2 * it + a) * P, P)], partsT[a][0][rows, 0])
                    last.then_inc(q_read, 1)


def route_experts_choice(core, c, wg_in, weight):
    with core.scope() as s:
        wg = s.sbuf("wg", [P, NE], F32)
        peak = s.sbuf("peak", [P, NT], F32)
        prob = s.sbuf("prob", [P, NT, NE], F32)
        prob_t = s.sbuf("prob_t", [P, TPB, B, NE], F32)
        rows = s.sbuf("rows", [B * NE, S], F32)
        left = s.sbuf("left", [B * NE, S], F32)
        top = s.sbuf("top", [B * NE, 8], F32)
        logits = s.psum("logits", [P, NT, NE])
        rows_ps = [s.psum(f"rows_ps{i}", [B * NE, BANK]) for i in range(2)]
        weight_ps = s.psum("weight_ps", [P, TPB, B, NE])
        loaded, scored, exped, step, turned, found, back = (
            s.sem(n) for n in ("loaded", "scored", "exped", "step", "turned", "found", "back"))
        block = s.block()

        @block.sync
        def _(sp):
            sp.dma_start(wg[:], wg_in).then_inc(loaded, 16)

        @block.tensor
        def _(pe):
            pe.wait_ge(loaded, 16)
            for t in range(NT):
                last = pe.matmul(logits[:, t, :], c.hT[:, t * P:(t + 1) * P], wg[:], start=True, stop=True)
            last.then_inc(scored, 1)
            pe.wait_ge(step, 6)
            for t in range(TPB):
                last = pe.transpose(rows_ps[t // 4][:, (t % 4) * P:(t % 4 + 1) * P],
                                    prob_t[:, t].rearrange("p b e -> p (b e)"), c.identf[:])
            last.then_inc(turned, 1)
            pe.wait_ge(back, 1)
            for t in range(TPB):
                last = pe.transpose(weight_ps[:, t].rearrange("p b e -> p (b e)"), rows[:, t * P:(t + 1) * P],
                                    c.identf[0:B * NE, 0:B * NE])
            last.then_inc(turned, 1)

        @block.scalar
        def _(act):
            act.wait_ge(step, 2)
            act.activation(prob[:], prob[:], ACT.Exp).then_inc(exped, 1)

        @block.vector
        def _(dve):
            def wide(v):
                return v.unsqueeze(2).broadcast_to([P, NT, NE])
            dve.wait_ge(scored, 1)
            dve.tensor_reduce(peak[:], logits[:], AX_X, ALU.max).then_inc(step, 1)
            dve.wait_ge(step, 1)
            dve.tensor_tensor(prob[:], logits[:], wide(peak[:]), ALU.subtract).then_inc(step, 1)
            dve.wait_ge(exped, 1)
            dve.tensor_reduce(peak[:], prob[:], AX_X, ALU.add).then_inc(step, 1)
            dve.wait_ge(step, 3)
            dve.reciprocal(peak[:], peak[:]).then_inc(step, 1)
            dve.wait_ge(step, 4)
            dve.tensor_tensor(prob[:], prob[:], wide(peak[:]), ALU.mult).then_inc(step, 1)
            dve.wait_ge(step, 5)
            dve.tensor_copy(prob_t[:].rearrange("p t b e -> p b t e"), prob[:].rearrange("p (b t) e -> p b t e", b=B))\
               .then_inc(step, 1)
            dve.wait_ge(turned, 1)
            for i in range(2):
                dve.tensor_copy(rows[:, i * BANK:(i + 1) * BANK], rows_ps[i][:])
                last = dve.tensor_copy(left[:, i * BANK:(i + 1) * BANK], rows_ps[i][:])
            last.then_inc(found, 2)
            for it in range(TOPK // 8):
                dve.wait_ge(found, 2 * it + 2)
                dve.max(top[:], left[:]).then_inc(found, 1)
                dve.wait_ge(found, 2 * it + 3)
                dve.match_replace(out=left[:], in_to_replace=top[:], in_values=left[:], imm_value=-1.0).then_inc(found, 1)
            dve.wait_ge(found, 2 * (TOPK // 8) + 2)
            dve.scalar_tensor_tensor(out=rows[:], in0=left[:], scalar=0.0, in1=rows[:], op0=ALU.is_lt,
                                     op1=ALU.mult).then_inc(back, 1)
            dve.wait_ge(turned, 2)
            dve.tensor_copy(weight[:], weight_ps[:])


def block0(core, c, top, ins):
    norm_modulate(core, c, 0, SA, CA)
    with core.scope() as s:
        Qp = s.sbuf("Qp", [P, H, S], F16)
        Kp = s.sbuf("Kp", [P, H, S], F16)
        V = s.sbuf("V", [P, TPB, H * HD0], F32)
        wqkv = s.sbuf("wqkv", [P, 3 * H * HD0], F32)
        wo = s.sbuf("wo", [P, H * HD0 // P, D], F32)
        rope = s.sbuf("rope", [P, TPB, 4, HD0], F32)
        with core.scope() as ld:
            loaded = ld.sem("loaded")
            block = ld.block()

            @block.sync
            def _(sp):
                sp.dma_start(wqkv[:], ins["L0_attn_wqkv"]).then_inc(loaded, 16)
                sp.dma_start(rope[:].rearrange("p t j d -> p t (j d)"), ins["rope"].rearrange("(t p) j d -> p t (j d)", p=P)).then_inc(loaded, 16)
                sp.dma_start(wo[:], ins["L0_attn_wo"].rearrange("(u p) d -> p u d", p=P)).then_inc(loaded, 16)
                sp.wait_ge(loaded, 48)
        ctxT = Qp[:].bitcast(F32).rearrange("p (u two) s -> p u (two s)", two=2)
        for b in range(B):
            project_rope(core, c, b, wqkv, rope, Qp, Kp, V)
            attend(core, c, 2, Qp, Kp, V, ctxT, 2, 2)
            project_out(core, c, b, 0, H // 2, ctxT, wo)
    norm_modulate(core, c, 0, SB, CB)
    with core.scope() as s:
        acc = s.sbuf("acc", [P, NT, D], F32)
        one = s.sbuf("one", [P, 1], F32)
        r = Routing(core, s)
        clear(core, [acc[:]])
        route_top1(core, c, ins["L0_ffn_Wg"], r, acc)
        clear(core, [one[:]], 1.0)
        experts(core, c, lambda e: ins["L0_ffn_w1s"], lambda e: ins["L0_ffn_w2s"],
                lambda e: ins["L0_ffn_w3s"].rearrange("(f p) d -> p f d", p=P), 1, lambda t, e: one[:], acc,
                lambda pool, sent: scatter_tokens(pool, r, sent))
        up, up2 = (ins[n].rearrange("e d f -> d e f") for n in ("L0_ffn_W1", "L0_ffn_W2"))
        down = ins["L0_ffn_W3"].rearrange("e (f p) d -> p (e f) d", p=P)
        sorted_experts(core, c, lambda e: up[:, bass.ds(e, 1), :], lambda e: up2[:, bass.ds(e, 1), :],
                       lambda e: down[:, bass.ds(e * FC, FC), :], r)
        gather_tokens(core, r, acc)
        add_gated(core, c, 0, acc, None)


def block1(core, c, top, ins, out):
    norm_modulate(core, c, 1, SA, CA)
    with core.scope() as s:
        Qp = s.sbuf("Qp", [P, H, S], F16)
        Kp = s.sbuf("Kp", [P, 4, S], F16)
        V = s.sbuf("V", [P, TPB, H * 32], F32)
        ctxT = s.sbuf("ctxT", [P, 4, S], F32)
        wqkv = s.sbuf("wqkv", [P, 3, D], F32)
        wo = s.sbuf("wo", [P, 4, D], F32)
        lora_weights(core, ins, wqkv, wo)
        clear(core, [Qp[:].bitcast(F32), V[:]])
        for b in range(B):
            project_narrow(core, c, b, wqkv, Qp, Kp, V)
            attend(core, c, 4, Qp, Kp, V, ctxT, 1, 1)
            project_out(core, c, b, 1, 4, ctxT, wo)
    norm_modulate(core, c, 1, SB, CB)
    with core.scope() as s:
        weight = s.sbuf("weight", [P, TPB, B, NE], F32)
        acc = s.sbuf("acc", [P, NT, D], F32)
        clear(core, [acc[:]])
        route_experts_choice(core, c, ins["gate_wT"], weight)
        experts(core, c, lambda e: ins["L1_ffn_w1"][e], None,
                lambda e: ins["L1_ffn_w2"][e].rearrange("(f p) d -> p f d", p=P), NE,
                lambda t, e: weight[:, t % TPB, t // TPB, bass.ds(e, 1)], acc)
        add_gated(core, c, 1, acc, out)


def build(nc, ins, out):
    core = Core(nc)
    with core.scope() as top:
        c = load_constants(core, top, ins)
        modulation(core, c, 0, ins["L0_cT"], ins["L0_wmod"])
        modulation(core, c, 1, ins["L1_cT"], ins["L1_wmod"])
        block0(core, c, top, ins)
        block1(core, c, top, ins, out)


def rope_tables():
    half = HD0 // 2
    fraction = (np.float32(2.0) * np.arange(half, dtype=np.float32) / np.float32(HD0)).astype(np.float32)
    timescale = np.power(np.float32(10000.0), fraction).astype(np.float32)
    angle = np.arange(S, dtype=np.float32)[:, None] / timescale
    cos, sin = np.cos(angle), np.sin(angle)
    k = [np.concatenate([cos, cos], 1), np.concatenate([sin, -sin], 1)]
    q = [t * np.float32(HD0 ** -0.5) for t in k]
    return np.stack(q + k, 1).astype(np.float32)


def layout(inputs):
    a = {n: np.asarray(v) for n, v in inputs.items()}
    keep = ["L0_attn_x", "L0_attn_wqkv", "L0_attn_wo", "L0_ffn_w1s", "L0_ffn_w2s", "L0_ffn_w3s", "L0_ffn_W1",
            "L0_ffn_W2", "L0_ffn_W3", "L0_ffn_Wg", "L0_wmod", "L1_wmod", "L1_ffn_w1", "L1_ffn_w2"]
    arrays = {n: a[n] for n in keep}
    arrays["L0_cT"], arrays["L1_cT"] = a["L0_c"].T, a["L1_c"].T
    arrays["gate_wT"] = a["L1_ffn_gate_w"].T
    arrays["rope"] = rope_tables()
    arrays["lora_w_qkv"] = np.stack([a["L1_attn_w" + n].T for n in "qkv"], 1)
    arrays["lora_a_qkv"] = np.stack([a["L1_attn_a" + n] for n in "qkv"], 1)
    arrays["lora_b_qkv"] = np.stack([a["L1_attn_b" + n].T for n in "qkv"], 1)

    def pad(v):
        v = v.reshape(v.shape[0], 4, 4, HD1)
        return np.pad(v, ((0, 0), (0, 0), (0, 0), (0, 32 - HD1))).reshape(v.shape[0], 4, P)
    arrays["lora_w_o"] = pad(a["L1_attn_wo"]).transpose(2, 1, 0)
    arrays["lora_a_o"] = pad(a["L1_attn_ao"])
    arrays["lora_b_o"] = a["L1_attn_bo"].T
    return {n: np.ascontiguousarray(v) for n, v in arrays.items()}


def kernel(**inputs):
    import concourse.bacc as bacc
    from concourse.bass_utils import run_bass_kernel_spmd

    nc = bacc.Bacc("TRN2", target_bir_lowering=False, num_devices=1)
    arrays = layout(inputs)
    ins = {n: nc.dram_tensor(n, v.shape, mybir.dt.from_np(v.dtype), kind="ExternalInput").ap()
           for n, v in arrays.items()}
    out = nc.dram_tensor("out", (B, S, D), F32, kind="ExternalOutput").ap()
    build(nc, ins, out)
    return run_bass_kernel_spmd(nc, [arrays], core_ids=[0]).results[0]["out"]
```

```python
from contextlib import ExitStack

import numpy as np

import concourse.bass as bass
from concourse import mybir

ALU = mybir.AluOpType
ACT = mybir.ActivationFunctionType
F32 = mybir.dt.float32
F16 = mybir.dt.float16
BF16 = mybir.dt.bfloat16
AX_X = mybir.AxisListType.X

P = 128
LAYERS = 2
B, S, D = 2, 1024, 128
TPB = S // P
NT = B * TPB
H = 16
HD0, HD1 = 64, 8
FF = 512
FC = FF // P
NE = 8
TOPK = 2 * S // NE
DIGITS = 15
A_BITS = 4
A = 2 ** A_BITS
RING = 4
BANK = 512
EPS = 1e-5
MASKED = -1e30
SA, CA, GA, SB, CB, GB = range(6)
FIRST = 0
ORDER = [0, 2, 4, 6, 7, 5, 3, 1]


class Core:

    def __init__(self, nc):
        self.nc = nc
        self.n = 0

    def scope(self):
        return Scope(self)


class Scope(ExitStack):

    def __init__(self, core):
        super().__init__()
        self.core = core

    def _name(self, name):
        self.core.n += 1
        return f"{name}_{self.core.n}"

    def sbuf(self, name, shape, dt):
        return self.enter_context(self.core.nc.sbuf_tensor(self._name(name), shape, dt))

    def psum(self, name, shape, dt=F32):
        return self.enter_context(self.core.nc.psum_tensor(self._name(name), shape, dt))

    def sem(self, name):
        handle = self.enter_context(self.core.nc.semaphore(self._name(name)))
        self.callback(lambda: self.core.nc.gpsimd.sem_clear(handle))
        return handle

    def gpsimd_dma_sem(self, name):
        return self.core.nc.alloc_semaphore(self._name(name))

    def block(self):
        return self.enter_context(self.core.nc.Block())


class Consts:

    def __init__(self, top):
        self.x = top.sbuf("x", [P, NT, D], F32)
        self.identf = top.sbuf("identf", [P, P], F32)
        self.identh = top.sbuf("identh", [P, P], F16)
        self.identb = top.sbuf("identb", [P, P], BF16)
        self.causal = top.sbuf("causal", [P, P], BF16)
        self.hT = top.sbuf("hT", [P, NT * P], F32)
        self.mod_all = top.sbuf("mod", [P, LAYERS, 6, B], F32)
        self.gate_b_all = top.sbuf("gate_b", [P, LAYERS, B, D], F32)
        self.mod = [self.mod_all[:, layer] for layer in range(LAYERS)]
        self.gate_b = [self.gate_b_all[:, layer] for layer in range(LAYERS)]


def start(core, ins, c, later):
    CLAMPED = 12
    with core.scope() as s:
        ct = s.sbuf("ct", [P, LAYERS, B], F32)
        wm = s.sbuf("wm", [P, LAYERS, 6 * D], F32)
        ex = s.sbuf("ex", [P, LAYERS, B], F32)
        silu = s.sbuf("silu", [P, LAYERS, B], F32)
        silu_b = s.sbuf("silu_b", [P, LAYERS, B, P], F32)
        g = s.sbuf("g", [P, 2, LAYERS, B, P], F32)
        mod_ps = s.psum("mod_ps", [P, LAYERS, 6, B])
        row_ps = s.psum("row_ps", [P, LAYERS, B, D])
        buffers = norm_buffers(s)
        x_in, c_in, loaded, arriving, made, exped, silu_ready, products, step = (
            s.sem(n) for n in ("x_in", "c_in", "loaded", "arriving", "made", "exped", "silu", "products", "step"))
        block = s.block()

        @block.sync
        def _(sp):
            for layer in range(LAYERS):
                sp.dma_start(ct[:, layer], ins[f"L{layer}_cT"]).then_inc(c_in, 16)
            sp.dma_start(c.x[:], ins["L0_attn_x"].rearrange("b (t p) d -> p (b t) d", p=P)).then_inc(x_in, 16)
            for layer in range(LAYERS):
                sp.dma_start(wm[:, layer], ins[f"L{layer}_wmod"]).then_inc(loaded, 16)
            for to, source in later:
                sp.dma_start(to, source).then_inc(arriving, 16)
            sp.wait_ge(arriving, 16 * len(later))

        @block.gpsimd
        def _(pool):
            pool.memset(c.identf[:], 0.0).then_inc(made, 1)
            pool.memset(c.causal[:], 0.0).then_inc(made, 1)
            pool.wait_ge(made, 2)
            pool.affine_select(out=c.identf[:], in_=c.identf[:], compare_op=ALU.not_equal, fill=1.0, base=0,
                               pattern=[[-1, P]], channel_multiplier=1).then_inc(made, 1)
            pool.affine_select(out=c.causal[:], in_=c.causal[:], compare_op=ALU.is_ge, fill=MASKED, base=0,
                               pattern=[[-1, P]], channel_multiplier=1).then_inc(made, 1)
            pool.wait_ge(made, 4)
            pool.tensor_copy(c.identh[:], c.identf[:]).then_inc(made, 1)
            pool.tensor_copy(c.identb[:], c.identf[:]).then_inc(made, 1)

        @block.scalar
        def _(act):
            act.wait_ge(c_in, 16 * LAYERS)
            act.activation(ex[:], ct[:], ACT.Exp, scale=-1.0).then_inc(exped, 1)

        @block.tensor
        def _(pe):
            pe.wait_ge(silu_ready, 2)
            pe.wait_ge(loaded, 16 * LAYERS)
            for layer in range(LAYERS):
                for j in range(6):
                    pe.matmul(mod_ps[:, layer, j, :], wm[:, layer, j * D:(j + 1) * D], silu[:, layer, :],
                              start=True, stop=True)
                for b in range(B):
                    last = pe.matmul(row_ps[:, layer, b, :], silu_b[:, layer, b, :],
                                     wm[:, layer, GB * D:(GB + 1) * D], start=True, stop=True)
            last.then_inc(products, 1)

        @block.vector
        def _(dve):
            dve.wait_ge(exped, 1)
            dve.tensor_scalar(ex[:], ex[:], 1.0, None, ALU.add).then_inc(step, 1)
            dve.wait_ge(step, 1)
            dve.reciprocal(ex[:], ex[:]).then_inc(step, 1)
            dve.wait_ge(step, 2)
            dve.tensor_tensor(silu[:], ex[:], ct[:], ALU.mult).then_inc(silu_ready, 1)
            dve.wait_ge(silu_ready, 1)
            dve.tensor_copy(silu_b[:], silu[:].unsqueeze(3).broadcast_to([P, LAYERS, B, P])).then_inc(silu_ready, 1)

        norm(block, buffers, c, 0, SA, CA, x_ready=(x_in, 16), ident_ready=(made, 4), mod_ready=(step, CLAMPED))

        @block.vector
        def _(dve):
            dve.wait_ge(products, 1)
            dve.tensor_copy(c.mod_all[:], mod_ps[:]).then_inc(step, 1)
            dve.tensor_copy(c.gate_b_all[:], row_ps[:]).then_inc(step, 1)
            dve.wait_ge(step, 4)
            n = 4
            for j in (CA, CB):
                dve.tensor_scalar(c.mod_all[:, :, j, :], c.mod_all[:, :, j, :], 1.0, None, ALU.add).then_inc(step, 1)
                n += 1
            for gate, sgn, mag in ((c.mod_all[:, :, GA, :], g[:, 0, :, :, 0], g[:, 1, :, :, 0]),
                                   (c.gate_b_all[:], g[:, 0], g[:, 1])):
                dve.wait_ge(step, n)
                dve.tensor_scalar(sgn, gate, 0.0, 2.0, ALU.is_ge, ALU.mult).then_inc(step, 1)
                dve.tensor_scalar(mag, gate, -1.0, None, ALU.mult).then_inc(step, 1)
                dve.wait_ge(step, n + 2)
                dve.tensor_tensor(mag, mag, gate, ALU.max).then_inc(step, 1)
                dve.tensor_scalar(sgn, sgn, -1.0, None, ALU.add).then_inc(step, 1)
                dve.wait_ge(step, n + 4)
                dve.tensor_scalar(mag, mag, 0.25, None, ALU.max).then_inc(step, 1)
                dve.wait_ge(step, n + 5)
                dve.tensor_tensor(gate, mag, sgn, ALU.mult).then_inc(step, 1)
                n += 6


def norm_modulate(core, c, layer, shift, scale, zeros=None):
    with core.scope() as s:
        buffers = norm_buffers(s)
        norm(s.block(), buffers, c, layer, shift, scale, zeros)


def norm_buffers(s):
    return ([s.sbuf(n, [P, NT, D], F32) for n in ("xc", "sq")], [s.sbuf(n, [P, NT], F32) for n in ("mean", "var")],
            [s.psum(f"xT{i}", [P, BANK]) for i in range(4)],
            [s.sem(n) for n in ("step", "squared", "rooted", "xhat", "turned")],
            [s.sem(f"centered{i}") for i in range(B)])


def norm(block, buffers, c, layer, shift, scale, zeros=None, x_ready=None, ident_ready=None, mod_ready=None):
    mod = c.mod[layer]
    (xc, sq), (mean, var), xT, (step, squared, rooted, xhat, turned), centered = buffers
    per_bank = BANK // P

    def bcast(v):
        return v.unsqueeze(2).broadcast_to([P, v.shape[1], D])

    halves = [slice(b * TPB, (b + 1) * TPB) for b in range(B)]

    def wait(eng, ready):
        if ready is not None:
            eng.wait_ge(*ready)

    @block.gpsimd
    def _(pool):
        pool.wait_ge(step, 2)
        pool.tensor_tensor(xc[:, halves[1], :], c.x[:, halves[1], :], bcast(mean[:, halves[1]]), ALU.subtract)\
            .then_inc(centered[1], 1)
        if zeros is not None:
            pool.memset(zeros, 0.0)

    @block.vector
    def _(dve):
        wait(dve, x_ready)
        for half in halves:
            last = dve.tensor_reduce(mean[:, half], c.x[:, half, :], AX_X, ALU.add)
        last.then_inc(step, 1)
        dve.wait_ge(step, 1)
        dve.tensor_scalar(mean[:], mean[:], 1.0 / D, None, ALU.mult).then_inc(step, 1)
        dve.wait_ge(step, 2)
        dve.tensor_tensor(xc[:, halves[0], :], c.x[:, halves[0], :], bcast(mean[:, halves[0]]),
                          ALU.subtract).then_inc(centered[0], 1)
        for i, half in enumerate(halves):
            dve.wait_ge(squared, i + 1)
            dve.tensor_reduce(var[:, half], sq[:, half, :], AX_X, ALU.add).then_inc(step, 1)
            dve.wait_ge(step, 3 + 2 * i)
            dve.tensor_scalar(var[:, half], var[:, half], 1.0 / D, EPS, ALU.mult, ALU.add).then_inc(step, 1)
        for i, half in enumerate(halves):
            dve.wait_ge(rooted, i + 1)
            dve.reciprocal(var[:, half], var[:, half]).then_inc(step, 1)
            dve.wait_ge(step, 7 + i)
            for q in range(2 * i, 2 * i + 2):
                part = slice(q * per_bank, (q + 1) * per_bank)
                dve.tensor_tensor(xc[:, part, :], xc[:, part, :], bcast(var[:, part]), ALU.mult).then_inc(xhat, 1)

    @block.scalar
    def _(act):
        for i, half in enumerate(halves):
            act.wait_ge(centered[i], 1)
            act.activation(sq[:, half, :], xc[:, half, :], ACT.Square).then_inc(squared, 1)
        for i, half in enumerate(halves):
            act.wait_ge(step, 4 + 2 * i)
            act.activation(var[:, half], var[:, half], ACT.Sqrt).then_inc(rooted, 1)
        wait(act, mod_ready)
        for q in range(4):
            b = q * per_bank // TPB
            act.wait_ge(turned, q + 1)
            act.activation(c.hT[:, q * BANK:(q + 1) * BANK], xT[q][:], ACT.Identity,
                           bias=mod[:, shift, b:b + 1], scale=mod[:, scale, b:b + 1])

    @block.tensor
    def _(pe):
        wait(pe, ident_ready)
        for q in range(4):
            pe.wait_ge(xhat, q + 1)
            for k in range(per_bank):
                last = pe.transpose(xT[q][:, k * P:(k + 1) * P], xc[:, q * per_bank + k, :], c.identf[:])
            last.then_inc(turned, 1)


def project_rope(core, c, b, wqkv, rope, Qp, Kp, V):
    CH = 6
    QK = 4
    HPC = BANK // HD0
    RING = QK
    LAG = 2
    with core.scope() as s:
        h_tile = [s.sbuf(f"h_tile{i}", [P, P], F32) for i in range(2)]
        by_cos = [s.sbuf(f"by_cos{i}", [P, HPC, 2, HD0 // 2], F32) for i in range(RING)]
        by_sin = [s.sbuf(f"by_sin{i}", [P, HPC, 2, HD0 // 2], F32) for i in range(RING)]
        turned = [s.sbuf(f"turned{i}", [P, HPC, 2, HD0 // 2], F32) for i in range(RING)]
        parts = [s.sbuf(f"parts{i}", [P, QK, HPC, 2, HD0], F16) for i in range(2)]
        proj = [s.psum(f"proj{i}", [P, BANK]) for i in range(4)]
        partsT = [s.psum(f"partsT{i}", [P, HPC, P], F16) for i in range(2)]
        (h_ready, projected, rope_read, v_read, roped, hi_done, lo_done, t_done, t_read) = (
            s.sem(n) for n in ("h_ready", "projected", "rope_read", "v_read", "roped", "hi_done", "lo_done",
                               "t_done", "t_read"))
        block = s.block()
        LOOPS = TPB // 2

        @block.tensor
        def _(pe):
            def project(t, a, turns=True):
                pe.wait_ge(h_ready, t + 1)
                for ch in range(CH):
                    tile, before = divmod(ch - 4, CH)
                    if before < QK:
                        pe.wait_ge(rope_read, (t + tile + 1) * QK + before + 1)
                    else:
                        pe.wait_ge(v_read, (t + tile + 1) * 2 + before - QK + 1)
                    pe.matmul(proj[(a * CH + ch) % 4][:], h_tile[a][:], wqkv[:, ch * BANK:(ch + 1) * BANK],
                              start=True, stop=True).then_inc(projected, 1)
                    if turns and 1 <= ch <= QK:
                        turn(t - 1, 1 - a, ch - 1)

            def turn(t, a, ch):
                pe.wait_ge(lo_done, QK * t + ch + 1 + RING)
                pe.wait_ge(t_read, QK * t + ch + 1)
                for h in range(HPC):
                    last = pe.transpose(partsT[ch % 2][:, h, :],
                                        parts[a][:, ch, h].rearrange("p a d -> p (a d)"), c.identh[:])
                last.then_inc(t_done, 1)

            project(0, 0, turns=False)
            project(1, 1)
            with pe.Fori(0, LOOPS - 1, 1) as it:
                for a in range(2):
                    project(2 * it + a + 2, a)
            for ch in range(QK):
                turn(TPB - 1, 1, ch)

        @block.vector
        def _(dve):
            dve.sem_inc(rope_read, QK)
            dve.sem_inc(lo_done, RING)

            def low_part(t, a, ch):
                dve.wait_ge(hi_done, QK * t + ch + 1)
                dve.tensor_tensor(parts[a][:, ch, :, 1, :], turned[ch % RING][:].rearrange("p h a d -> p h (a d)"),
                                  parts[a][:, ch, :, 0, :], ALU.subtract).then_inc(lo_done, 1)

            def rotate(t, a, first=False):
                for ch in range(QK):
                    table = 2 * (ch // 2)
                    dve.wait_ge(projected, CH * t + ch + 1)
                    dve.wait_ge(roped, QK * t + ch + 1)
                    src = proj[(a * CH + ch) % 4][:].rearrange("p (h d) -> p h d", h=HPC)
                    for out, tab in ((by_cos, table), (by_sin, table + 1)):
                        last = dve.tensor_tensor(out[ch % RING][:].rearrange("p h a d -> p h (a d)"), src,
                                                 rope[:, t, tab, :].unsqueeze(1).broadcast_to([P, HPC, HD0]), ALU.mult)
                    last.then_inc(rope_read, 1)
                    if ch >= LAG:
                        low_part(t, a, ch - LAG)
                    elif not first:
                        low_part(t - 1, 1 - a, QK + ch - LAG)

            rotate(0, 0, first=True)
            rotate(1, 1)
            with dve.Fori(0, LOOPS - 1, 1) as it:
                for a in range(2):
                    rotate(2 * it + a + 2, a)
            for ch in range(QK - LAG, QK):
                low_part(TPB - 1, 1, ch)

        @block.gpsimd
        def _(pool):
            pool.sem_inc(roped, RING)
            with pool.Fori(0, LOOPS, 1) as it:
                for g in range(2 * QK):
                    pool.wait_ge(rope_read, 2 * QK * it + g + 1 + QK)
                    pool.wait_ge(lo_done, 2 * QK * it + g + 1)
                    for half in range(2):
                        last = pool.tensor_tensor(turned[g % RING][:, :, half, :], by_cos[g % RING][:, :, half, :],
                                                  by_sin[g % RING][:, :, 1 - half, :], ALU.add)
                    last.then_inc(roped, 1)

        @block.scalar
        def _(act):
            act.sem_inc(v_read, 2)
            act.sem_inc(t_read, 2)

            def h_copy(t, a):
                act.copy(h_tile[a][:], c.hT[:, bass.ds(t * P + b * S, P)]).then_inc(h_ready, 1)

            def high_part(t, a, ch):
                act.wait_ge(roped, QK * t + ch + 1 + RING)
                act.copy(parts[a][:, ch, :, 0, :],
                         turned[ch % RING][:].rearrange("p h a d -> p h (a d)")).then_inc(hi_done, 1)

            def evacuate(t, ch):
                act.wait_ge(t_done, QK * t + ch + 1)
                dst = Qp if ch < 2 else Kp
                act.copy(dst[:, (ch % 2) * HPC:(ch % 2 + 1) * HPC, bass.ds(t * P, P)], partsT[ch % 2][:])\
                   .then_inc(t_read, 1)

            def tile(t, a, first=False, last=False):
                for ch in range(QK):
                    if not first:
                        evacuate(t - 1, ch)
                    high_part(t, a, ch)
                for half in range(2):
                    act.wait_ge(projected, CH * t + QK + half + 1)
                    act.copy(V[:, t, half * BANK:(half + 1) * BANK], proj[(a * CH + QK + half) % 4][:])\
                       .then_inc(v_read, 1)
                if not last:
                    h_copy(t + 2, a)

            h_copy(0, 0)
            h_copy(1, 1)
            tile(0, 0, first=True)
            tile(1, 1)
            with act.Fori(0, LOOPS - 2, 1) as it:
                for a in range(2):
                    tile(2 * it + a + 2, a)
            tile(TPB - 2, 0, last=True)
            tile(TPB - 1, 1, last=True)
            for ch in range(QK):
                evacuate(TPB - 1, ch)


def attend(core, c, U, Qp, Kp, V, ctxT, q_orders, k_heads):
    HW = P // U
    LOOPS = H // U // 2
    TILES = 2 * TPB
    tiles = [(a, i) for a in range(2) for i in ORDER]
    items = [(p, h) for p in range(TILES) for h in range(U)]
    N = len(items)
    width = [(i + 1) * P for _, i in tiles]
    chunks = [-(-w // BANK) for w in width]
    first_chunk, n_chunks = [], 0
    for p, h in items:
        first_chunk.append(n_chunks)
        n_chunks += chunks[p]
    through = [U * sum(chunks[:p + 1]) // 2 for p in range(TILES)]
    INVERT, CONTEXT, COPY, NORMALISE = 2, 3, U + 3, U + 4
    with core.scope() as s:
        Qs = [s.sbuf(f"Qs{i}", [P, q_orders, U, S], F16) for i in range(2)]
        Ks = [s.sbuf(f"Ks{i}", [P, k_heads, S], F16) for i in range(2)]
        Vs = [s.sbuf(f"Vs{i}", [P, TPB, U, HW], F32) for i in range(2)]
        prob = [s.sbuf(f"prob{i}", [P, S], F32) for i in range(2)]
        probT = [s.sbuf(f"probT{i}", [P, U, S], F32) for i in range(2)]
        negmax = s.sbuf("negmax", [P, 4], F32)
        total = s.sbuf("total", [P, 4, U], F32)
        inv = s.sbuf("inv", [P, 2, U], F32)
        inv_b = [s.sbuf(f"inv_b{i}", [P, U, HW], F32) for i in range(2)]
        inv_row = [s.sbuf(f"inv_row{i}", [P, P], F32) for i in range(2)]
        score = [s.psum(f"score{i}", [P, S]) for i in range(2)]
        probT_ps = [s.psum(f"probT_ps{i}", [P, BANK]) for i in range(2)]
        ctx_ps = [s.psum(f"ctx_ps{i}", [P, 4, P]) for i in range(2)]
        staged = [s.sem(f"staged{i}") for i in range(2)]
        (scored, maxed, exped, t_done, inv_made, inv_ready, inv_copied, pv_done, ctx_done) = (
            s.sem(n) for n in ("scored", "maxed", "exped", "t_done", "inv_made", "inv_ready", "inv_copied",
                               "pv_done", "ctx_done"))
        evac = [s.sem(f"evac{i}") for i in range(2)]
        block = s.block()
        DMAS = (1 if q_orders == 1 else 3) + 2

        def steps(n, it, item_tasks, tile_tasks):
            for lag, task in item_tasks:
                m = n - lag
                if 0 <= m < N:
                    task(it, m)
                elif m < 0 and it is not FIRST:
                    task(it - 1, m + N)
            for lag, task in tile_tasks:
                m, turn = n - lag + 1, it
                if m < U:
                    if it is FIRST:
                        continue
                    m, turn = m + N, it - 1
                p, rest = divmod(m, U)
                if p <= TILES and (rest == 0 or task.__name__ == "context"):
                    task(turn, p - 1, *([rest] if task.__name__ == "context" else []))

        def turns(eng, item_tasks, tile_tasks):
            for n in range(N):
                steps(n, FIRST, item_tasks, tile_tasks)
            with eng.Fori(1, LOOPS, 1) as it:
                for n in range(N):
                    steps(n, it, item_tasks, tile_tasks)
            for n in range(N, N + NORMALISE + 1):
                steps(n, LOOPS - 1, item_tasks, tile_tasks)

        @block.sync
        def _(sp):
            def load(u, a):
                heads = bass.ds(u * U, U)
                sp.dma_start(Qs[a][:, 0], Qp[:, heads, :]).then_inc(staged[a], 16)
                if q_orders == 2:
                    sp.dma_start(Qs[a][0:HD0, 1], Qp[HD0:P, heads, :]).then_inc(staged[a], 16)
                    sp.dma_start(Qs[a][HD0:P, 1], Qp[0:HD0, heads, :]).then_inc(staged[a], 16)
                sp.dma_start(Ks[a][:], Kp[:, bass.ds(u * k_heads, k_heads), :]).then_inc(staged[a], 16)
                sp.dma_start(Vs[a][:].rearrange("p t h d -> p t (h d)"), V[:, :, bass.ds(u * P, P)]).then_inc(staged[a], 16)
            load(0, 0)
            load(1, 1)
            with sp.Fori(0, LOOPS - 1, 1) as it:
                for a in range(2):
                    sp.wait_ge(ctx_done, (2 * it + a + 1) * TPB + 2)
                    load(2 * it + a + 2, a)

        @block.tensor
        def _(pe):
            def scores(it, n):
                p, h = items[n]
                a, i = tiles[p]
                if n % (N // 2) == 0:
                    pe.wait_ge(staged[a], (it + 1) * (16 * DMAS))
                pe.wait_ge(exped, it * N + n + 1)
                out = score[n % 2]
                for order in range(q_orders):
                    for k0 in range(0, width[p], BANK):
                        k1 = min(k0 + BANK, width[p])
                        pe.matmul(out[:, k0:k1], Qs[a][:, order, h, i * P:(i + 1) * P],
                                  Ks[a][:, h if k_heads > 1 else 0, k0:k1], start=(order == 0),
                                  stop=(order == q_orders - 1 and k1 < width[p]))
                pe.matmul(out[:, i * P:width[p]], c.identb[:], c.causal[:], start=False,
                          stop=True).then_inc(scored, 1)

            def turn(it, n):
                p, h = items[n]
                pe.wait_ge(exped, it * N + n + 1 + 2)
                for k in range(chunks[p]):
                    m = first_chunk[n] + k
                    pe.wait_ge(evac[m % 2], it * (n_chunks // 2) + m // 2 + 1)
                    for j in range(4 * k, min(4 * k + 4, tiles[p][1] + 1)):
                        last = pe.transpose(probT_ps[m % 2][:, (j % 4) * P:(j % 4 + 1) * P],
                                            prob[n % 2][:, j * P:(j + 1) * P], c.identf[:])
                    last.then_inc(t_done, 1)

            def context(it, p, slice_no):
                a, i = tiles[p]
                if slice_no == 0:
                    pe.wait_ge(ctx_done, it * TILES + p + 1)
                    pe.wait_ge(inv_ready, it * TILES + p + 1)
                    pe.matmul(ctx_ps[p % 2][:, 1, :], inv_b[p % 2][:].rearrange("p h d -> p (h d)"), c.identf[:],
                              start=True, stop=True)
                    for e in range(2):
                        pe.wait_ge(evac[e], it * (n_chunks // 2) + through[p] + 1)
                for j in range((i + 1) * slice_no // U, (i + 1) * (slice_no + 1) // U):
                    for h in range(U):
                        last = pe.matmul(ctx_ps[p % 2][h * HW:(h + 1) * HW, 0, :], Vs[a][:, j, h, :],
                                         probT[p % 2][:, h, j * P:(j + 1) * P], start=(j == 0), stop=(j == i))
                if slice_no == U - 1:
                    last.then_inc(pv_done, 1)

            turns(pe, ((0, scores), (2, turn)), ((CONTEXT, context),))

        def evacuate(eng, copy, it, n, e):
            p, h = items[n]
            for k in range(chunks[p]):
                m = first_chunk[n] + k
                if m % 2 == e:
                    eng.wait_ge(t_done, it * n_chunks + m + 1 + 4)
                    eng.wait_ge(pv_done, it * TILES + p + 1)
                    w = min(BANK, width[p] - k * BANK)
                    copy(probT[p % 2][:, h, k * BANK:k * BANK + w], probT_ps[e][:, 0:w]).then_inc(evac[e], 1)

        @block.vector
        def _(dve):
            dve.sem_inc(evac[0], 1)
            dve.sem_inc(ctx_done, 2)
            dve.sem_inc(pv_done, 2)
            def row_max(it, n):
                p, h = items[n]
                dve.wait_ge(scored, it * N + n + 1)
                dve.tensor_reduce(negmax[:, n % 4:n % 4 + 1], score[n % 2][:, 0:width[p]], AX_X, ALU.max,
                                  negate=True).then_inc(maxed, 1)

            def invert(it, p):
                dve.wait_ge(exped, it * N + (p + 1) * U + 2)
                dve.wait_ge(pv_done, it * TILES + p + 1)
                dve.reciprocal(inv[:, p % 2, :], total[:, p % 4, :]).then_inc(inv_made, 1)
                dve.wait_ge(inv_made, it * TILES + p + 1)
                dve.tensor_copy(inv_b[p % 2][:], inv[:, p % 2, :].unsqueeze(2).broadcast_to([P, U, HW]))\
                   .then_inc(inv_ready, 1)

            def normalise(it, p):
                a, i = tiles[p]
                dve.wait_ge(inv_copied, it * TILES + p + 1 + 2)
                dve.tensor_tensor(ctxT[:, 2 * it + a, i * P:(i + 1) * P], ctx_ps[p % 2][:, 0, :],
                                  inv_row[p % 2][:], ALU.mult).then_inc(ctx_done, 1)

            turns(dve, ((0, row_max), (2, lambda it, n: evacuate(dve, dve.tensor_copy, it, n, 0))),
                  ((INVERT, invert), (NORMALISE, normalise)))

        @block.scalar
        def _(act):
            act.sem_inc(exped, 2)
            act.sem_inc(evac[1], 1)
            act.sem_inc(t_done, 4)
            act.sem_inc(inv_copied, 2)
            def exponentials(it, n):
                p, h = items[n]
                act.wait_ge(maxed, it * N + n + 1)
                before = first_chunk[n - 1] if n else n_chunks - chunks[-1]
                act.wait_ge(t_done, (it * n_chunks + before + 4) if n else (it * n_chunks + 4 - chunks[-1]))
                act.activation(prob[n % 2][:, 0:width[p]], score[n % 2][:, 0:width[p]], ACT.Exp,
                               bias=negmax[:, n % 4:n % 4 + 1], accum_out=total[:, p % 4, h:h + 1])\
                   .then_inc(exped, 1)

            def copy_row(it, p):
                act.wait_ge(pv_done, it * TILES + p + 1 + 2)
                act.wait_ge(ctx_done, it * TILES + p + 1)
                act.copy(inv_row[p % 2][:], ctx_ps[p % 2][:, 1, :]).then_inc(inv_copied, 1)

            turns(act, ((1, exponentials), (2, lambda it, n: evacuate(act, act.copy, it, n, 1))),
                  ((COPY, copy_row),))


def project_out(core, c, b, layer, units, ctxT, wo):
    HALF = S // BANK
    with core.scope() as s:
        y = [s.sbuf(f"y{i}", [P, BANK], F32) for i in range(HALF)]
        y_ps = [s.psum(f"y_ps{i}", [P, BANK]) for i in range(HALF)]
        yT = [s.psum(f"yT{i}", [P, BANK]) for i in range(HALF)]
        summed, gated, turned = (s.sem(n) for n in ("summed", "gated", "turned"))
        block = s.block()

        @block.tensor
        def _(pe):
            for half in range(HALF):
                for u in range(units):
                    last = pe.matmul(y_ps[half][:], wo[:, u, :], ctxT[:, u, half * BANK:(half + 1) * BANK],
                                     start=(u == 0), stop=(u == units - 1))
                last.then_inc(summed, 1)
            for half in range(HALF):
                pe.wait_ge(gated, half + 1)
                for k in range(BANK // P):
                    last = pe.transpose(yT[half][:, k * P:(k + 1) * P], y[half][:, k * P:(k + 1) * P], c.identf[:])
                last.then_inc(turned, 1)

        @block.scalar
        def _(act):
            for half in range(HALF):
                act.wait_ge(summed, half + 1)
                act.activation(y[half][:], y_ps[half][:], ACT.Copy, scale=c.mod[layer][:, GA, b:b + 1])\
                   .then_inc(gated, 1)

        @block.vector
        def _(dve):
            for half in range(HALF):
                dve.wait_ge(turned, half + 1)
                t0 = b * TPB + half * (BANK // P)
                xs = c.x[:, t0:t0 + BANK // P, :].rearrange("p t d -> p (t d)")
                dve.tensor_tensor(xs, yT[half][:], xs, ALU.add)


SLOT_TILES = NT + NE


class Routing:

    def __init__(self, core, s):
        self.slot = s.sbuf("slot", [P, NT], mybir.dt.uint32)
        self.expert = s.sbuf("expert", [P, SLOT_TILES], mybir.dt.int32)
        self.h = s.sbuf("h", [P, NT, D], F32)
        nc = core.nc
        self.x_sorted = nc.dram_tensor("x_sorted", [SLOT_TILES * P, D], F32).ap()
        self.y_sorted = nc.dram_tensor("y_sorted", [SLOT_TILES * P, D], F32).ap()


class Shared:

    def __init__(self, s):
        self.up = s.sbuf("shared_up", [P, FF], F32)
        self.up2 = s.sbuf("shared_up2", [P, FF], F32)
        self.down = s.sbuf("shared_down", [P, FC, D], F32)


def route_top1(core, c, ins, r, zeros, w):
    with core.scope() as s:
        wg = s.sbuf("wg", [P, NE], F32)
        best = s.sbuf("best", [P, NT], F32)
        place = s.sbuf("place", [P, NE], F32)
        steps_k = s.sbuf("steps_k", [P, NT], F32)
        tile_no = s.sbuf("tile_no", [P, SLOT_TILES], F32)
        ones = s.sbuf("ones", [P, P], F32)
        before = s.sbuf("before", [P, P], F32)
        hit = s.sbuf("hit", [P, NT, NE], F32)
        mask = s.sbuf("mask", [P, NE, NT], F32)
        same = s.sbuf("same", [P, NE, NT], F32)
        upto = s.sbuf("upto", [P, NE, NT], F32)
        earlier = s.sbuf("earlier", [P, NE, NT], F32)
        tiles = s.sbuf("tiles", [P, NE], F32)
        end = s.sbuf("end", [P, NE], F32)
        start = s.sbuf("start", [P, NE], F32)
        past = s.sbuf("past", [P, SLOT_TILES, NE], F32)
        owner = s.sbuf("owner", [P, SLOT_TILES], F32)
        slot_f = s.sbuf("slot_f", [P, NT], F32)
        logits = s.psum("logits", [P, NT * 4, NE])
        rank = s.psum("rank", [P, BANK])
        count = s.psum("count", [P, BANK])
        hx = [s.psum(f"hx{i}", [P, BANK]) for i in range(4)]
        loaded, placed, zeroed, scored, step, ranked, turned = (
            s.sem(n) for n in ("loaded", "placed", "zeroed", "scored", "step", "ranked", "turned"))
        block = s.block()

        @block.sync
        def _(sp):
            sp.dma_start(wg[:], ins["L0_ffn_Wg"]).then_inc(loaded, 16)
            for t0 in range(0, SLOT_TILES, NE):
                sp.dma_start(r.x_sorted[t0 * P:(t0 + NE) * P, :].rearrange("(t p) d -> p t d", p=P),
                             zeros[:, 0:NE, :]).then_inc(zeroed, 16)
            sp.dma_start(w.up[:], ins["L0_ffn_w1s"]).then_inc(zeroed, 16)
            sp.dma_start(w.up2[:], ins["L0_ffn_w2s"]).then_inc(zeroed, 16)
            sp.dma_start(w.down[:], ins["L0_ffn_w3s"].rearrange("(f p) d -> p f d", p=P)).then_inc(zeroed, 16)
            sp.wait_ge(zeroed, 16 * (SLOT_TILES // NE + 3))

        @block.gpsimd
        def _(pool):
            pool.iota(place[:], pattern=[[-1, NE]], base=NE, channel_multiplier=0,
                      allow_small_or_imprecise_dtypes=True)
            pool.iota(steps_k[:], pattern=[[P, NT]], base=0, channel_multiplier=0,
                      allow_small_or_imprecise_dtypes=True)
            pool.iota(tile_no[:], pattern=[[1, SLOT_TILES]], base=0, channel_multiplier=0,
                      allow_small_or_imprecise_dtypes=True)
            pool.memset(ones[:], 1.0).then_inc(placed, 1)
            pool.wait_ge(placed, 1)
            pool.affine_select(out=before[:], in_=ones[:], compare_op=ALU.is_gt, fill=0.0, base=0,
                               pattern=[[1, P]], channel_multiplier=-1).then_inc(placed, 1)

        @block.tensor
        def _(pe):
            pe.wait_ge(loaded, 16)
            for t in range(NT):
                last = pe.matmul(logits[:, t, :], c.hT[:, t * P:(t + 1) * P], wg[:], start=True, stop=True)
            last.then_inc(scored, 1)
            for t in range(NT):
                last = pe.transpose(hx[t // 4][:, (t % 4) * P:(t % 4 + 1) * P], c.hT[:, t * P:(t + 1) * P], c.identf[:])
            last.then_inc(turned, 1)
            pe.wait_ge(placed, 2)
            pe.wait_ge(ranked, 1)
            pe.matmul(rank[:, 0:NE * NT], before[:], mask[:].rearrange("p e t -> p (e t)"), start=True, stop=False)
            pe.matmul(rank[:, 0:NE * NT], ones[:], earlier[:].rearrange("p e t -> p (e t)"), start=False, stop=True)
            pe.matmul(count[:, 0:NE], ones[:], upto[:, :, NT - 1], start=True, stop=True).then_inc(ranked, 1)

        @block.scalar
        def _(act):
            act.wait_ge(turned, 1)
            for q in range(4):
                act.copy(r.h[:, 4 * q:4 * q + 4, :].rearrange("p t d -> p (t d)"), hx[q][:])

        @block.vector
        def _(dve):
            count_steps = [0]

            def link(instruction):
                count_steps[0] += 1
                instruction.then_inc(step, 1)
                dve.wait_ge(step, count_steps[0])

            def wide(v):
                return v.unsqueeze(2).broadcast_to([P, NT, NE])
            lg = logits[:, 0:NT, :]
            dve.memset(same[:], 1.0)
            dve.wait_ge(scored, 1)
            link(dve.tensor_reduce(best[:], lg, AX_X, ALU.max))
            dve.memset(same[:, :, 0:1], 0.0)
            link(dve.tensor_tensor(hit[:], lg, wide(best[:]), ALU.is_ge))
            dve.wait_ge(placed, 1)
            link(dve.tensor_tensor(hit[:], hit[:], place[:].unsqueeze(1).broadcast_to([P, NT, NE]), ALU.mult))
            link(dve.tensor_reduce(best[:], hit[:], AX_X, ALU.max))
            link(dve.tensor_tensor(mask[:].rearrange("p e t -> p t e"), hit[:], wide(best[:]), ALU.is_equal))
            flat = [v[:].rearrange("p e t -> p (e t)") for v in (same, mask, upto, earlier)]
            link(dve.tensor_tensor_scan(flat[2], flat[0], flat[1], 0.0, ALU.mult, ALU.add))
            dve.tensor_tensor(flat[3], flat[2], flat[1], ALU.subtract).then_inc(ranked, 1)
            dve.wait_ge(ranked, 2)
            link(dve.tensor_tensor(upto[:], count[:, 0:NE].unsqueeze(2).broadcast_to([P, NE, NT]),
                                   steps_k[:].unsqueeze(1).broadcast_to([P, NE, NT]), ALU.is_gt))
            link(dve.tensor_reduce(tiles[:], upto[:], AX_X, ALU.add))
            link(dve.tensor_tensor_scan(end[:], ones[:, 0:NE], tiles[:], 0.0, ALU.mult, ALU.add))
            link(dve.tensor_tensor(start[:], end[:], tiles[:], ALU.subtract))
            link(dve.tensor_scalar(start[:], start[:], float(P), None, ALU.mult))
            link(dve.tensor_tensor(upto[:], rank[:, 0:NE * NT].rearrange("p (e t) -> p e t", e=NE),
                                   start[:].unsqueeze(2).broadcast_to([P, NE, NT]), ALU.add))
            link(dve.tensor_tensor(upto[:], upto[:], mask[:], ALU.mult))
            link(dve.tensor_reduce(slot_f[:], upto[:].rearrange("p e t -> p t e"), AX_X, ALU.add))
            dve.tensor_copy(r.slot[:], slot_f[:])
            link(dve.tensor_tensor(past[:], tile_no[:].unsqueeze(2).broadcast_to([P, SLOT_TILES, NE]),
                                   end[:].unsqueeze(1).broadcast_to([P, SLOT_TILES, NE]), ALU.is_ge))
            link(dve.tensor_reduce(owner[:], past[:], AX_X, ALU.add))
            link(dve.tensor_scalar(owner[:], owner[:], float(NE - 1), None, ALU.min))
            dve.tensor_copy(r.expert[:], owner[:])


def scatter_tokens(pool, r, sent):
    for t in range(NT):
        pool.indirect_dma_start(out=r.x_sorted, out_offset=bass.IndirectOffsetOnAxis(ap=r.slot[:, t:t + 1], axis=0),
                                in_=r.h[:, t, :], in_offset=None).then_inc(sent[t // 4], 16)
    for q in range(4):
        pool.wait_ge(sent[q], 16 * 4)


def gather_tokens(pool, r, sent):
    for t in range(NT):
        pool.indirect_dma_start(out=r.h[:, t, :], out_offset=None, in_=r.y_sorted,
                                in_offset=bass.IndirectOffsetOnAxis(ap=r.slot[:, t:t + 1], axis=0))\
            .then_inc(sent[t // 4], 16)


def finish_tokens(dve, c, r, step, sent, q, shared):
    part = slice(4 * q, 4 * q + 4)
    gate = c.gate_b[0][:, 4 * q // TPB, :].unsqueeze(1).broadcast_to([P, 4, D])
    dve.wait_ge(sent[q], 16 * 4)
    dve.tensor_tensor(r.h[:, part, :], shared, r.h[:, part, :], ALU.add).then_inc(step, 1)
    dve.wait_ge(step, 2 * q + 1)
    dve.tensor_tensor(r.h[:, part, :], r.h[:, part, :], gate, ALU.mult).then_inc(step, 1)
    dve.wait_ge(step, 2 * q + 2)
    dve.tensor_tensor(c.x[:, part, :], c.x[:, part, :], r.h[:, part, :], ALU.add)


def sorted_experts(core, c, up, up2, down, r):
    AHEAD = 4
    LOOPS = SLOT_TILES // AHEAD
    with core.scope() as s:
        def ring(name, shape, n=2):
            return [s.sbuf(f"{name}{i}", shape, F32) for i in range(n)]
        x_in, w_up, w_up2, w_down = (ring(n, shape, AHEAD) for n, shape in
                                     (("x_in", [P, D]), ("w_up", [P, FF]), ("w_up2", [P, FF]), ("w_down", [P, FC, D])))
        xT, y_out, gelu, hidden = (ring(n, shape) for n, shape in
                                   (("xT", [P, P]), ("y_out", [P, D]), ("gelu", [P, FC, P]), ("hidden", [P, FC, P])))
        xT_ps, u_ps, u2_ps, y_ps = ([s.psum(f"{n}{i}", [P, FC, P]) for i in range(2)]
                                    for n in ("xT_ps", "u_ps", "u2_ps", "y_ps"))
        x_staged, w_staged = ([s.sem(f"{n}{i}") for i in range(AHEAD)] for n in ("x_staged", "w_staged"))
        stored = [s.sem(f"stored{i}") for i in range(2)]
        x_turned, x_ready, upped, gelued, hidden_ready, y_ready, y_copied = (
            s.sem(n) for n in ("x_turned", "x_ready", "upped", "gelued", "hidden_ready", "y_ready", "y_copied"))
        block = s.block()

        def ring_of(it, k):
            return AHEAD * it + k, k % AHEAD, it + k // AHEAD

        @block.sync
        def _(sp):
            def load(it, k):
                t, a, _ = ring_of(it, k)
                sp.dma_start(x_in[a][:], r.x_sorted[bass.ds(t * P, P), :]).then_inc(x_staged[a], 16)
                e = sp.value_load(r.expert[0:1, bass.ds(t, 1)], min_val=0, max_val=NE - 1)
                sp.dma_start(w_up[a][:], up(e)).then_inc(w_staged[a], 16)
                sp.dma_start(w_up2[a][:], up2(e)).then_inc(w_staged[a], 16)
                sp.dma_start(w_down[a][:], down(e)).then_inc(w_staged[a], 16)

            for k in range(AHEAD):
                load(0, k)
            with sp.Fori(0, LOOPS - 1, 1) as it:
                for k in range(AHEAD):
                    sp.wait_ge(y_ready, AHEAD * it + k + 1)
                    load(it, k + AHEAD)

        @block.tensor
        def _(pe):
            def turn(it, k):
                t, a, turns = ring_of(it, k)
                pe.wait_ge(x_staged[a], (turns + 1) * 16)
                pe.wait_ge(x_ready, t + 1)
                pe.transpose(xT_ps[a % 2][:, 0, :], x_in[a][:], c.identf[:]).then_inc(x_turned, 1)

            def inner(it, k):
                t, a, turns = ring_of(it, k)
                pe.wait_ge(w_staged[a], (turns + 1) * 48)
                pe.wait_ge(x_ready, t + 1 + 2)
                pe.wait_ge(hidden_ready, t + 1)
                for out, w in ((u_ps, w_up), (u2_ps, w_up2)):
                    for f in range(FC):
                        last = pe.matmul(out[a % 2][:, f, :], w[a][:, f * P:(f + 1) * P], xT[a % 2][:],
                                         start=True, stop=True)
                    last.then_inc(upped, 1)

            def outer(it, k):
                t, a, _ = ring_of(it, k)
                pe.wait_ge(hidden_ready, t + 1 + 2)
                pe.wait_ge(y_copied, t + 1)
                for f in range(FC):
                    last = pe.matmul(y_ps[a % 2][:, 0, :], hidden[a % 2][:, f, :], w_down[a][:, f, :],
                                     start=(f == 0), stop=(f == FC - 1))
                last.then_inc(y_ready, 1)

            turn(0, 0)
            inner(0, 0)
            turn(0, 1)
            with pe.Fori(0, LOOPS - 1, 1) as it:
                for k in range(AHEAD):
                    inner(it, k + 1)
                    turn(it, k + 2)
                    outer(it, k)
            for k in range(AHEAD):
                if k + 1 < AHEAD:
                    inner(LOOPS - 1, k + 1)
                if k + 2 < AHEAD:
                    turn(LOOPS - 1, k + 2)
                outer(LOOPS - 1, k)

        @block.scalar
        def _(act):
            def activate(it, k):
                t, a, _ = ring_of(it, k)
                act.wait_ge(upped, 2 * t + 1)
                act.wait_ge(hidden_ready, t + 1)
                act.activation(gelu[a % 2][:], u_ps[a % 2][:], ACT.Gelu).then_inc(gelued, 1)

            def store(it, k):
                t, a, _ = ring_of(it, k)
                act.wait_ge(y_copied, t + 1 + 2)
                act.dma_start(r.y_sorted[bass.ds(t * P, P), :], y_out[a % 2][:]).then_inc(stored[a % 2], 16)

            activate(0, 0)
            activate(0, 1)
            with act.Fori(0, LOOPS - 1, 1) as it:
                for k in range(AHEAD):
                    activate(it, k + 2)
                    store(it, k)
            for k in range(AHEAD):
                if k + 2 < AHEAD:
                    activate(LOOPS - 1, k + 2)
                store(LOOPS - 1, k)
            for i in range(2):
                act.wait_ge(stored[i], 16 + SLOT_TILES // 2 * 16)

        @block.vector
        def _(dve):
            dve.sem_inc(x_ready, 2)
            dve.sem_inc(hidden_ready, 2)
            dve.sem_inc(y_copied, 2)
            for i in range(2):
                dve.sem_inc(stored[i], 16)

            def x_copy(it, k):
                t, a, _ = ring_of(it, k)
                dve.wait_ge(x_turned, t + 1)
                dve.tensor_copy(xT[a % 2][:], xT_ps[a % 2][:, 0, :]).then_inc(x_ready, 1)

            def hide(it, k):
                t, a, _ = ring_of(it, k)
                dve.wait_ge(gelued, t + 1)
                dve.wait_ge(upped, 2 * t + 2)
                dve.tensor_tensor(hidden[a % 2][:], u2_ps[a % 2][:], gelu[a % 2][:], ALU.mult).then_inc(hidden_ready, 1)

            def y_copy(it, k):
                t, a, _ = ring_of(it, k)
                dve.wait_ge(y_ready, t + 1)
                dve.wait_ge(stored[a % 2], (2 * it + k // 2 + 1) * 16)
                dve.tensor_copy(y_out[a % 2][:], y_ps[a % 2][:, 0, :]).then_inc(y_copied, 1)

            x_copy(0, 0)
            hide(0, 0)
            x_copy(0, 1)
            with dve.Fori(0, LOOPS - 1, 1) as it:
                for k in range(AHEAD):
                    hide(it, k + 1)
                    x_copy(it, k + 2)
                    y_copy(it, k)
            for k in range(AHEAD):
                if k + 1 < AHEAD:
                    hide(LOOPS - 1, k + 1)
                if k + 2 < AHEAD:
                    x_copy(LOOPS - 1, k + 2)
                y_copy(LOOPS - 1, k)


def shared_expert(core, c, w, first, acc, meanwhile, finish=None):
    CHUNKS = NT * P // BANK // 2
    TPC = BANK // P
    with core.scope() as s:
        gelu = [s.sbuf(f"gelu{i}", [P, BANK], F32) for i in range(2)]
        hidden = [s.sbuf(f"hidden{i}", [P, FC, BANK], F32) for i in range(2)]
        u_ps = [s.psum(f"u_ps{i}", [P, BANK]) for i in range(2)]
        u2_ps = [s.psum(f"u2_ps{i}", [P, BANK]) for i in range(2)]
        y_ps = [s.psum(f"y_ps{i}", [P, TPC, D]) for i in range(2)]
        upped, gelued, multiplied, y_ready, step = (
            s.sem(n) for n in ("upped", "gelued", "multiplied", "y_ready", "step"))
        sent = [s.gpsimd_dma_sem(f"sent{q}") for q in range(4)]
        block = s.block()

        @block.gpsimd
        def _(pool):
            meanwhile(pool, sent)

        @block.tensor
        def _(pe):
            def down_product(ch):
                pe.wait_ge(multiplied, (ch + 1) * FC)
                for t in range(TPC):
                    for f in range(FC):
                        last = pe.matmul(y_ps[ch][:, t, :], hidden[ch][:, f, t * P:(t + 1) * P],
                                         w.down[:, f, :], start=(f == 0), stop=(f == FC - 1))
                last.then_inc(y_ready, 1)

            for ch in range(CHUNKS):
                rhs = c.hT[:, (first + ch) * BANK:(first + ch + 1) * BANK]
                for f in range(FC):
                    k = ch * FC + f
                    if k >= 2:
                        pe.wait_ge(gelued, k - 1)
                    pe.matmul(u_ps[f % 2][:], w.up[:, f * P:(f + 1) * P], rhs, start=True, stop=True).then_inc(upped, 1)
                    if k >= 2:
                        pe.wait_ge(multiplied, k - 1)
                    pe.matmul(u2_ps[f % 2][:], w.up2[:, f * P:(f + 1) * P], rhs, start=True, stop=True).then_inc(upped, 1)
                    if f == 1 and ch >= 1:
                        down_product(ch - 1)
            down_product(CHUNKS - 1)

        @block.scalar
        def _(act):
            for k in range(CHUNKS * FC):
                act.wait_ge(upped, 2 * k + 1)
                if k >= 2:
                    act.wait_ge(multiplied, k - 1)
                act.activation(gelu[k % 2][:], u_ps[k % 2][:], ACT.Gelu).then_inc(gelued, 1)

        @block.vector
        def _(dve):
            for ch in range(CHUNKS):
                for f in range(FC):
                    k = ch * FC + f
                    dve.wait_ge(gelued, k + 1)
                    dve.wait_ge(upped, 2 * k + 2)
                    dve.tensor_tensor(hidden[ch][:, f, :], u2_ps[f % 2][:], gelu[f % 2][:], ALU.mult).then_inc(multiplied, 1)
            if finish is not None:
                for q in range(first):
                    finish(dve, step, sent, q, acc[:, q * TPC:(q + 1) * TPC, :])
            for ch in range(CHUNKS):
                dve.wait_ge(y_ready, ch + 1)
                if finish is not None:
                    finish(dve, step, sent, first + ch, y_ps[ch][:])
                else:
                    dve.tensor_copy(acc[:, (first + ch) * TPC:(first + ch + 1) * TPC, :], y_ps[ch][:])


def norm_and_weights(core, c, ins, wqkv, wo, Qp, V):
    RANK = 16
    with core.scope() as s:
        a_qkv = s.sbuf("a_qkv", [RANK, 3, D], F32)
        b_qkv = s.sbuf("b_qkv", [RANK, 3, D], F32)
        a_o = s.sbuf("a_o", [RANK, 4, P], F32)
        b_o = s.sbuf("b_o", [RANK, D], F32)
        low_qkv = s.psum("low_qkv", [P, 3, D])
        low_o = s.psum("low_o", [P, 4, D])
        loaded, product = s.sem("loaded"), s.sem("product")
        buffers = norm_buffers(s)
        block = s.block()
        norm(block, buffers, c, 1, SA, CA)

        @block.gpsimd
        def _(pool):
            pool.memset(V[:], 0.0)
            pool.memset(Qp[:].bitcast(F32), 0.0)
        loads = ((a_qkv, "a_qkv"), (b_qkv, "b_qkv"), (a_o, "a_o"), (b_o, "b_o"), (wqkv, "w_qkv"), (wo, "w_o"))

        @block.sync
        def _(sp):
            for buffer, name in loads:
                sp.dma_start(buffer[:], ins["lora_" + name]).then_inc(loaded, 16)

        @block.tensor
        def _(pe):
            pe.wait_ge(loaded, 16 * len(loads))
            for j in range(3):
                last = pe.matmul(low_qkv[:, j, :], a_qkv[:, j, :], b_qkv[:, j, :], start=True, stop=True)
            last.then_inc(product, 1)
            for g in range(4):
                last = pe.matmul(low_o[:, g, :], a_o[:, g, :], b_o[:], start=True, stop=True)
            last.then_inc(product, 1)

        @block.vector
        def _(dve):
            dve.wait_ge(loaded, 16 * len(loads))
            dve.wait_ge(product, 2)
            dve.scalar_tensor_tensor(out=wqkv[:], in0=low_qkv[:], scalar=1.0 / RANK, in1=wqkv[:],
                                     op0=ALU.mult, op1=ALU.add)
            dve.scalar_tensor_tensor(out=wo[:], in0=low_o[:], scalar=1.0 / RANK, in1=wo[:],
                                     op0=ALU.mult, op1=ALU.add)


def project_narrow(core, c, b, wqkv, Qp, Kp, V):
    G = 4
    LOOPS = TPB // 2
    with core.scope() as s:
        h_tile = [s.sbuf(f"h_tile{i}", [P, P], F32) for i in range(2)]
        qk = [s.sbuf(f"qk{i}", [P, 2, H, HD1], F32) for i in range(2)]
        parts = [s.sbuf(f"parts{i}", [P, 2, H, 2, 2, HD1], F16) for i in range(2)]
        proj = [s.psum(f"proj{i}", [P, 3 * D]) for i in range(2)]
        partsT = [[s.psum(f"partsT{i}{j}", [P, 2, G, P], F16) for j in range(2)] for i in range(2)]
        h_ready, projected, copied, hi_done, lo_done, t_done, q_read, k_read = (
            s.sem(n) for n in ("h_ready", "projected", "copied", "hi_done", "lo_done", "t_done", "q_read", "k_read"))
        block = s.block()

        def slots(a, which):
            v = parts[a][:, which]
            return (v[:, :, :, 0, :], v[:, :, :, 1, :]) if which == 0 else (v[:, :, 0, :, :], v[:, :, 1, :, :])

        @block.tensor
        def _(pe):
            def project(it):
                for a in range(2):
                    pe.wait_ge(h_ready, 2 * it + a + 1)
                    pe.wait_ge(copied, 2 * it + a + 1)
                    pe.matmul(proj[a][:], h_tile[a][:], wqkv[:].rearrange("p j d -> p (j d)"),
                              start=True, stop=True).then_inc(projected, 1)

            def turn(it):
                for a in range(2):
                    pe.wait_ge(lo_done, 2 * it + a + 1 + 2)
                    pe.wait_ge(q_read, 2 * it + a + 1)
                    pe.wait_ge(k_read, 2 * it + a + 1)
                    for which in range(2):
                        for g in range(G):
                            last = pe.transpose(partsT[a][which][:, 0, g, :],
                                                parts[a][:, which, g * G:(g + 1) * G].rearrange("p h a b d -> p (h a b d)"),
                                                c.identh[:])
                    last.then_inc(t_done, 1)

            project(0)
            with pe.Fori(0, LOOPS - 1, 1) as it:
                project(it + 1)
                turn(it)
            turn(LOOPS - 1)

        @block.scalar
        def _(act):
            act.sem_inc(copied, 2)
            act.sem_inc(k_read, 2)

            def take_h(it):
                for a in range(2):
                    act.wait_ge(projected, 2 * it + a + 1)
                    act.copy(h_tile[a][:], c.hT[:, bass.ds((2 * it + a) * P + b * S, P)]).then_inc(h_ready, 1)

            def take_qkv(it):
                for a in range(2):
                    act.wait_ge(projected, 2 * it + a + 1 + 2)
                    act.wait_ge(lo_done, 2 * it + a + 1)
                    q, k, v = (proj[a][:, j * D:(j + 1) * D] for j in range(3))
                    act.mul(qk[a][:, 0].rearrange("p h d -> p (h d)"), q, float(HD1) ** -0.5)
                    act.copy(qk[a][:, 1].rearrange("p h d -> p (h d)"), k)
                    act.copy(V[:, 2 * it + a, :].rearrange("p (h d) -> p h d", h=H)[:, :, 0:HD1],
                             v.rearrange("p (h d) -> p h d", h=H)).then_inc(copied, 1)

            def take_k(it):
                for a in range(2):
                    act.wait_ge(t_done, 2 * it + a + 1 + 2)
                    act.copy(Kp[:, :, bass.ds((2 * it + a) * P, P)], partsT[a][1][:, 0]).then_inc(k_read, 1)

            take_h(0)
            take_qkv(0)
            take_h(1)
            with act.Fori(0, LOOPS - 2, 1) as it:
                take_qkv(it + 1)
                take_h(it + 2)
                take_k(it)
            take_qkv(LOOPS - 1)
            take_k(LOOPS - 2)
            take_k(LOOPS - 1)

        @block.vector
        def _(dve):
            dve.sem_inc(projected, 2)
            dve.sem_inc(lo_done, 2)
            dve.sem_inc(t_done, 2)
            dve.sem_inc(q_read, 2)

            def split(it):
                for a in range(2):
                    dve.wait_ge(copied, 2 * it + a + 1 + 2)
                    dve.wait_ge(t_done, 2 * it + a + 1)
                    for which in range(2):
                        src = qk[a][:, which].unsqueeze(2).broadcast_to([P, H, 2, HD1])
                        last = dve.tensor_copy(slots(a, which)[0], src)
                    last.then_inc(hi_done, 1)
                    dve.wait_ge(hi_done, 2 * it + a + 1)
                    for which in range(2):
                        src = qk[a][:, which].unsqueeze(2).broadcast_to([P, H, 2, HD1])
                        last = dve.tensor_tensor(slots(a, which)[1], src, slots(a, which)[0], ALU.subtract)
                    last.then_inc(lo_done, 1)

            def take_q(it):
                for a in range(2):
                    dve.wait_ge(t_done, 2 * it + a + 1 + 2)
                    q_heads = Qp[:].rearrange("p (g r) s -> p g r s", r=G)
                    for r in range(G):
                        rows = slice(32 * r, 32 * r + 32)
                        last = dve.tensor_copy(q_heads[rows, :, r, bass.ds((2 * it + a) * P, P)], partsT[a][0][rows, 0])
                    last.then_inc(q_read, 1)

            split(0)
            with dve.Fori(0, LOOPS - 1, 1) as it:
                split(it + 1)
                take_q(it)
            take_q(LOOPS - 1)


class Choice:

    def __init__(self, core, s):
        self.token = s.sbuf("token", [P, B, NE, 2], mybir.dt.uint32)
        nc = core.nc
        self.rows = nc.dram_tensor("rows", [NT * P, D + NE], F32).ap()
        self.w_up = [s.sbuf(f"w_up{i}", [P, FF], F32) for i in range(RING)]
        self.w_down = [s.sbuf(f"w_down{i}", [P, FC, D], F32) for i in range(RING)]
        self.staged = [s.sem(f"staged{i}") for i in range(RING)]
        self.slots = nc.dram_tensor("slots", [B, NE, TOPK], mybir.dt.uint32).ap()


def route_experts_choice(core, c, ins, r, out):
    UNROLL = 3
    with core.scope() as s:
        I32 = mybir.dt.int32
        wg = s.sbuf("wg", [P, NE], F32)
        tables = s.sbuf("tables", [P, 2 * P + NE], F32)
        same, earlier, own = tables[:, 0:P], tables[:, P:2 * P], tables[:, 2 * P:]
        numbers = s.sbuf("numbers", [P, DIGITS + 1, 4], I32)
        sixteen = s.sbuf("sixteen", [P, A], I32)
        ids = s.sbuf("ids", [P, NT], F16)
        row = s.sbuf("row", [P, NT, D + NE], F32)
        peak = s.sbuf("peak", [P, NT], F32)
        prob = s.sbuf("prob", [P, NT, NE], F32)
        turned_prob = s.sbuf("turned_prob", [P, P], F32)
        reach = s.sbuf("reach", [P, 3, P], F32)
        counts = s.sbuf("counts", [P, 4], BF16)
        same_b = s.sbuf("same_b", [P, P], BF16)
        tried = s.sbuf("tried", [P, 4], F32)
        kept = s.sbuf("kept", [P, 4], F32)
        best = s.sbuf("best", [P, 1], F32)
        above = s.sbuf("above", [P, P], F32)
        tie = s.sbuf("tie", [P, P], F32)
        upto = s.sbuf("upto", [P, P], F32)
        ones = s.sbuf("ones", [P, P], F32)
        left = s.sbuf("left", [P, 2], F32)
        place = s.sbuf("place", [P, P], F32)
        slot, high, low = (s.sbuf(n, [P, NT * NE], I32) for n in ("slot", "high", "low"))
        hot_high, hot_low = (s.sbuf(n, [P, NT, NE, A], F16) for n in ("hot_high", "hot_low"))
        spread = s.sbuf("spread", [P, B, NE, A], F32)
        chosen_f = s.sbuf("chosen_f", [P, B, A], F32)
        chosen = s.sbuf("chosen", [P, B, A], mybir.dt.uint32)
        logits = s.psum("logits", [P, NT, NE])
        turn_ps = s.psum("turn_ps", [P, P])
        total = s.psum("total", [P, 8])
        ids_ps = s.psum("ids_ps", [P, B, NE, A])
        hx = [s.psum(f"hx{i}", [P, BANK]) for i in range(4)]
        loaded, tabled, scored, exped, step, counted, totaled, turned, rowed, stored, listed, hot, linked = (
            s.sem(n) for n in ("loaded", "tabled", "scored", "exped", "step", "counted", "totaled", "turned",
                               "rowed", "stored", "listed", "hot", "linked"))
        block = s.block()

        @block.sync
        def _(sp):
            sp.dma_start(wg[:], ins["gate_wT"]).then_inc(loaded, 16)
            sp.dma_start(numbers[:].rearrange("p n j -> p (n j)"), ins["numbers"]).then_inc(tabled, 16)
            sp.dma_start(tables[:], ins["tables"]).then_inc(tabled, 16)
            sp.dma_start(sixteen[:], ins["sixteen"]).then_inc(tabled, 16)
            sp.dma_start(ids[:], ins["ids"]).then_inc(tabled, 16)
            sp.dma_start(out.rearrange("b (t p) d -> p (b t) d", p=P), c.x[:]).then_inc(stored, 16)
            for k in range(RING):
                load_expert(sp, ins, r, k, k)
            sp.wait_ge(rowed, 5)
            sp.dma_start(r.rows.rearrange("(t p) c -> p t c", p=P), row[:]).then_inc(stored, 16)
            sp.wait_ge(listed, 1)
            sp.dma_start(r.slots.rearrange("b e (a x) -> (e a) b x", x=A), chosen[:]).then_inc(listed, 16)
            sp.wait_ge(listed, 17)
            sp.dma_start(r.token[:], r.slots.rearrange("b e (p i) -> p b e i", i=2)).then_inc(listed, 16)
            sp.wait_ge(listed, 33)
            sp.wait_ge(stored, 32)

        @block.tensor
        def _(pe):
            pe.wait_ge(loaded, 16)
            for t in range(NT):
                last = pe.matmul(logits[:, t, :], c.hT[:, t * P:(t + 1) * P], wg[:], start=True, stop=True)
            last.then_inc(scored, 1)
            for t in range(NT):
                last = pe.transpose(hx[t // 4][:, (t % 4) * P:(t % 4 + 1) * P], c.hT[:, t * P:(t + 1) * P], c.identf[:])
                if t % 4 == 3:
                    last.then_inc(scored, 1)
            pe.wait_ge(step, 5)
            pe.transpose(turn_ps[:], prob[:].rearrange("p t e -> p (t e)"), c.identf[:]).then_inc(turned, 1)
            pe.wait_ge(tabled, 64)
            with pe.Fori(0, DIGITS // UNROLL, 1) as it:
                for k in range(UNROLL):
                    pe.wait_ge(counted, UNROLL * it + k + 1)
                    pe.matmul(total[:, 0:4], same_b[:], counts[:], start=True, stop=True).then_inc(totaled, 1)
            pe.wait_ge(counted, DIGITS + 1)
            pe.matmul(total[:, 0:1], same, left[:, 0:1], start=True, stop=True)
            pe.matmul(total[:, 1:2], earlier, left[:, 1:2], start=True, stop=True).then_inc(totaled, 1)
            pe.wait_ge(counted, DIGITS + 2)
            pe.matmul(total[:, 2:3], earlier, upto[:, P - 1:P], start=True, stop=True).then_inc(totaled, 1)
            pe.wait_ge(counted, DIGITS + 3)
            pe.transpose(turn_ps[:], place[:], c.identf[:]).then_inc(turned, 1)
            pe.wait_ge(hot, 2)
            for b in range(B):
                for t in range(b * TPB, (b + 1) * TPB):
                    last = pe.matmul(ids_ps[:, b].rearrange("p e a -> p (e a)"),
                                     hot_high[:, t].rearrange("p e a -> p (e a)"),
                                     hot_low[:, t].rearrange("p e a -> p (e a)"),
                                     start=(t % TPB == 0), stop=(t % TPB == TPB - 1))
            last.then_inc(turned, 1)

        @block.scalar
        def _(act):
            act.wait_ge(step, 2)
            act.activation(prob[:], prob[:], ACT.Exp).then_inc(exped, 1)
            for q in range(4):
                act.wait_ge(scored, q + 2)
                act.copy(row[:, 4 * q:4 * q + 4, 0:D], hx[q][:].rearrange("p (t d) -> p t d", d=D)).then_inc(rowed, 1)
            act.wait_ge(step, 5)
            act.copy(row[:, :, D:D + NE], prob[:]).then_inc(rowed, 1)

        @block.gpsimd
        def _(pool):
            pool.wait_ge(tabled, 64)
            pool.wait_ge(step, 10)
            numbered = hot_low[:].rearrange("p t e a -> p t (e a)")
            pool.tensor_tensor(numbered, numbered, ids[:].unsqueeze(2).broadcast_to([P, NT, NE * A]), ALU.mult)\
                .then_inc(hot, 1)

        @block.vector
        def _(dve):
            def wide(v):
                return v.unsqueeze(2).broadcast_to([P, NT, NE])
            dve.wait_ge(scored, 1)
            dve.tensor_reduce(peak[:], logits[:], AX_X, ALU.max).then_inc(step, 1)
            dve.wait_ge(step, 1)
            dve.tensor_tensor(prob[:], logits[:], wide(peak[:]), ALU.subtract).then_inc(step, 1)
            dve.memset(ones[:], 1.0)
            dve.memset(counts[:], float(P))
            dve.wait_ge(exped, 1)
            dve.tensor_reduce(peak[:], prob[:], AX_X, ALU.add).then_inc(step, 1)
            dve.wait_ge(step, 3)
            dve.reciprocal(peak[:], peak[:]).then_inc(step, 1)
            dve.wait_ge(step, 4)
            dve.tensor_tensor(prob[:], prob[:], wide(peak[:]), ALU.mult).then_inc(step, 1)
            dve.wait_ge(tabled, 64)
            dve.tensor_copy(tried[:].bitcast(I32), numbers[:, 0, :])
            dve.tensor_copy(same_b[:], same)
            dve.wait_ge(turned, 1)
            dve.tensor_copy(turned_prob[:], turn_ps[:]).then_inc(step, 1)
            dve.wait_ge(step, 6)
            def narrow(n):
                for j in range(3):
                    last = dve.tensor_scalar(reach[:, j, :], turned_prob[:], tried[:, j:j + 1], None, ALU.is_ge, ALU.add,
                                             accum_out=counts[:, j:j + 1])
                last.then_inc(counted, 1)
                dve.wait_ge(totaled, n + 1)
                dve.scalar_tensor_tensor(out=kept[:], in0=total[:, 0:4], scalar=TOPK - 0.5, in1=tried[:],
                                         op0=ALU.is_gt, op1=ALU.mult).then_inc(linked, 1)
                dve.wait_ge(linked, 3 * n + 1)
                dve.tensor_reduce(best[:], kept[:], AX_X, ALU.max).then_inc(linked, 1)
                dve.wait_ge(linked, 3 * n + 2)
                dve.tensor_tensor(tried[:].bitcast(I32), numbers[:, bass.ds(n + 1, 1), :].rearrange("p n j -> p (n j)"),
                                  best[:].bitcast(I32).broadcast_to([P, 4]), ALU.bitwise_or).then_inc(linked, 1)
                dve.wait_ge(linked, 3 * n + 3)

            with dve.Fori(0, DIGITS // UNROLL, 1) as it:
                for k in range(UNROLL):
                    narrow(UNROLL * it + k)
            value = best[:]
            dve.tensor_scalar(above[:], turned_prob[:], value, None, ALU.is_gt, ALU.add, accum_out=left[:, 0:1])
            dve.tensor_scalar(tie[:], turned_prob[:], value, None, ALU.is_equal, ALU.add, accum_out=left[:, 1:2])\
               .then_inc(counted, 1)
            dve.wait_ge(counted, DIGITS + 1)
            dve.tensor_tensor_scan(upto[:], ones[:], tie[:], 0.0, ALU.mult, ALU.add)
            dve.wait_ge(totaled, DIGITS + 1)
            dve.tensor_scalar(left[:, 0:1], total[:, 0:1], -1.0, float(TOPK), ALU.mult, ALU.add).then_inc(linked, 1)
            dve.wait_ge(linked, 3 * DIGITS + 1)
            dve.tensor_tensor(left[:, 1:2], left[:, 0:1], total[:, 1:2], ALU.subtract).then_inc(linked, 1)
            dve.wait_ge(linked, 3 * DIGITS + 2)
            dve.scalar_tensor_tensor(out=tie[:], in0=upto[:], scalar=left[:, 1:2], in1=tie[:], op0=ALU.is_le,
                                     op1=ALU.mult).then_inc(linked, 1)
            dve.wait_ge(linked, 3 * DIGITS + 3)
            dve.tensor_tensor(above[:], above[:], tie[:], ALU.add).then_inc(linked, 1)
            dve.wait_ge(linked, 3 * DIGITS + 4)
            dve.tensor_tensor_scan(upto[:], ones[:], above[:], 0.0, ALU.mult, ALU.add).then_inc(counted, 1)
            dve.wait_ge(counted, DIGITS + 2)
            dve.wait_ge(totaled, DIGITS + 2)
            dve.scalar_tensor_tensor(out=place[:], in0=upto[:], scalar=total[:, 2:3], in1=above[:], op0=ALU.add,
                                     op1=ALU.mult).then_inc(counted, 1)
            dve.wait_ge(turned, 2)
            dve.tensor_scalar(slot[:], turn_ps[:], -1.0, None, ALU.add).then_inc(step, 1)
            dve.wait_ge(step, 7)
            dve.tensor_scalar(high[:], slot[:], A_BITS, None, ALU.arith_shift_right).then_inc(step, 1)
            dve.tensor_scalar(low[:], slot[:], A - 1, None, ALU.bitwise_and).then_inc(step, 1)
            dve.wait_ge(step, 9)
            dve.tensor_tensor(hot_low[:].rearrange("p t e a -> p (t e) a"),
                              low[:].unsqueeze(2).broadcast_to([P, NT * NE, A]),
                              sixteen[:].unsqueeze(1).broadcast_to([P, NT * NE, A]), ALU.is_equal).then_inc(step, 1)
            dve.tensor_tensor(hot_high[:].rearrange("p t e a -> p (t e) a"),
                              high[:].unsqueeze(2).broadcast_to([P, NT * NE, A]),
                              sixteen[:].unsqueeze(1).broadcast_to([P, NT * NE, A]), ALU.is_equal).then_inc(hot, 1)
            dve.wait_ge(turned, 3)
            dve.tensor_tensor(spread[:], ids_ps[:], own.unsqueeze(1).unsqueeze(3).broadcast_to([P, B, NE, A]),
                              ALU.mult).then_inc(step, 1)
            dve.wait_ge(step, 11)
            dve.tensor_reduce(chosen_f[:], spread[:].rearrange("p b e a -> p b a e"), AX_X, ALU.add).then_inc(step, 1)
            dve.wait_ge(step, 12)
            dve.tensor_copy(chosen[:], chosen_f[:]).then_inc(listed, 1)


def load_expert(sp, ins, r, e, k):
    sp.dma_start(r.w_up[k][:], ins["L1_ffn_w1"][e]).then_inc(r.staged[k], 16)
    sp.dma_start(r.w_down[k][:], ins["L1_ffn_w2"][e].rearrange("(f p) d -> p f d", p=P)).then_inc(r.staged[k], 16)


def chosen_experts(core, c, ins, r, out):
    LOOPS = NE // RING
    TILES = B * 2
    out_rows = out.rearrange("b s d -> (b s) d")
    with core.scope() as s:
        rows = [s.sbuf(f"rows{i}", [P, TILES, D + NE], F32) for i in range(RING)]
        w_up, w_down, staged = r.w_up, r.w_down, r.staged
        y_out = [s.sbuf(f"y_out{i}", [P, TILES, D], F32) for i in range(RING)]
        xT = [s.sbuf(f"xT{i}", [P, BANK], F32) for i in range(2)]
        hidden = [s.sbuf(f"hidden{i}", [P, FC, BANK], F32) for i in range(2)]
        u_ps = [s.psum(f"u_ps{i}", [P, BANK]) for i in range(FC)]
        xT_ps = [s.psum(f"xT_ps{i}", [P, BANK]) for i in range(2)]
        y_ps = [s.psum(f"y_ps{i}", [P, TILES, D]) for i in range(2)]
        gathered = [s.gpsimd_dma_sem(f"gathered{i}") for i in range(RING)]
        added = s.gpsimd_dma_sem("added")
        x_turned, x_ready, upped, gelued, y_ready, y_copied, y_free = (
            s.sem(n) for n in ("x_turned", "x_ready", "upped", "gelued", "y_ready", "y_copied", "y_free"))
        block = s.block()

        @block.sync
        def _(sp):
            with sp.Fori(0, LOOPS - 1, 1) as it:
                for k in range(RING):
                    sp.wait_ge(y_ready, RING * it + k + 1)
                    load_expert(sp, ins, r, RING * (it + 1) + k, k)

        @block.gpsimd
        def _(pool):
            def index(e, i):
                return bass.IndirectOffsetOnAxis(ap=r.token[:, i // 2, e, i % 2:i % 2 + 1], axis=0)

            def gather(e):
                if e >= RING:
                    pool.wait_ge(y_copied, e - RING + 1 + 2)
                for i in range(TILES):
                    pool.indirect_dma_start(out=rows[e % RING][:, i, :], out_offset=None, in_=r.rows,
                                            in_offset=index(e, i)).then_inc(gathered[e % RING], 16)

            for e in range(RING - 1):
                gather(e)
            for e in range(NE):
                if e + RING - 1 < NE:
                    gather(e + RING - 1)
                pool.wait_ge(y_copied, e + 1 + 2)
                if e >= 1:
                    pool.wait_ge(added, 16 * TILES * e)
                    pool.sem_inc(y_free, 1)
                for i in range(TILES):
                    pool.indirect_dma_start(out=out_rows, out_offset=index(e, i), in_=y_out[e % RING][:, i, :],
                                            in_offset=None, compute_op=ALU.add).then_inc(added, 16)
            pool.wait_ge(added, 16 * TILES * NE)

        @block.tensor
        def _(pe):
            def turn(it, k):
                e = RING * it + k
                pe.wait_ge(gathered[k % RING], (it + k // RING + 1) * (16 * TILES))
                pe.wait_ge(x_ready, e + 1)
                for i in range(TILES):
                    last = pe.transpose(xT_ps[k % 2][:, i * P:(i + 1) * P], rows[k % RING][:, i, 0:D], c.identf[:])
                last.then_inc(x_turned, 1)

            def inner(it, k):
                e = RING * it + k
                pe.wait_ge(staged[k % RING], (it + k // RING + 1) * 32)
                pe.wait_ge(x_ready, e + 1 + 2)
                for f in range(FC):
                    pe.wait_ge(gelued, FC * e + f + 1)
                    pe.matmul(u_ps[f][:], w_up[k % RING][:, f * P:(f + 1) * P], xT[k % 2][:],
                              start=True, stop=True).then_inc(upped, 1)

            def outer(it, k):
                e = RING * it + k
                pe.wait_ge(gelued, FC * (e + 1) + FC)
                pe.wait_ge(y_copied, e + 1)
                for i in range(TILES):
                    for f in range(FC):
                        last = pe.matmul(y_ps[k % 2][:, i, :], hidden[k % 2][:, f, i * P:(i + 1) * P],
                                         w_down[k % RING][:, f, :], start=(f == 0), stop=(f == FC - 1))
                last.then_inc(y_ready, 1)

            turn(0, 0)
            inner(0, 0)
            turn(0, 1)
            with pe.Fori(0, LOOPS - 1, 1) as it:
                for k in range(RING):
                    inner(it, k + 1)
                    turn(it, k + 2)
                    outer(it, k)
            for k in range(RING):
                if k + 1 < RING:
                    inner(LOOPS - 1, k + 1)
                if k + 2 < RING:
                    turn(LOOPS - 1, k + 2)
                outer(LOOPS - 1, k)

        @block.scalar
        def _(act):
            act.sem_inc(gelued, FC)
            with act.Fori(0, LOOPS, 1) as it:
                for k in range(RING):
                    e = RING * it + k
                    for f in range(FC):
                        act.wait_ge(upped, FC * e + f + 1)
                        act.activation(hidden[k % 2][:, f, :], u_ps[f][:], ACT.Gelu).then_inc(gelued, 1)

        @block.vector
        def _(dve):
            dve.sem_inc(x_ready, 2)
            dve.sem_inc(y_copied, 2)
            dve.sem_inc(y_free, RING)

            def x_copy(it, k):
                e = RING * it + k
                dve.wait_ge(x_turned, e + 1)
                dve.tensor_copy(xT[k % 2][:], xT_ps[k % 2][:]).then_inc(x_ready, 1)

            def y_copy(it, k):
                e = RING * it + k
                dve.wait_ge(y_ready, e + 1)
                dve.wait_ge(y_free, e + 1)
                for i in range(TILES):
                    last = dve.scalar_tensor_tensor(out=y_out[k][:, i, :], in0=y_ps[k % 2][:, i, :],
                                                    scalar=rows[k][:, i, bass.ds(D + e, 1)],
                                                    in1=c.gate_b[1][:, i // 2, :], op0=ALU.mult, op1=ALU.mult)
                last.then_inc(y_copied, 1)

            x_copy(0, 0)
            x_copy(0, 1)
            with dve.Fori(0, LOOPS - 1, 1) as it:
                for k in range(RING):
                    x_copy(it, k + 2)
                    y_copy(it, k)
            for k in range(RING):
                if k + 2 < RING:
                    x_copy(LOOPS - 1, k + 2)
                y_copy(LOOPS - 1, k)


def block0(core, c, ins):
    with core.scope() as s:
        Qp = s.sbuf("Qp", [P, H, S], F16)
        Kp = s.sbuf("Kp", [P, H, S], F16)
        V = s.sbuf("V", [P, TPB, H * HD0], F32)
        wqkv = s.sbuf("wqkv", [P, 3 * H * HD0], F32)
        wo = s.sbuf("wo", [P, H * HD0 // P, D], F32)
        rope = s.sbuf("rope", [P, TPB, 4, HD0], F32)
        start(core, ins, c, (
            (wqkv[:], ins["L0_attn_wqkv"]),
            (rope[:].rearrange("p t j d -> p t (j d)"), ins["rope"].rearrange("(t p) j d -> p t (j d)", p=P)),
            (wo[:], ins["L0_attn_wo"].rearrange("(u p) d -> p u d", p=P))))
        ctxT = Qp[:].bitcast(F32).rearrange("p (u two) s -> p u (two s)", two=2)
        for b in range(B):
            project_rope(core, c, b, wqkv, rope, Qp, Kp, V)
            attend(core, c, 2, Qp, Kp, V, ctxT, 2, 2)
            project_out(core, c, b, 0, H // 2, ctxT, wo)
    with core.scope() as s:
        acc = s.sbuf("acc", [P, NT, D], F32)
        norm_modulate(core, c, 0, SB, CB, zeros=acc[:])
        r = Routing(core, s)
        w = Shared(s)
        route_top1(core, c, ins, r, acc, w)
        shared_expert(core, c, w, 0, acc, lambda pool, sent: scatter_tokens(pool, r, sent))
        up, up2 = (ins[n].rearrange("e d f -> d e f") for n in ("L0_ffn_W1", "L0_ffn_W2"))
        down = ins["L0_ffn_W3"].rearrange("e (f p) d -> p (e f) d", p=P)
        sorted_experts(core, c, lambda e: up[:, bass.ds(e, 1), :], lambda e: up2[:, bass.ds(e, 1), :],
                       lambda e: down[:, bass.ds(e * FC, FC), :], r)
        shared_expert(core, c, w, NT * P // BANK // 2, acc, lambda pool, sent: gather_tokens(pool, r, sent),
                      lambda dve, step, sent, q, shared: finish_tokens(dve, c, r, step, sent, q, shared))


def block1(core, c, ins, out):
    with core.scope() as s:
        Qp = s.sbuf("Qp", [P, H, S], F16)
        Kp = s.sbuf("Kp", [P, 4, S], F16)
        V = s.sbuf("V", [P, TPB, H * 32], F32)
        ctxT = s.sbuf("ctxT", [P, 4, S], F32)
        wqkv = s.sbuf("wqkv", [P, 3, D], F32)
        wo = s.sbuf("wo", [P, 4, D], F32)
        norm_and_weights(core, c, ins, wqkv, wo, Qp, V)
        for b in range(B):
            project_narrow(core, c, b, wqkv, Qp, Kp, V)
            attend(core, c, 4, Qp, Kp, V, ctxT, 1, 1)
            project_out(core, c, b, 1, 4, ctxT, wo)
    norm_modulate(core, c, 1, SB, CB)
    with core.scope() as s:
        r = Choice(core, s)
        route_experts_choice(core, c, ins, r, out)
        chosen_experts(core, c, ins, r, out)


def build(nc, ins, out):
    core = Core(nc)
    with core.scope() as top:
        c = Consts(top)
        block0(core, c, ins)
        block1(core, c, ins, out)


def rope_tables():
    half = HD0 // 2
    fraction = (np.float32(2.0) * np.arange(half, dtype=np.float32) / np.float32(HD0)).astype(np.float32)
    timescale = np.power(np.float32(10000.0), fraction).astype(np.float32)
    angle = np.arange(S, dtype=np.float32)[:, None] / timescale
    cos, sin = np.cos(angle), np.sin(angle)
    k = [np.concatenate([cos, cos], 1), np.concatenate([sin, -sin], 1)]
    q = [t * np.float32(HD0 ** -0.5) for t in k]
    return np.stack(q + k, 1).astype(np.float32)


def choice_tables():
    part = np.arange(P)
    tile, expert = part // NE, part % NE
    same = (tile[:, None] // TPB == tile // TPB) & (expert[:, None] == expert)
    earlier = same & (tile[:, None] < tile)
    own = part[:, None] // A == np.arange(NE)
    tables = np.concatenate([same, earlier, own], 1).astype(np.float32)
    numbers = np.zeros((DIGITS + 1, 4), np.int32)
    for n in range(DIGITS):
        numbers[n, 0:3] = np.array([1, 2, 3]) << 2 * (DIGITS - 1 - n)
    numbers = np.broadcast_to(numbers.reshape(1, -1), (P, 4 * (DIGITS + 1)))
    sixteen = np.broadcast_to(np.arange(A, dtype=np.int32), (P, A))
    ids = (np.arange(NT)[None, :] * P + part[:, None]).astype(np.float16)
    return {"tables": tables, "numbers": numbers, "sixteen": sixteen, "ids": ids}


def layout(inputs):
    a = {n: np.asarray(v) for n, v in inputs.items()}
    keep = ["L0_attn_x", "L0_attn_wqkv", "L0_attn_wo", "L0_ffn_w1s", "L0_ffn_w2s", "L0_ffn_w3s", "L0_ffn_W1",
            "L0_ffn_W2", "L0_ffn_W3", "L0_ffn_Wg", "L0_wmod", "L1_wmod", "L1_ffn_w1", "L1_ffn_w2"]
    arrays = {n: a[n] for n in keep}
    arrays["L0_cT"], arrays["L1_cT"] = a["L0_c"].T, a["L1_c"].T
    arrays["gate_wT"] = a["L1_ffn_gate_w"].T
    arrays["rope"] = rope_tables()
    arrays.update(choice_tables())
    arrays["lora_w_qkv"] = np.stack([a["L1_attn_w" + n].T for n in "qkv"], 1)
    arrays["lora_a_qkv"] = np.stack([a["L1_attn_a" + n] for n in "qkv"], 1)
    arrays["lora_b_qkv"] = np.stack([a["L1_attn_b" + n].T for n in "qkv"], 1)

    def pad(v):
        v = v.reshape(v.shape[0], 4, 4, HD1)
        return np.pad(v, ((0, 0), (0, 0), (0, 0), (0, 32 - HD1))).reshape(v.shape[0], 4, P)
    arrays["lora_w_o"] = pad(a["L1_attn_wo"]).transpose(2, 1, 0)
    arrays["lora_a_o"] = pad(a["L1_attn_ao"])
    arrays["lora_b_o"] = a["L1_attn_bo"].T
    return {n: np.ascontiguousarray(v) for n, v in arrays.items()}


def kernel(**inputs):
    import concourse.bacc as bacc
    from concourse.bass_utils import run_bass_kernel_spmd

    nc = bacc.Bacc("TRN2", target_bir_lowering=False, num_devices=1)
    arrays = layout(inputs)
    ins = {n: nc.dram_tensor(n, v.shape, mybir.dt.from_np(v.dtype), kind="ExternalInput").ap()
           for n, v in arrays.items()}
    out = nc.dram_tensor("out", (B, S, D), F32, kind="ExternalOutput").ap()
    build(nc, ins, out)
    return run_bass_kernel_spmd(nc, [arrays], core_ids=[0]).results[0]["out"]
```
